# Optimizing a Trainium2 kernel written in Bass

```python
import numpy as np
import jax
import jax.numpy as jnp

def _softmax(x, axis=-1):
    return jax.nn.softmax(x, axis=axis)

def _gelu(x):
    return jax.nn.gelu(x, approximate=True)

def _silu(x):
    return jax.nn.silu(x)

def _sigmoid(x):
    return jax.nn.sigmoid(x)

def _layernorm(x, axis=-1, eps=1e-05):
    m = jnp.mean(x, axis=axis, keepdims=True)
    v = jnp.var(x, axis=axis, keepdims=True)
    return (x - m) / jnp.sqrt(v + eps)

def _scatter_add(tgt, idx, src, axis=0):
    return tgt.at[idx].add(src)

def _segment_sum(src, seg, n):
    return jax.ops.segment_sum(src, seg, n)
kernel_name = 'mk_recurrent_d2_jaxref_r8_09d4a2'

def setup_inputs(seed: int=0):
    np.random.seed(seed)
    _w = jnp.asarray

    def _L0_attn_setup():
        import jax, jax.numpy as jnp
        import numpy as np
        EPS = 1e-06

        def rms_norm(x, scale):
            x32 = x.astype(jnp.float32)
            mean2 = jnp.mean(jnp.square(x32), axis=-1, keepdims=True)
            return x32 * jax.lax.rsqrt(mean2 + EPS) * scale
        key = jax.random.key(seed)
        ks = jax.random.split(key, 7)
        B, S, E, H, D = (2, 256, 256, 16, 128)
        w_std = 1.0 / np.sqrt(E)
        x = jax.random.normal(ks[0], (B, S, E), jnp.float32)
        wq = jax.random.normal(ks[1], (E, H, D), jnp.float32) * w_std
        wk = jax.random.normal(ks[2], (E, H, D), jnp.float32) * w_std
        wv = jax.random.normal(ks[3], (E, H, D), jnp.float32) * w_std
        wo = jax.random.normal(ks[4], (H, D, E), jnp.float32) * (1.0 / np.sqrt(H * D))
        q_scale = jnp.ones((D,), jnp.float32)
        k_scale = jnp.ones((D,), jnp.float32)
        return {'x': x, 'wq': wq, 'wk': wk, 'wv': wv, 'wo': wo, 'q_scale': q_scale, 'k_scale': k_scale}
    _L0_attn_in = _L0_attn_setup()

    def _L0_ffn_setup():
        import math
        import jax, jax.numpy as jnp
        import numpy as np
        from jax import lax
        D = 256
        I = 128
        E = 32
        K = 4
        NG = 8
        TKG = 3
        NSH = 2
        SCALE = 2.5
        CF = 1.25
        B, S = (2, 256)

        def _router(x, router_w, e_bias):
            scores = jax.nn.sigmoid(x @ router_w.T)
            sc = scores + e_bias[None, :]
            T = x.shape[0]
            gs = sc.reshape(T, NG, E // NG)
            group_scores = lax.top_k(gs, 2)[0].sum(-1)
            _, gidx = lax.top_k(group_scores, TKG)
            gmask = jnp.zeros((T, NG), sc.dtype).at[jnp.arange(T)[:, None], gidx].set(1.0)
            smask = jnp.repeat(gmask, E // NG, axis=1)
            masked = jnp.where(smask > 0, sc, 0.0)
            _, topk_idx = lax.top_k(masked, K)
            topk_w = jnp.take_along_axis(scores, topk_idx, axis=1)
            topk_w = topk_w / (topk_w.sum(-1, keepdims=True) + 1e-20)
            topk_w = topk_w * SCALE
            return (topk_idx.astype(jnp.int32), topk_w)

        def _moe_forward(hidden_states, router_w, e_bias, W_gate, W_up, W_down, shared_gate, shared_up, shared_down):
            b, s, d = hidden_states.shape
            T = b * s
            C = int(math.ceil(CF * T / E))
            EC = E * C
            x = hidden_states.reshape(T, d)
            topk_idx, topk_w = _router(x, router_w, e_bias)
            expert_flat = topk_idx.reshape(-1)
            w_flat = topk_w.reshape(-1)
            tok_flat = jnp.repeat(jnp.arange(T, dtype=jnp.int32), K)
            sort_ix = jnp.argsort(expert_flat)
            e_sorted = expert_flat[sort_ix]
            tok_s = tok_flat[sort_ix]
            w_s = w_flat[sort_ix]
            counts = jnp.zeros(E, jnp.int32).at[e_sorted].add(1)
            group_start = jnp.concatenate([jnp.zeros(1, jnp.int32), jnp.cumsum(counts)[:-1].astype(jnp.int32)])
            pos = jnp.arange(T * K, dtype=jnp.int32) - group_start[e_sorted]
            valid = pos < C
            dest = e_sorted * C + jnp.where(valid, pos, 0)
            slots_token = jnp.zeros(EC, jnp.int32).at[dest].add(jnp.where(valid, tok_s, 0))
            slots_w = jnp.zeros(EC, w_s.dtype).at[dest].add(jnp.where(valid, w_s, 0.0))
            Xp = x[slots_token].reshape(E, C, d)
            G = jnp.einsum('ecd,edi->eci', Xp, W_gate)
            U = jnp.einsum('ecd,edi->eci', Xp, W_up)
            Y = jnp.einsum('eci,eid->ecd', jax.nn.silu(G) * U, W_down)
            Yf = Y.reshape(EC, d) * slots_w[:, None]
            out = jnp.zeros((T, d), x.dtype).at[slots_token].add(Yf)
            shared = jax.nn.silu(x @ shared_gate.T) * (x @ shared_up.T) @ shared_down.T
            return (out + shared).reshape(b, s, d)
        key = jax.random.key(seed)
        ks = jax.random.split(key, 8)

        def rn(k, shape, scale=0.02):
            return jax.random.normal(k, shape, jnp.float32) * scale
        return {'hidden_states': jax.random.normal(ks[0], (B, S, D), jnp.float32), 'router_w': rn(ks[1], (E, D)), 'e_bias': jnp.zeros((E,), jnp.float32), 'W_gate': rn(ks[2], (E, D, I)), 'W_up': rn(ks[3], (E, D, I)), 'W_down': rn(ks[4], (E, I, D)), 'shared_gate': rn(ks[5], (I * NSH, D)), 'shared_up': rn(ks[6], (I * NSH, D)), 'shared_down': rn(ks[7], (D, I * NSH))}
    _L0_ffn_in = _L0_ffn_setup()

    def _L1_attn_setup():
        import jax, jax.numpy as jnp
        import numpy as np
        D_MODEL = 256
        N_HEAD = 16
        MLP_HIDDEN = 704
        NORMALIZER = 16.0

        def rmsnorm(x, w, eps=1e-05):
            return x * jax.lax.rsqrt(jnp.mean(x * x, axis=-1, keepdims=True) + eps) * w

        def _reference_tuple_inner(x, Wq, Wk, Wkg1, Wkg2, bkg2, Wv, Wg, bg, Wo, ln1_w, ln2_w, W1, W3, W2):
            B, L, d = x.shape
            H = N_HEAD
            hd = d // H
            kd = d // 2 // H
            scaling = (d // H) ** (-0.5)
            xn = rmsnorm(x, ln1_w)
            q = xn @ Wq
            k = xn @ Wk * scaling
            gk = jax.nn.log_sigmoid(xn @ Wkg1 @ Wkg2 + bkg2) / NORMALIZER
            v = xn @ Wv
            g = xn @ Wg + bg
            split = lambda t, dh: t.reshape(B, L, H, dh).transpose(1, 0, 2, 3)
            qh, kh, gh = (split(q, kd), split(k, kd), split(gk, kd))
            vh = split(v, hd)
            S0 = jnp.zeros((B, H, kd, hd), x.dtype)

            def step(S, inp):
                qt, kt, vt, gt = inp
                S = S * jnp.exp(gt)[..., None] + kt[..., None] * vt[..., None, :]
                ot = jnp.einsum('bhk,bhkd->bhd', qt, S)
                return (S, ot)
            Sf, o = jax.lax.scan(step, S0, (qh, kh, vh, gh))
            mu = jnp.mean(o, axis=-1, keepdims=True)
            var = jnp.var(o, axis=-1, keepdims=True)
            o = (o - mu) * jax.lax.rsqrt(var + 1e-05)
            o = o.transpose(1, 0, 2, 3).reshape(B, L, d)
            o = jax.nn.silu(g) * o
            x = x + o @ Wo
            xn2 = rmsnorm(x, ln2_w)
            x = x + jax.nn.silu(xn2 @ W1) * (xn2 @ W3) @ W2
            return (x, Sf)
        key = jax.random.key(seed)
        d, B, L, Hd = (D_MODEL, 2, 512, MLP_HIDDEN)
        ks = jax.random.split(key, 12)
        w = lambda k, shape, s=0.02: jax.random.normal(k, shape, jnp.float32) * s
        return {'x': jax.random.normal(ks[0], (B, L, d), jnp.float32), 'Wq': w(ks[1], (d, d // 2)), 'Wk': w(ks[2], (d, d // 2)), 'Wkg1': w(ks[3], (d, 16)), 'Wkg2': w(ks[4], (16, d // 2)), 'bkg2': jnp.zeros((d // 2,), jnp.float32), 'Wv': w(ks[5], (d, d)), 'Wg': w(ks[6], (d, d)), 'bg': jnp.zeros((d,), jnp.float32), 'Wo': w(ks[7], (d, d)), 'ln1_w': jnp.ones((d,), jnp.float32), 'ln2_w': jnp.ones((d,), jnp.float32), 'W1': w(ks[8], (d, Hd)), 'W3': w(ks[9], (d, Hd)), 'W2': w(ks[10], (Hd, d))}
    _L1_attn_in = _L1_attn_setup()

    def _L1_ffn_setup():
        import jax, jax.numpy as jnp
        import numpy as np
        B, T, D = (2, 128, 256)
        E, F, K = (64, 64, 4)
        S, HS = (2, 64 * 4)
        key = jax.random.key(seed)
        ks = jax.random.split(key, 9)
        s = 0.02
        f32 = jnp.float32
        return {'x': jax.random.normal(ks[0], (B, T, D), f32), 'router_w': jax.random.normal(ks[1], (D, E), f32) * s, 'router_bias': jnp.zeros((E,), f32), 'wg': jax.random.normal(ks[2], (E, D, F), f32) * s, 'wu': jax.random.normal(ks[3], (E, D, F), f32) * s, 'wd': jax.random.normal(ks[4], (E, F, D), f32) * s, 'swg': jax.random.normal(ks[5], (S, D, HS), f32) * s, 'swu': jax.random.normal(ks[6], (S, D, HS), f32) * s, 'swd': jax.random.normal(ks[7], (S, HS, D), f32) * s}
    _L1_ffn_in = _L1_ffn_setup()
    _d = {'L0_attn_x': _L0_attn_in['x'], 'L0_attn_wq': _L0_attn_in['wq'], 'L0_attn_wk': _L0_attn_in['wk'], 'L0_attn_wv': _L0_attn_in['wv'], 'L0_attn_wo': _L0_attn_in['wo'], 'L0_attn_q_scale': _L0_attn_in['q_scale'], 'L0_attn_k_scale': _L0_attn_in['k_scale'], 'L0_ffn_router_w': _L0_ffn_in['router_w'], 'L0_ffn_e_bias': _L0_ffn_in['e_bias'], 'L0_ffn_W_gate': _L0_ffn_in['W_gate'], 'L0_ffn_W_up': _L0_ffn_in['W_up'], 'L0_ffn_W_down': _L0_ffn_in['W_down'], 'L0_ffn_shared_gate': _L0_ffn_in['shared_gate'], 'L0_ffn_shared_up': _L0_ffn_in['shared_up'], 'L0_ffn_shared_down': _L0_ffn_in['shared_down'], 'L1_attn_Wq': _L1_attn_in['Wq'], 'L1_attn_Wk': _L1_attn_in['Wk'], 'L1_attn_Wkg1': _L1_attn_in['Wkg1'], 'L1_attn_Wkg2': _L1_attn_in['Wkg2'], 'L1_attn_bkg2': _L1_attn_in['bkg2'], 'L1_attn_Wv': _L1_attn_in['Wv'], 'L1_attn_Wg': _L1_attn_in['Wg'], 'L1_attn_bg': _L1_attn_in['bg'], 'L1_attn_Wo': _L1_attn_in['Wo'], 'L1_attn_ln1_w': _L1_attn_in['ln1_w'], 'L1_attn_ln2_w': _L1_attn_in['ln2_w'], 'L1_attn_W1': _L1_attn_in['W1'], 'L1_attn_W3': _L1_attn_in['W3'], 'L1_attn_W2': _L1_attn_in['W2'], 'L1_ffn_router_w': _L1_ffn_in['router_w'], 'L1_ffn_router_bias': _L1_ffn_in['router_bias'], 'L1_ffn_wg': _L1_ffn_in['wg'], 'L1_ffn_wu': _L1_ffn_in['wu'], 'L1_ffn_wd': _L1_ffn_in['wd'], 'L1_ffn_swg': _L1_ffn_in['swg'], 'L1_ffn_swu': _L1_ffn_in['swu'], 'L1_ffn_swd': _L1_ffn_in['swd']}
    _x0 = _d['L0_attn_x']
    _d['L0_attn_x'] = jax.random.normal(jax.random.fold_in(jax.random.key(seed), 1), (1, 1024, 256), dtype=_x0.dtype)
    del _x0
    return _d

def reference(L0_attn_x, L0_attn_wq, L0_attn_wk, L0_attn_wv, L0_attn_wo, L0_attn_q_scale, L0_attn_k_scale, L0_ffn_router_w, L0_ffn_e_bias, L0_ffn_W_gate, L0_ffn_W_up, L0_ffn_W_down, L0_ffn_shared_gate, L0_ffn_shared_up, L0_ffn_shared_down, L1_attn_Wq, L1_attn_Wk, L1_attn_Wkg1, L1_attn_Wkg2, L1_attn_bkg2, L1_attn_Wv, L1_attn_Wg, L1_attn_bg, L1_attn_Wo, L1_attn_ln1_w, L1_attn_ln2_w, L1_attn_W1, L1_attn_W3, L1_attn_W2, L1_ffn_router_w, L1_ffn_router_bias, L1_ffn_wg, L1_ffn_wu, L1_ffn_wd, L1_ffn_swg, L1_ffn_swu, L1_ffn_swd):

    def _L0_attn_ref(x, wq, wk, wv, wo, q_scale, k_scale):
        import jax, jax.numpy as jnp
        import numpy as np
        EPS = 1e-06

        def rms_norm(x, scale):
            x32 = x.astype(jnp.float32)
            mean2 = jnp.mean(jnp.square(x32), axis=-1, keepdims=True)
            return x32 * jax.lax.rsqrt(mean2 + EPS) * scale
        q = jnp.einsum('bse,ehd->bshd', x, wq)
        k = jnp.einsum('bse,ehd->bshd', x, wk)
        v = jnp.einsum('bse,ehd->bshd', x, wv)
        qn = rms_norm(q, q_scale)
        kn = rms_norm(k, k_scale)
        scores = jnp.einsum('bqhd,bkhd->bhqk', qn, kn)
        attn = jax.nn.softmax(scores, axis=-1)
        out = jnp.einsum('bhqk,bkhd->bqhd', attn, v)
        return jnp.einsum('bqhd,hde->bqe', out, wo)

    def _L0_ffn_ref(hidden_states, router_w, e_bias, W_gate, W_up, W_down, shared_gate, shared_up, shared_down):
        import math
        import jax, jax.numpy as jnp
        import numpy as np
        from jax import lax
        D = 256
        I = 128
        E = 32
        K = 4
        NG = 8
        TKG = 3
        NSH = 2
        SCALE = 2.5
        CF = 1.25
        B, S = (2, 256)

        def _router(x, router_w, e_bias):
            scores = jax.nn.sigmoid(x @ router_w.T)
            sc = scores + e_bias[None, :]
            T = x.shape[0]
            gs = sc.reshape(T, NG, E // NG)
            group_scores = lax.top_k(gs, 2)[0].sum(-1)
            _, gidx = lax.top_k(group_scores, TKG)
            gmask = jnp.zeros((T, NG), sc.dtype).at[jnp.arange(T)[:, None], gidx].set(1.0)
            smask = jnp.repeat(gmask, E // NG, axis=1)
            masked = jnp.where(smask > 0, sc, 0.0)
            _, topk_idx = lax.top_k(masked, K)
            topk_w = jnp.take_along_axis(scores, topk_idx, axis=1)
            topk_w = topk_w / (topk_w.sum(-1, keepdims=True) + 1e-20)
            topk_w = topk_w * SCALE
            return (topk_idx.astype(jnp.int32), topk_w)

        def _moe_forward(hidden_states, router_w, e_bias, W_gate, W_up, W_down, shared_gate, shared_up, shared_down):
            b, s, d = hidden_states.shape
            T = b * s
            C = int(math.ceil(CF * T / E))
            EC = E * C
            x = hidden_states.reshape(T, d)
            topk_idx, topk_w = _router(x, router_w, e_bias)
            expert_flat = topk_idx.reshape(-1)
            w_flat = topk_w.reshape(-1)
            tok_flat = jnp.repeat(jnp.arange(T, dtype=jnp.int32), K)
            sort_ix = jnp.argsort(expert_flat)
            e_sorted = expert_flat[sort_ix]
            tok_s = tok_flat[sort_ix]
            w_s = w_flat[sort_ix]
            counts = jnp.zeros(E, jnp.int32).at[e_sorted].add(1)
            group_start = jnp.concatenate([jnp.zeros(1, jnp.int32), jnp.cumsum(counts)[:-1].astype(jnp.int32)])
            pos = jnp.arange(T * K, dtype=jnp.int32) - group_start[e_sorted]
            valid = pos < C
            dest = e_sorted * C + jnp.where(valid, pos, 0)
            slots_token = jnp.zeros(EC, jnp.int32).at[dest].add(jnp.where(valid, tok_s, 0))
            slots_w = jnp.zeros(EC, w_s.dtype).at[dest].add(jnp.where(valid, w_s, 0.0))
            Xp = x[slots_token].reshape(E, C, d)
            G = jnp.einsum('ecd,edi->eci', Xp, W_gate)
            U = jnp.einsum('ecd,edi->eci', Xp, W_up)
            Y = jnp.einsum('eci,eid->ecd', jax.nn.silu(G) * U, W_down)
            Yf = Y.reshape(EC, d) * slots_w[:, None]
            out = jnp.zeros((T, d), x.dtype).at[slots_token].add(Yf)
            shared = jax.nn.silu(x @ shared_gate.T) * (x @ shared_up.T) @ shared_down.T
            return (out + shared).reshape(b, s, d)
        return _moe_forward(hidden_states, router_w, e_bias, W_gate, W_up, W_down, shared_gate, shared_up, shared_down)

    def _L1_attn_ref(x, Wq, Wk, Wkg1, Wkg2, bkg2, Wv, Wg, bg, Wo, ln1_w, ln2_w, W1, W3, W2):
        import jax, jax.numpy as jnp
        import numpy as np
        D_MODEL = 256
        N_HEAD = 16
        MLP_HIDDEN = 704
        NORMALIZER = 16.0

        def rmsnorm(x, w, eps=1e-05):
            return x * jax.lax.rsqrt(jnp.mean(x * x, axis=-1, keepdims=True) + eps) * w

        def _reference_tuple_inner(x, Wq, Wk, Wkg1, Wkg2, bkg2, Wv, Wg, bg, Wo, ln1_w, ln2_w, W1, W3, W2):
            B, L, d = x.shape
            H = N_HEAD
            hd = d // H
            kd = d // 2 // H
            scaling = (d // H) ** (-0.5)
            xn = rmsnorm(x, ln1_w)
            q = xn @ Wq
            k = xn @ Wk * scaling
            gk = jax.nn.log_sigmoid(xn @ Wkg1 @ Wkg2 + bkg2) / NORMALIZER
            v = xn @ Wv
            g = xn @ Wg + bg
            split = lambda t, dh: t.reshape(B, L, H, dh).transpose(1, 0, 2, 3)
            qh, kh, gh = (split(q, kd), split(k, kd), split(gk, kd))
            vh = split(v, hd)
            S0 = jnp.zeros((B, H, kd, hd), x.dtype)

            def step(S, inp):
                qt, kt, vt, gt = inp
                S = S * jnp.exp(gt)[..., None] + kt[..., None] * vt[..., None, :]
                ot = jnp.einsum('bhk,bhkd->bhd', qt, S)
                return (S, ot)
            Sf, o = jax.lax.scan(step, S0, (qh, kh, vh, gh))
            mu = jnp.mean(o, axis=-1, keepdims=True)
            var = jnp.var(o, axis=-1, keepdims=True)
            o = (o - mu) * jax.lax.rsqrt(var + 1e-05)
            o = o.transpose(1, 0, 2, 3).reshape(B, L, d)
            o = jax.nn.silu(g) * o
            x = x + o @ Wo
            xn2 = rmsnorm(x, ln2_w)
            x = x + jax.nn.silu(xn2 @ W1) * (xn2 @ W3) @ W2
            return (x, Sf)
        return _reference_tuple_inner(x, Wq, Wk, Wkg1, Wkg2, bkg2, Wv, Wg, bg, Wo, ln1_w, ln2_w, W1, W3, W2)[0]

    def _L1_ffn_ref(x, router_w, router_bias, wg, wu, wd, swg, swu, swd):
        import jax, jax.numpy as jnp
        import numpy as np
        B, T, D = (2, 128, 256)
        E, F, K = (64, 64, 4)
        S, HS = (2, 64 * 4)
        b, t, d = x.shape
        flat = x.reshape(b * t, d)
        n = flat.shape[0]
        logits = flat @ router_w
        scores = jax.nn.softmax(logits, axis=-1)
        _, topk_idx = jax.lax.top_k(logits + router_bias, K)
        topk_scores = jnp.take_along_axis(scores, topk_idx, axis=-1)
        topk_scores = topk_scores / topk_scores.sum(axis=-1, keepdims=True)
        comb = jnp.zeros((n, E), dtype=flat.dtype).at[jnp.arange(n)[:, None], topk_idx].set(topk_scores)
        g = jax.nn.silu(jnp.einsum('nd,edf->nef', flat, wg))
        u = jnp.einsum('nd,edf->nef', flat, wu)
        routed = jnp.einsum('ne,nef,efd->nd', comb, g * u, wd)
        sg = jax.nn.silu(jnp.einsum('nd,sdh->nsh', flat, swg))
        su = jnp.einsum('nd,sdh->nsh', flat, swu)
        shared = jnp.einsum('nsh,shd->nd', sg * su, swd)
        return (routed + shared).reshape(b, t, d)
    x = L0_attn_x
    xn = _layernorm(x, axis=-1)
    s = _L0_attn_ref(xn, L0_attn_wq, L0_attn_wk, L0_attn_wv, L0_attn_wo, L0_attn_q_scale, L0_attn_k_scale)
    g = _silu(_L0_ffn_ref(xn, L0_ffn_router_w, L0_ffn_e_bias, L0_ffn_W_gate, L0_ffn_W_up, L0_ffn_W_down, L0_ffn_shared_gate, L0_ffn_shared_up, L0_ffn_shared_down))
    x = x + s * g
    xn = _layernorm(x, axis=-1)
    s = _L1_attn_ref(xn, L1_attn_Wq, L1_attn_Wk, L1_attn_Wkg1, L1_attn_Wkg2, L1_attn_bkg2, L1_attn_Wv, L1_attn_Wg, L1_attn_bg, L1_attn_Wo, L1_attn_ln1_w, L1_attn_ln2_w, L1_attn_W1, L1_attn_W3, L1_attn_W2)
    g = _silu(_L1_ffn_ref(xn, L1_ffn_router_w, L1_ffn_router_bias, L1_ffn_wg, L1_ffn_wu, L1_ffn_wd, L1_ffn_swg, L1_ffn_swu, L1_ffn_swd))
    x = x + s * g
    return x

_drawn_inputs = setup_inputs


def setup_inputs(seed=0):
    import zlib

    import numpy as np

    out = dict(_drawn_inputs(seed))
    spreads = {'L0_attn_q_scale': (1.0, 0.6),
     'L0_attn_k_scale': (1.0, 0.6),
     'L0_ffn_e_bias': (0.0, 0.8),
     'L1_attn_bkg2': (0.0, 0.8),
     'L1_attn_bg': (0.0, 0.8),
     'L1_attn_ln1_w': (1.0, 0.6),
     'L1_attn_ln2_w': (1.0, 0.6),
     'L1_ffn_router_bias': (0.0, 0.8)}
    factors = {'L0_attn_wq': 7.309,
     'L0_attn_wk': 7.319,
     'L0_attn_wv': 7.324,
     'L0_attn_wo': 7.322,
     'L0_ffn_router_w': 8.0,
     'L0_ffn_W_gate': 8.0,
     'L0_ffn_W_up': 8.0,
     'L0_ffn_W_down': 8.0,
     'L0_ffn_shared_gate': 7.946,
     'L0_ffn_shared_up': 7.872,
     'L0_ffn_shared_down': 7.883,
     'L1_attn_Wq': 8.0,
     'L1_attn_Wk': 8.0,
     'L1_attn_Wkg1': 8.0,
     'L1_attn_Wkg2': 8.0,
     'L1_attn_Wv': 8.0,
     'L1_attn_Wg': 8.0,
     'L1_attn_Wo': 8.0,
     'L1_attn_W1': 8.0,
     'L1_attn_W3': 8.0,
     'L1_attn_W2': 8.0,
     'L1_ffn_router_w': 8.0,
     'L1_ffn_wg': 8.0,
     'L1_ffn_wu': 8.0,
     'L1_ffn_wd': 8.0,
     'L1_ffn_swg': 4.789,
     'L1_ffn_swu': 4.694,
     'L1_ffn_swd': 4.728}
    for name, (base, spread) in spreads.items():
        noise = np.random.default_rng([zlib.crc32(name.encode()), seed]).standard_normal(out[name].shape)
        drawn = base * np.exp(spread * noise) if base else spread * noise
        out[name] = jnp.asarray(drawn.astype(out[name].dtype))
    for name, factor in factors.items():
        out[name] = (out[name] * factor).astype(out[name].dtype)
    return out
```

```python
import concourse.bass as bass
import numpy as np
from concourse import mybir
from contextlib import ExitStack

F32 = mybir.dt.float32
F16 = mybir.dt.float16
ALU = mybir.AluOpType
ACT = mybir.ActivationFunctionType
AX = mybir.AxisListType

P = 128
T = 1024
NT = T // P
D = 256
DC = D // P
HALF = 512
LN_EPS = 1e-5

H, HD = 16, 128
RMS_EPS0 = 1e-6
WSCALE = 64.0

E0, NG0, GE0, TKG0, K0, I0 = 32, 8, 4, 3, 4, 128
CAP = int(np.ceil(1.25 * T / E0))
SLOTS = E0 * CAP
ST = SLOTS // P
ROUTE_SCALE = 2.5
IS = 256

GH, GK, GV = 16, 8, 16
RMS_EPS1 = 1e-5
GATE_NORM = 16.0
HID = 704
E1, F1, K1 = 64, 64, 4
SH1 = 512

SENTINEL = -1.0e30
TAKEN = -3.0e38


class Chain:

    def __init__(self, engine, done):
        self.engine, self.done, self.count = engine, done, 0

    def __call__(self, instruction):
        self.count += 1
        instruction.then_inc(self.done, 1)
        self.engine.wait_ge(self.done, self.count)


def bcast(ap, axis, n):
    a = ap.unsqueeze(axis)
    shape = list(a.shape)
    shape[axis] = n
    return a.to_broadcast(shape)


def constants(nc, env):
    sb, sem = env["sb"], env["sem"]
    ident = sb("ident", [P, P], F32)
    ident16 = sb("ident16", [P, P], F16)
    ones16 = sb("ones16", [P, P], F16)
    upper16 = sb("upper16", [P, P], F16)
    steps = sb("steps", [P, CAP], F32)
    slot_expert = sb("slot_expert", [P, ST, E0], F32)
    spread = sb("spread", [P, GK, P], F16)
    gather_h = sb("gather_h", [P, GK, P], F32)
    env.update(ident=ident, ident16=ident16, ones16=ones16, upper16=upper16, steps=steps,
               slot_expert=slot_expert, spread=spread, gather_h=gather_h)
    pool_done = sem("const_pool_done")
    with nc.Block() as block:
        @block.gpsimd
        def _(pool):
            chain = Chain(pool, pool_done)
            for m in (ident, ident16):
                chain(pool.memset(m[:, :], 0.0))
                chain(pool.affine_select(out=m[:, :], in_=m[:, :], compare_op=ALU.not_equal, fill=1.0,
                                         base=0, pattern=[[-1, P]], channel_multiplier=1))
            chain(pool.memset(ones16[:, :], 1.0))
            chain(pool.affine_select(out=upper16[:, :], in_=ones16[:, :], compare_op=ALU.is_gt, fill=0.0,
                                     base=0, pattern=[[1, P]], channel_multiplier=-1))
            chain(pool.iota(steps[:, :], [[1, CAP]], base=1, channel_multiplier=0,
                            allow_small_or_imprecise_dtypes=True))
            chain(pool.memset(slot_expert[:, :, :], 1.0))
            chain(pool.affine_select(out=slot_expert[:, :, :], in_=slot_expert[:, :, :], compare_op=ALU.is_ge,
                                     fill=0.0, base=0, pattern=[[P, ST], [-CAP, E0]], channel_multiplier=1))
            chain(pool.affine_select(out=slot_expert[:, :, :], in_=slot_expert[:, :, :], compare_op=ALU.is_ge,
                                     fill=0.0, base=CAP - 1, pattern=[[-P, ST], [CAP, E0]],
                                     channel_multiplier=-1))
            chain(pool.memset(spread[:, :, :], 1.0))
            chain(pool.affine_select(out=spread[:, :, :], in_=spread[:, :, :], compare_op=ALU.is_ge, fill=0.0,
                                     base=0, pattern=[[GH * GK, GK], [1, P]], channel_multiplier=-GK))
            chain(pool.affine_select(out=spread[:, :, :], in_=spread[:, :, :], compare_op=ALU.is_ge, fill=0.0,
                                     base=GK - 1, pattern=[[-GH * GK, GK], [-1, P]], channel_multiplier=GK))
            chain(pool.memset(gather_h[:, :, :], 1.0))
            chain(pool.affine_select(out=gather_h[:, :, :], in_=gather_h[:, :, :], compare_op=ALU.is_ge, fill=0.0,
                                     base=0, pattern=[[GH * GK, GK], [-GK, P]], channel_multiplier=1))
            chain(pool.affine_select(out=gather_h[:, :, :], in_=gather_h[:, :, :], compare_op=ALU.is_ge, fill=0.0,
                                     base=GK - 1, pattern=[[-GH * GK, GK], [GK, P]], channel_multiplier=-1))


def layer_norm(nc, env, tag, x, xn, xnT):
    sem, ident, psum = env["sem"], env["ident"], env["psum"]
    with ExitStack() as local:
        stats = local.enter_context(nc.sbuf_tensor(tag + "_stats", [P, NT, 6], F32))
        mv = local.enter_context(nc.sbuf_tensor(tag + "_mv", [P, NT, 2], F32))
        var = local.enter_context(nc.sbuf_tensor(tag + "_var", [P, NT], F32))
        std = local.enter_context(nc.sbuf_tensor(tag + "_std", [P, NT], F32))
        inv = local.enter_context(nc.sbuf_tensor(tag + "_inv", [P, NT], F32))
        stats_done, mv_done, var_ready, std_ready = (sem(tag + s) for s in ("_st", "_mv", "_var", "_std"))
        inv_done, xn_ready, xT_ready, evac_done = (sem(tag + s) for s in ("_inv", "_xn", "_xT", "_ev"))
        with nc.Block() as block:
            @block.vector
            def _(dve):
                if "x_loaded" in env and tag == "ln0":
                    dve.wait_ge(env["x_loaded"], 16)
                for n in range(NT):
                    dve.bn_stats(stats[:, n, :], x[:, n, :]).then_inc(stats_done, 1)
                for n in range(NT):
                    dve.wait_ge(stats_done, n + 1)
                    dve.bn_aggr(mv[:, n, :], stats[:, n, :]).then_inc(mv_done, 1)
                dve.wait_ge(mv_done, NT)
                dve.tensor_scalar(var[:, :], mv[:, :, 1], LN_EPS, None, ALU.add).then_inc(var_ready, 1)
                dve.wait_ge(std_ready, 1)
                dve.reciprocal(inv[:, :], std[:, :]).then_inc(inv_done, 1)
                dve.wait_ge(inv_done, 1)
                for n in range(NT):
                    dve.tensor_scalar(xn[:, n, :], x[:, n, :], mv[:, n, 0:1], inv[:, n:n + 1],
                                      ALU.subtract, ALU.mult).then_inc(xn_ready, 1)

            @block.scalar
            def _(act):
                act.wait_ge(var_ready, 1)
                act.activation(std[:, :], var[:, :], ACT.Sqrt).then_inc(std_ready, 1)
                for n in range(NT):
                    act.wait_ge(xT_ready, n + 1)
                    act.activation(xnT[:, :, n * P:(n + 1) * P],
                                   psum[:, n % 2, 0:D].rearrange("p (c t) -> p c t", c=DC),
                                   ACT.Copy).then_inc(evac_done, 1)

            @block.tensor
            def _(pe):
                for n in range(NT):
                    pe.wait_ge(xn_ready, n + 1)
                    if n >= 2:
                        pe.wait_ge(evac_done, n - 1)
                    for c in range(DC):
                        last = pe.transpose(psum[:, n % 2, c * P:(c + 1) * P], xn[:, n, c * P:(c + 1) * P],
                                            ident[:, :])
                    last.then_inc(xT_ready, 1)


def split16(nc, env, tag, pairs):
    done = env["sem"](tag + "_high")
    with nc.Block() as block:
        @block.vector
        def _(dve):
            for i, (x, high, low) in enumerate(pairs):
                dve.tensor_copy(high, x).then_inc(done, 1)
                dve.wait_ge(done, i + 1)
                dve.tensor_tensor(low, x, high, ALU.subtract)


def top_k_mask(dve, chain, scores, k, best, named, replaced, mask):
    m = scores.shape[2] - 8
    chain(dve.memset(named, SENTINEL))
    for n in range(NT):
        chain(dve.max(best[:, n, :], scores[:, n, 0:m]))
    chain(dve.tensor_copy(named[:, :, 0:k], best[:, :, 0:k]))
    for n in range(NT):
        chain(dve.match_replace(replaced[:, n, :], named[:, n, :], scores[:, n, :], TAKEN))
    chain(dve.tensor_scalar(mask, replaced[:, :, 0:m], TAKEN / 2, None, ALU.is_lt))


def route0(nc, env, router_w, e_bias):
    sem, psum, ident = env["sem"], env["psum"], env["ident"]
    xnT, ones16, upper16, steps = env["xnT"], env["ones16"], env["upper16"], env["steps"]
    member, wk_h, wk_l = env["member"], env["wk_h"], env["wk_l"]
    with ExitStack() as local:
        def tmp(name, shape, dt=F32):
            return local.enter_context(nc.sbuf_tensor("r0_" + name, shape, dt))
        rw, rwT, bias = tmp("rw", [E0, D]), tmp("rwT", [P, DC, E0]), tmp("bias", [P, E0])
        prob, sc = tmp("prob", [P, NT, E0]), tmp("sc", [P, NT, E0])
        hi2, lo2, sums = tmp("hi2", [P, NT * NG0, 2]), tmp("lo2", [P, NT * NG0, 2]), tmp("sums", [P, NT * NG0, 2])
        gs, gr, gm = tmp("gs", [P, NT, NG0 + 8]), tmp("gr", [P, NT, NG0 + 8]), tmp("gm", [P, NT, NG0])
        es, er, sel = tmp("es", [P, NT, E0 + 8]), tmp("er", [P, NT, E0 + 8]), tmp("sel", [P, NT, E0])
        best, named = tmp("best", [P, NT, 8]), tmp("named", [P, NT, 8])
        sel16 = tmp("sel16", [P, NT, E0], F16)
        w, wsum, winv = tmp("w", [P, NT, E0]), tmp("wsum", [P, NT]), tmp("winv", [P, NT])
        keep, place = tmp("keep", [P, NT, E0]), tmp("place", [P, NT, E0])
        loaded = [sem("r0_ld0"), sem("r0_ld1")]
        rwT_ready, rwT_done, logits_ready, prob_ready = (sem("r0_" + s) for s in ("rwT", "rwTd", "lg", "pr"))
        sel_ready, pos_ready, dve_done = (sem("r0_" + s) for s in ("sel", "pos", "dve"))
        logits = psum[:, 0, 0:NT * E0].rearrange("p (n e) -> p n e", n=NT)
        pos = psum[:, 1, 0:NT * E0].rearrange("p (n e) -> p n e", n=NT)
        turned = psum[:, 2, 0:DC * E0].rearrange("p (c e) -> p c e", c=DC)
        with nc.Block() as block:
            @block.sync
            def _(sp):
                sp.dma_start(rw[:, :], router_w).then_inc(loaded[0], 16)
                sp.dma_start(bias[:, :], e_bias.partition_broadcast(P)).then_inc(loaded[1], 16)

            @block.tensor
            def _(pe):
                pe.wait_ge(loaded[0], 16)
                for c in range(DC):
                    last = pe.transpose(turned[:, c, :], rw[:, c * P:(c + 1) * P], ident[0:E0, 0:E0])
                last.then_inc(rwT_ready, 1)
                pe.wait_ge(rwT_done, 1)
                for n in range(NT):
                    for c in range(DC):
                        last = pe.matmul(logits[:, n, :], xnT[:, c, n * P:(n + 1) * P], rwT[:, c, :],
                                         start=(c == 0), stop=(c == DC - 1))
                last.then_inc(logits_ready, 1)
                pe.wait_ge(sel_ready, 1)
                for n in range(NT):
                    for i in range(n):
                        pe.matmul(pos[:, n, :], ones16[:, :], sel16[:, i, :], start=(i == 0), stop=False)
                    last = pe.matmul(pos[:, n, :], upper16[:, :], sel16[:, n, :], start=(n == 0), stop=True)
                last.then_inc(pos_ready, 1)

            @block.scalar
            def _(act):
                act.wait_ge(rwT_ready, 1)
                act.activation(rwT[:, :, :], turned, ACT.Copy).then_inc(rwT_done, 1)
                act.wait_ge(logits_ready, 1)
                act.activation(prob[:, :, :], logits, ACT.Sigmoid).then_inc(prob_ready, 1)

            @block.vector
            def _(dve):
                chain = Chain(dve, dve_done)
                dve.wait_ge(prob_ready, 1)
                dve.wait_ge(loaded[1], 16)
                chain(dve.tensor_tensor(sc[:, :, :], prob[:, :, :], bcast(bias[:, :], 1, NT), ALU.add))
                pair = sc[:, :, :].rearrange("p n (g a b) -> p (n g) a b", a=2, b=2)
                chain(dve.tensor_tensor(hi2[:, :, :], pair[:, :, :, 0], pair[:, :, :, 1], ALU.max))
                chain(dve.tensor_tensor(lo2[:, :, :], pair[:, :, :, 0], pair[:, :, :, 1], ALU.min))
                chain(dve.tensor_tensor(sums[:, :, :], hi2[:, :, :], lo2[:, :, :], ALU.add))
                chain(dve.tensor_tensor(lo2[:, :, 0], hi2[:, :, 0], hi2[:, :, 1], ALU.add))
                chain(dve.tensor_tensor(lo2[:, :, 1], sums[:, :, 0], sums[:, :, 1], ALU.max))
                chain(dve.memset(gs[:, :, :], SENTINEL))
                chain(dve.tensor_tensor(gs[:, :, 0:NG0], lo2[:, :, 0].rearrange("p (n g) -> p n g", n=NT),
                                        lo2[:, :, 1].rearrange("p (n g) -> p n g", n=NT), ALU.max))
                top_k_mask(dve, chain, gs[:, :, :], TKG0, best[:, :, :], named[:, :, :], gr[:, :, :], gm[:, :, :])
                chain(dve.memset(es[:, :, :], SENTINEL))
                for a in range(GE0):
                    chain(dve.tensor_tensor(es[:, :, a:E0:GE0], sc[:, :, a:E0:GE0], gm[:, :, :], ALU.mult))
                chain(dve.tensor_scalar(es[:, :, 0:E0], es[:, :, 0:E0], 0.0, None, ALU.add))
                top_k_mask(dve, chain, es[:, :, :], K0, best[:, :, :], named[:, :, :], er[:, :, :], sel[:, :, :])
                dve.tensor_copy(sel16[:, :, :], sel[:, :, :]).then_inc(sel_ready, 1)
                chain(dve.tensor_tensor(w[:, :, :], prob[:, :, :], sel[:, :, :], ALU.mult))
                chain(dve.reduce_sum(wsum[:, :], w[:, :, :], AX.X))
                chain(dve.tensor_scalar(wsum[:, :], wsum[:, :], 1e-20, None, ALU.add))
                chain(dve.reciprocal(winv[:, :], wsum[:, :]))
                chain(dve.scalar_tensor_tensor(w[:, :, :], w[:, :, :], ROUTE_SCALE, bcast(winv[:, :], 2, E0),
                                               ALU.mult, ALU.mult))
                dve.wait_ge(pos_ready, 1)
                chain(dve.scalar_tensor_tensor(keep[:, :, :], pos, float(CAP), sel[:, :, :], ALU.is_lt, ALU.mult))
                chain(dve.scalar_tensor_tensor(place[:, :, :], pos, 1.0, keep[:, :, :], ALU.add, ALU.mult))
                chain(dve.tensor_tensor(w[:, :, :], w[:, :, :], keep[:, :, :], ALU.mult))
                chain(dve.tensor_copy(wk_h[:, :, :], w[:, :, :]))
                chain(dve.tensor_tensor(wk_l[:, :, :], w[:, :, :], wk_h[:, :, :], ALU.subtract))
                for n in range(NT):
                    chain(dve.tensor_tensor(member[:, n, :, :], bcast(place[:, n, :], 2, CAP),
                                            bcast(steps[:, :], 1, E0), ALU.is_equal))


def experts0(nc, env, w_gate, w_up, w_down):
    sem, psum = env["sem"], env["psum"]
    xn_h, xn_l, member, wk_h, wk_l = (env[k] for k in ("xn_h", "xn_l", "member", "wk_h", "wk_l"))
    slot_expert, yT = env["slot_expert"], env["yT"]
    w_slot = env["w_slot"]
    cuts = [(0, 512), (512, 512), (1024, 256)]
    with ExitStack() as local:
        def tmp(name, shape, dt=F32):
            return local.enter_context(nc.sbuf_tensor("e0_" + name, shape, dt))
        xgT = tmp("xgT", [P, DC, SLOTS])
        wmask = tmp("wmask", [P, ST, E0])
        gathered, xg_done, ws_ready, wm_done = (sem("e0_" + s) for s in ("ga", "xg", "ws", "wm"))
        ws = psum[:, 7, 0:ST * E0].rearrange("p (s e) -> p s e", s=ST)
        with nc.Block() as block:
            @block.tensor
            def _(pe):
                for c in range(DC):
                    for k, (at, size) in enumerate(cuts):
                        bank = c * len(cuts) + k
                        for n in range(NT):
                            slots = member[:, n, :, :].rearrange("p e c -> p (e c)")[:, at:at + size]
                            pe.matmul(psum[:, bank, 0:size], xn_h[:, n, c * P:(c + 1) * P], slots,
                                      start=(n == 0), stop=False)
                            last = pe.matmul(psum[:, bank, 0:size], xn_l[:, n, c * P:(c + 1) * P], slots,
                                             start=False, stop=(n == NT - 1))
                        last.then_inc(gathered, 1)
                for s in range(ST):
                    for n in range(NT):
                        slots = member[:, n, :, :].rearrange("p e c -> p (e c)")[:, s * P:(s + 1) * P]
                        pe.matmul(ws[:, s, :], slots, wk_h[:, n, :], start=(n == 0), stop=False)
                        last = pe.matmul(ws[:, s, :], slots, wk_l[:, n, :], start=False, stop=(n == NT - 1))
                last.then_inc(ws_ready, 1)

            @block.scalar
            def _(act):
                for c in range(DC):
                    for k, (at, size) in enumerate(cuts):
                        bank = c * len(cuts) + k
                        act.wait_ge(gathered, bank + 1)
                        act.activation(xgT[:, c, at:at + size], psum[:, bank, 0:size], ACT.Copy).then_inc(xg_done, 1)

            @block.vector
            def _(dve):
                dve.wait_ge(ws_ready, 1)
                dve.tensor_tensor(wmask[:, :, :], ws, slot_expert[:, :, :], ALU.mult).then_inc(wm_done, 1)
                dve.wait_ge(wm_done, 1)
                dve.reduce_sum(w_slot[:, :], wmask[:, :, :], AX.X).then_inc(wm_done, 1)

        wgu = [tmp(f"wgu{b}", [P, DC, 2, I0]) for b in range(2)]
        wd = [tmp(f"wd{b}", [P, D]) for b in range(2)]
        sg = [tmp(f"sg{b}", [P, CAP]) for b in range(2)]
        hT = [tmp(f"hT{b}", [P, CAP]) for b in range(2)]
        gate_loaded = [sem(f"e0_lg{b}") for b in range(2)]
        up_loaded = [sem(f"e0_lu{b}") for b in range(2)]
        down_loaded = [sem(f"e0_ld{b}") for b in range(2)]
        gu_ready, silu_done, h_ready, y_ready, y_done = (sem("e0_" + s) for s in ("gu", "si", "h", "y", "yd"))
        with nc.Block() as block:
            @block.sync
            def _(sp):
                def load(e, b):
                    for j, (src, got) in enumerate(((w_gate, gate_loaded), (w_up, up_loaded))):
                        sp.dma_start(wgu[b][:, :, j, :],
                                     src[bass.ds(e, 1), :, :].rearrange("o (c p) i -> p (o c) i", p=P)).then_inc(got[b], 16)
                    sp.dma_start(wd[b][:, :], src2(e)).then_inc(down_loaded[b], 16)

                def src2(e):
                    return w_down[bass.ds(e, 1), :, :].rearrange("o i d -> (o i) d")
                for b in range(2):
                    load(b, b)
                with sp.Fori(0, E0 // 2 - 1) as i:
                    for b in range(2):
                        sp.wait_ge(y_ready, 2 * i + b + 1)
                        load(2 * i + b + 2, b)

            @block.tensor
            def _(pe):
                with pe.Fori(0, E0 // 2) as i:
                    for b in range(2):
                        e = 2 * i + b
                        pe.wait_ge(gate_loaded[b], 16 * i + 16)
                        pe.wait_ge(up_loaded[b], 16 * i + 16)
                        for j in range(2):
                            for c in range(DC):
                                last = pe.matmul(psum[:, b, j * CAP:(j + 1) * CAP], wgu[b][:, c, j, :],
                                                 xgT[:, c, bass.ds(e * CAP, CAP)], start=(c == 0), stop=(c == DC - 1))
                        last.then_inc(gu_ready, 1)
                    for b in range(2):
                        e = 2 * i + b
                        pe.wait_ge(down_loaded[b], 16 * i + 16)
                        pe.wait_ge(h_ready, e + 1)
                        for c in range(DC):
                            last = pe.matmul(psum[:, 2 + b, c * CAP:(c + 1) * CAP], wd[b][:, c * P:(c + 1) * P],
                                             hT[b][:, :], start=True, stop=True)
                        last.then_inc(y_ready, 1)

            @block.scalar
            def _(act):
                with act.Fori(0, E0 // 2) as i:
                    for b in range(2):
                        act.wait_ge(gu_ready, 2 * i + b + 1)
                        act.activation(sg[b][:, :], psum[:, b, 0:CAP], ACT.Silu).then_inc(silu_done, 1)

            @block.vector
            def _(dve):
                with dve.Fori(0, E0 // 2) as i:
                    for b in range(2):
                        dve.wait_ge(silu_done, 2 * i + b + 1)
                        dve.tensor_tensor(hT[b][:, :], psum[:, b, CAP:2 * CAP], sg[b][:, :], ALU.mult).then_inc(h_ready, 1)
                    for b in range(2):
                        dve.wait_ge(y_ready, 2 * i + b + 1)
                        dve.tensor_copy(yT[:, :, bass.ds((2 * i + b) * CAP, CAP)],
                                        psum[:, 2 + b, 0:DC * CAP].rearrange("p (c s) -> p c s", c=DC)).then_inc(y_done, 1)


def combine0(nc, env, shared_gate, shared_up, shared_down):
    sem, psum, ident = env["sem"], env["psum"], env["ident"]
    member, yT, w_slot, xnT, gate0 = (env[k] for k in ("member", "yT", "w_slot", "xnT", "gate0"))
    ident16 = env["ident16"]
    IC = IS // P
    with ExitStack() as local:
        def tmp(name, shape, dt=F32):
            return local.enter_context(nc.sbuf_tensor("c0_" + name, shape, dt))
        w3 = [tmp(f"w{i}", [P, 2, D]) for i in range(3)]
        w3T = [tmp(f"wT{i}", [P, 2, D]) for i in range(3)]
        sg = tmp("sg", [P, 2, HALF])
        hT = tmp("hT", [P, IC, T])
        loaded = [sem(f"c0_ld{i}") for i in range(3)]
        wT_ready, wT_done, gu_ready, silu_done, h_ready = (sem("c0_" + s) for s in ("wT", "wTd", "gu", "si", "h"))
        with nc.Block() as block:
            @block.sync
            def _(sp):
                for i, src in enumerate((shared_gate, shared_up, shared_down)):
                    sp.dma_start(w3[i][:, :, :], src.rearrange("(a p) d -> p a d", p=P)).then_inc(loaded[i], 16)

            @block.tensor
            def _(pe):
                for i in range(3):
                    pe.wait_ge(loaded[i], 16)
                    for a in range(2):
                        for c in range(2):
                            last = pe.transpose(psum[:, i, (c * 2 + a) * P:(c * 2 + a + 1) * P],
                                                w3[i][:, a, c * P:(c + 1) * P], ident[:, :])
                    last.then_inc(wT_ready, 1)
                pe.wait_ge(wT_done, 3)
                for step in range(2 * IC):
                    t, ic = step // IC, step % IC
                    bank = 4 + 2 * (step % 2)
                    if step >= 2:
                        pe.wait_ge(h_ready, step - 1)
                    for j in range(2):
                        for c in range(DC):
                            last = pe.matmul(psum[:, bank + j, :], w3T[j][:, c, ic * P:(ic + 1) * P],
                                             xnT[:, c, t * HALF:(t + 1) * HALF], start=(c == 0), stop=(c == DC - 1))
                    last.then_inc(gu_ready, 1)

            @block.scalar
            def _(act):
                for i in range(3):
                    act.wait_ge(wT_ready, i + 1)
                    act.activation(w3T[i][:, :, :], psum[:, i, :].rearrange("p (c x) -> p c x", c=2),
                                   ACT.Copy).then_inc(wT_done, 1)
                for step in range(2 * IC):
                    act.wait_ge(gu_ready, step + 1)
                    if step >= 2:
                        act.wait_ge(h_ready, step - 1)
                    act.activation(sg[:, step % 2, :], psum[:, 4 + 2 * (step % 2), :], ACT.Silu).then_inc(silu_done, 1)

            @block.vector
            def _(dve):
                for step in range(2 * IC):
                    t, ic = step // IC, step % IC
                    dve.wait_ge(silu_done, step + 1)
                    dve.tensor_tensor(hT[:, ic, t * HALF:(t + 1) * HALF], psum[:, 5 + 2 * (step % 2), :],
                                      sg[:, step % 2, :], ALU.mult).then_inc(h_ready, 1)

        yw_h, yw_l = tmp("yw_h", [P, ST, D], F16), tmp("yw_l", [P, ST, D], F16)
        turned = [tmp(f"turned{b}", [P, ST, P], F16) for b in range(2)]
        y_ready, yh_done, yl_done, m_ready, m_done, o_ready, o_done = (
            sem("c1_" + s) for s in ("y", "yh", "yl", "m", "md", "o", "od"))
        mcuts = [(0, 8), (8, ST - 8)]
        with nc.Block() as block:
            @block.tensor
            def _(pe):
                for s in range(ST):
                    if s >= 2:
                        pe.wait_ge(yl_done, s - 1)
                    for c in range(DC):
                        last = pe.transpose(psum[:, s % 2, c * P:(c + 1) * P], yT[:, c, s * P:(s + 1) * P], ident[:, :])
                    last.then_inc(y_ready, 1)
                for n in range(NT):
                    slots = member[:, n, :, :].rearrange("p e c -> p (e c)")
                    for k, (at, size) in enumerate(mcuts):
                        step = 2 * n + k
                        if step >= 2:
                            pe.wait_ge(m_done, step - 1)
                        for s in range(at, at + size):
                            out = psum[:, 2 + k, :].bitcast(F16)[:, (s - at) * P:(s - at + 1) * P]
                            last = pe.transpose(out, slots[:, s * P:(s + 1) * P], ident16[:, :])
                        last.then_inc(m_ready, 1)
                    pe.wait_ge(m_done, 2 * n + 2)
                    if n == 0:
                        pe.wait_ge(yl_done, ST)
                    if n >= 2:
                        pe.wait_ge(o_done, n - 1)
                    out = psum[:, 4 + n % 2, 0:D]
                    for s in range(ST):
                        pe.matmul(out, turned[n % 2][:, s, :], yw_h[:, s, :], start=(s == 0), stop=False)
                        pe.matmul(out, turned[n % 2][:, s, :], yw_l[:, s, :], start=False, stop=False)
                    for ic in range(IC):
                        last = pe.matmul(out, hT[:, ic, n * P:(n + 1) * P], w3T[2][:, ic, :],
                                         start=False, stop=(ic == IC - 1))
                    last.then_inc(o_ready, 1)

            @block.scalar
            def _(act):
                for n in range(NT):
                    for k, (at, size) in enumerate(mcuts):
                        act.wait_ge(m_ready, 2 * n + k + 1)
                        if n >= 2:
                            act.wait_ge(o_ready, n - 1)
                        act.copy(turned[n % 2][:, at:at + size, :].rearrange("p s x -> p (s x)").bitcast(F32),
                                 psum[:, 2 + k, 0:size * P // 2]).then_inc(m_done, 1)
                for n in range(NT):
                    act.wait_ge(o_done, n + 1)
                    act.activation(gate0[:, n, :], gate0[:, n, :], ACT.Silu)

            @block.vector
            def _(dve):
                for s in range(ST):
                    dve.wait_ge(y_ready, s + 1)
                    dve.tensor_scalar(yw_h[:, s, :], psum[:, s % 2, 0:D], w_slot[:, s:s + 1], None,
                                      ALU.mult).then_inc(yh_done, 1)
                    dve.wait_ge(yh_done, s + 1)
                    dve.scalar_tensor_tensor(yw_l[:, s, :], psum[:, s % 2, 0:D], w_slot[:, s:s + 1], yw_h[:, s, :],
                                             ALU.mult, ALU.subtract).then_inc(yl_done, 1)
                for n in range(NT):
                    dve.wait_ge(o_ready, n + 1)
                    dve.tensor_copy(gate0[:, n, :], psum[:, 4 + n % 2, 0:D]).then_inc(o_done, 1)


def mixture0(nc, env, w):
    with ExitStack() as local:
        def tmp(name, shape, dt=F32):
            return local.enter_context(nc.sbuf_tensor(name, shape, dt))
        env["member"] = tmp("member", [P, NT, E0, CAP], F16)
        env["wk_h"], env["wk_l"] = tmp("wk_h", [P, NT, E0], F16), tmp("wk_l", [P, NT, E0], F16)
        env["yT"] = tmp("yT", [P, DC, SLOTS])
        env["w_slot"] = tmp("w_slot", [P, ST])
        xn_h, xn_l = tmp("xn_h", [P, NT, D], F16), tmp("xn_l", [P, NT, D], F16)
        env["xn_h"], env["xn_l"] = xn_h, xn_l
        split16(nc, env, "xn0tok", [(env["xn"][:, :, :], xn_h[:, :, :], xn_l[:, :, :])])
        route0(nc, env, w["L0_ffn_router_w"], w["L0_ffn_e_bias"])
        experts0(nc, env, w["L0_ffn_W_gate"], w["L0_ffn_W_up"], w["L0_ffn_W_down"])
        combine0(nc, env, w["L0_ffn_shared_gate"], w["L0_ffn_shared_up"], w["L0_ffn_shared_down"])


def store_tokens(nc, env, tag, out, tile):
    stored = env["sem"](tag + "_stored")
    with nc.Block() as block:
        @block.sync
        def _(sp):
            sp.dma_start(out.rearrange("(n p) d -> p n d", p=P), tile[:, :, :]).then_inc(stored, 16)
            sp.wait_ge(stored, 16)


def attention0(nc, env, w):
    sem, psum, ident, ident16 = env["sem"], env["psum"], env["ident"], env["ident16"]
    xT_h, xT_l, oT_h, oT_l = (env[k] for k in ("xT_h", "xT_l", "oT_h", "oT_l"))
    wq, wk, wv = (w["L0_attn_" + k].rearrange("(c p) h d -> p c h d", p=P) for k in ("wq", "wk", "wv"))
    SIDE = [("qk", 0), ("qk", 1), ("qk", 2), ("qk", 3), ("turn", 0), ("turn", 1), ("turn", 2), ("v", 0),
            ("turn", 3), ("v", 1)]
    PLAN = {0: ([0], [1]), 1: ([2], [3]), 2: ([], []), 3: ([], []), 4: ([4], [5]), 5: ([6], [7]),
            6: ([8], [9]), 7: ([], [])}
    NORM_SLOT = 3
    NS = len(SIDE)
    QK_LAST = SIDE.index(("qk", 3))
    TURN_LAST = SIDE.index(("turn", 3))
    V_LAST = SIDE.index(("v", 1))
    LOWS = [i for i, (kind, _) in enumerate(SIDE) if kind != "qk"]
    QT = NT
    KT = NT
    PROB = 4096.0
    S_BANK, T_BANK, O_BANK, SIDE_BANK = 0, 4, 6, 7
    with ExitStack() as local:
        def tmp(name, shape, dt=F32):
            return local.enter_context(nc.sbuf_tensor("a0_" + name, shape, dt))
        wf = [tmp(f"wf{b}", [P, DC, 3, HD]) for b in range(2)]
        w_h = [tmp(f"wh{b}", [P, DC, 3, HD], F16) for b in range(2)]
        w_l = [tmp(f"wl{b}", [P, DC, 3, HD], F16) for b in range(2)]
        qk = tmp("qk", [P, NT, 2, HD])
        sq = tmp("sq", [P, NT, 2, HD])
        ss, power, rnorm = tmp("ss", [P, NT * 2]), tmp("power", [P, NT * 2]), tmp("rnorm", [P, NT * 2])
        qkT_h = [tmp(f"qkTh{b}", [P, 2, T], F16) for b in range(2)]
        qkT_l = [tmp(f"qkTl{b}", [P, 2, T], F16) for b in range(2)]
        v_h = [tmp(f"vh{b}", [P, NT, HD], F16) for b in range(2)]
        v_l = [tmp(f"vl{b}", [P, NT, HD], F16) for b in range(2)]
        lifts = tmp("lifts", [P, 2])
        scales = tmp("scales", [P, 2])
        qk_scale = tmp("qk_scale", [P, 2])
        nmax, total, tsc, rtot = (tmp(n, [P, 2]) for n in ("nmax", "total", "tsc", "rtot"))
        ex = [tmp(f"ex{b}", [P, T]) for b in range(2)]
        pr = [tmp(f"pr{b}", [P, 2, T], F16) for b in range(2)]
        pT = [tmp(f"pT{b}", [P, 2, KT, HALF], F16) for b in range(2)]

        w_loaded = [sem(f"a0_wld{b}") for b in range(2)]
        scale_loaded = [sem(f"a0_sld{b}") for b in range(2)]
        (scale_ready, w_scaled, w_high, w_ready, side_ready, side_high, side_free, sq_ready, ss_ready,
         var_ready, pow_ready, r_ready, qkn_ready, s_ready, max_ready, exp_ready, tsc_ready, rt_ready, ph_ready,
         p_ready, t_ready, pT_ready, pv_ready, o_high, o_free) = (sem("a0_" + s) for s in (
             "sc", "ws", "wh", "wr", "sr", "sh", "sf", "sq", "ss", "vr", "pw", "rr", "qn", "s", "mx", "ex",
             "ts", "rt", "ph", "p", "t", "pT", "pv", "oh", "of"))

        def heads(engine, head):
            head(0, 0, True, False)
            with engine.Fori(0, (H - 2) // 2) as i:
                for b in range(2):
                    head(2 * i + 1 + b, (1 + b) % 2, False, False)
            head(H - 1, (H - 1) % 2, False, True)

        def sides(m, part, job, t):
            for s in PLAN[m][part]:
                job(t, s)

        with nc.Block() as block:
            @block.sync
            def _(sp):
                for i, name in enumerate(("L0_attn_q_scale", "L0_attn_k_scale")):
                    sp.dma_start(scales[:, i:i + 1], w[name].rearrange("(p a) -> p a", a=1)).then_inc(scale_loaded[i], 16)

                def load(h, b):
                    for j, src in enumerate((wq, wk, wv)):
                        sp.dma_start(wf[b][:, :, j, :], src[:, :, bass.ds(h, 1), :].rearrange("p c o d -> p c (o d)"))\
                          .then_inc(w_loaded[b], 16)
                load(0, 0)
                load(1, 1)
                with sp.Fori(0, (H - 2) // 2) as i:
                    for b in range(2):
                        sp.wait_ge(w_ready, 2 * i + b + 1)
                        load(2 * i + b + 2, b)

            @block.gpsimd
            def _(pool):
                pool.memset(power[:, :], -0.5).then_inc(pow_ready, 1)
                pool.memset(lifts[:, 0:1], WSCALE).then_inc(pow_ready, 1)
                pool.memset(lifts[:, 1:2], 1.0 / WSCALE).then_inc(pow_ready, 1)
                pool.wait_ge(scale_loaded[0], 16)
                pool.wait_ge(scale_loaded[1], 16)
                pool.tensor_tensor(qk_scale[:, 0:1], scales[:, 0:1], scales[:, 1:2], ALU.mult).then_inc(scale_ready, 1)
                pool.memset(qk_scale[:, 1:2], 1.0).then_inc(scale_ready, 1)
                pool.wait_ge(pow_ready, 3)

                def split_weights(t, b, loads):
                    pool.wait_ge(w_loaded[b], 48 * loads)
                    if not isinstance(t, int) or t >= 2:
                        pool.wait_ge(side_ready, NS * (t - 2) + V_LAST + 1)
                    lift = lifts[:, 0:1].to_broadcast([P, DC * 3 * HD])
                    flat, high = (x.rearrange("p c j d -> p (c j d)") for x in (wf[b][:, :, :, :], w_h[b][:, :, :, :]))
                    pool.tensor_tensor(high, flat, lift, ALU.mult).then_inc(w_high, 1)
                    pool.wait_ge(w_high, t + 1)
                    pool.tensor_tensor(flat, flat, lift, ALU.mult).then_inc(w_scaled, 1)
                    pool.wait_ge(w_scaled, t + 1)
                    pool.tensor_tensor(w_l[b][:, :, :, :], wf[b][:, :, :, :], w_h[b][:, :, :, :],
                                       ALU.subtract).then_inc(w_ready, 1)

                def normalise(t):
                    pool.wait_ge(side_free, NS * t + QK_LAST + 1)
                    pool.tensor_tensor(sq[:, :, :, :], qk[:, :, :, :], qk[:, :, :, :], ALU.mult).then_inc(sq_ready, 1)
                    pool.wait_ge(var_ready, t + 1)
                    pool.tensor_tensor(rnorm[:, :], ss[:, :], power[:, :], ALU.pow).then_inc(r_ready, 1)
                    pool.wait_ge(r_ready, 2 * t + 1)
                    pool.tensor_tensor(rnorm[:, :], rnorm[:, :], lifts[:, 1:2].to_broadcast([P, NT * 2]),
                                       ALU.mult).then_inc(r_ready, 1)
                    pool.wait_ge(r_ready, 2 * t + 2)
                    flat = qk[:, :, :, :].rearrange("p n j d -> p (n j) d")
                    pool.tensor_tensor(flat, flat, bcast(rnorm[:, :], 2, HD), ALU.mult).then_inc(qkn_ready, 1)

                split_weights(0, 0, 1)
                split_weights(1, 1, 1)
                normalise(0)
                with pool.Fori(0, (H - 2) // 2) as i:
                    for b in range(2):
                        normalise(2 * i + b + 1)
                        split_weights(2 * i + b + 2, b, i + 2)
                normalise(H - 1)

            @block.tensor
            def _(pe):
                def side(t, s, b):
                    kind, g = SIDE[s]
                    if not (isinstance(t, int) and t == 0 and s == 0):
                        pe.wait_ge(side_free, NS * t + s)
                    out = psum[:, SIDE_BANK, :]
                    if kind == "turn":
                        if g == 0:
                            pe.wait_ge(qkn_ready, t + 1)
                        for k in range(4):
                            last = pe.transpose(out[:, k * P:(k + 1) * P], qk[:, 4 * (g % 2) + k, g // 2, :], ident[:, :])
                    else:
                        if s == 0:
                            pe.wait_ge(w_ready, t + 1)
                        tiles, j0, j1 = (2, 0, 2) if kind == "qk" else (4, 2, 3)
                        cols = (j1 - j0) * HD
                        for k in range(tiles):
                            n = g * tiles + k
                            dst = out[:, k * cols:(k + 1) * cols]
                            for c in range(DC):
                                xh, xl = (x[:, c, n * P:(n + 1) * P] for x in (xT_h, xT_l))
                                wh, wl = (x[b][:, c, j0:j1, :].rearrange("p j d -> p (j d)") for x in (w_h, w_l))
                                pe.matmul(dst, xh, wh, start=(c == 0), stop=False)
                                pe.matmul(dst, xh, wl, start=False, stop=False)
                                last = pe.matmul(dst, xl, wh, start=False, stop=(c == DC - 1))
                    last.then_inc(side_ready, 1)

                def scores(t, m, b):
                    if m == 0:
                        pe.wait_ge(side_free, NS * t + TURN_LAST + 1)
                    if not (isinstance(t, int) and t == 0 and m < 2):
                        pe.wait_ge(exp_ready, QT * t + m - 1)
                    qh, ql = (x[b][:, 0, m * P:(m + 1) * P] for x in (qkT_h, qkT_l))
                    bank = S_BANK + 2 * (m % 2)
                    kh, kl = ([x[b][:, 1, f * HALF:(f + 1) * HALF] for f in range(2)] for x in (qkT_h, qkT_l))
                    for f in range(2):
                        pe.matmul(psum[:, bank + f, :], qh, kh[f], start=True, stop=False)
                    for f in range(2):
                        pe.matmul(psum[:, bank + f, :], qh, kl[f], start=False, stop=False)
                    for f in range(2):
                        last = pe.matmul(psum[:, bank + f, :], ql, kh[f], start=False, stop=True)
                    last.then_inc(s_ready, 1)

                def turn(t, m):
                    pe.wait_ge(p_ready, QT * t + m + 1)
                    if not (isinstance(t, int) and t == 0 and m == 0):
                        pe.wait_ge(pT_ready, QT * t + m)
                    for part in range(2):
                        for k in range(KT):
                            out = psum[:, T_BANK + part, :].bitcast(F16)[:, k * P:(k + 1) * P]
                            last = pe.transpose(out, pr[m % 2][:, part, k * P:(k + 1) * P], ident16[:, :])
                    last.then_inc(t_ready, 1)

                def values(t, g, piece, b):
                    if piece == 0:
                        pe.wait_ge(pT_ready, QT * t + 4 * g + 4)
                        pe.wait_ge(side_free, NS * t + V_LAST + 1)
                        if not (isinstance(t, int) and t == 0 and g == 0):
                            pe.wait_ge(o_free, 2 * t + g)
                    out = psum[:, O_BANK, :]
                    for k in (2 * piece, 2 * piece + 1):
                        ph, pl = (pT[g][:, part, k, :] for part in range(2))
                        pe.matmul(out, v_h[b][:, k, :], ph, start=(k == 0), stop=False)
                        pe.matmul(out, v_h[b][:, k, :], pl, start=False, stop=False)
                        last = pe.matmul(out, v_l[b][:, k, :], ph, start=False, stop=(k == KT - 1))
                    if piece == 3:
                        last.then_inc(pv_ready, 1)

                def head(t, b, first, end):
                    nb = 1 - b
                    for m in range(QT):
                        if not end:
                            sides(m, 0, lambda u, s: side(u, s, nb), t + 1)
                        if m < QT - 1:
                            scores(t, m + 1, b)
                        elif not end:
                            scores(t + 1, 0, nb)
                        if m > 0:
                            turn(t, m - 1)
                        elif not first:
                            turn(t - 1, QT - 1)
                        if not end:
                            sides(m, 1, lambda u, s: side(u, s, nb), t + 1)
                        if m >= 5:
                            values(t, 0, m - 5, b)
                        elif not first:
                            values(t - 1, *((0, 3) if m == 0 else (1, m - 1)), nb)

                for s in range(NS):
                    side(0, s, 0)
                scores(0, 0, 0)
                heads(pe, head)
                turn(H - 1, QT - 1)
                values(H - 1, 0, 3, (H - 1) % 2)
                for piece in range(4):
                    values(H - 1, 1, piece, (H - 1) % 2)

            @block.scalar
            def _(act):
                def side(t, s, b):
                    kind, g = SIDE[s]
                    act.wait_ge(side_ready, NS * t + s + 1)
                    bank = psum[:, SIDE_BANK, :]
                    later = not isinstance(t, int)
                    if kind == "qk":
                        if s == 0 and (later or t > 0):
                            act.wait_ge(side_ready, NS * (t - 1) + TURN_LAST + 1)
                        act.activation(qk[:, 2 * g:2 * g + 2, :, :].rearrange("p n j d -> p (n j d)"), bank,
                                               ACT.Copy).then_inc(side_free, 1)
                    elif kind == "turn":
                        j, at = g // 2, (g % 2) * HALF
                        act.activation(qkT_h[b][:, j, at:at + HALF], bank, ACT.Copy,
                                       scale=qk_scale[:, j:j + 1]).then_inc(side_high, 1)
                    else:
                        if g == 0 and (later or t >= 2):
                            act.wait_ge(pv_ready, 2 * t - 2)
                        act.activation(v_h[b][:, 4 * g:4 * g + 4, :].rearrange("p n d -> p (n d)"), bank, ACT.Copy,
                                       scale=1.0 / WSCALE).then_inc(side_high, 1)

                def exps(t, m):
                    act.wait_ge(max_ready, QT * t + m + 1)
                    if not (isinstance(t, int) and t == 0 and m < 2):
                        act.wait_ge(p_ready, QT * t + m - 1)
                    bank = S_BANK + 2 * (m % 2)
                    act.activation(ex[m % 2][:, :], psum[:, bank:bank + 2, :].rearrange("p a b -> p (a b)"), ACT.Exp,
                                   bias=nmax[:, m % 2:m % 2 + 1], accum_out=total[:, m % 2:m % 2 + 1]).then_inc(exp_ready, 1)

                def turned(t, m):
                    act.wait_ge(t_ready, QT * t + m + 1)
                    if m % 4 == 0 and (not isinstance(t, int) or t > 0):
                        act.wait_ge(pv_ready, 2 * (t - 1) + m // 4 + 1)
                    dst = pT[m // 4][:, :, :, (m % 4) * P:(m % 4 + 1) * P].bitcast(F32)
                    src = psum[:, T_BANK:T_BANK + 2, :].rearrange("p a (k q) -> p a k q", k=KT)
                    act.copy(dst, src).then_inc(pT_ready, 1)

                def outputs(t, g):
                    act.wait_ge(pv_ready, 2 * t + g + 1)
                    act.activation(oT_h[:, bass.ds(t, 1), g * HALF:(g + 1) * HALF],
                                   psum[:, O_BANK:O_BANK + 1, :], ACT.Copy, scale=1.0 / PROB).then_inc(o_high, 1)

                def head(t, b, first, end):
                    nb = 1 - b
                    for m in range(QT):
                        if not end:
                            sides(m, 0, lambda u, s: side(u, s, nb), t + 1)
                        if m > 0:
                            turned(t, m - 1)
                        elif not first:
                            turned(t - 1, QT - 1)
                        if m < QT - 1:
                            exps(t, m + 1)
                        elif not end:
                            exps(t + 1, 0)
                        if not end:
                            sides(m, 1, lambda u, s: side(u, s, nb), t + 1)
                        if not first and m == 0:
                            outputs(t - 1, 0)
                        if not first and m == 4:
                            outputs(t - 1, 1)

                act.wait_ge(scale_ready, 2)
                for s in range(NS):
                    side(0, s, 0)
                exps(0, 0)
                heads(act, head)
                turned(H - 1, QT - 1)
                outputs(H - 1, 0)
                outputs(H - 1, 1)

            @block.vector
            def _(dve):
                def side(t, s, b):
                    kind, g = SIDE[s]
                    bank = psum[:, SIDE_BANK, :]
                    if kind == "qk":
                        return
                    dve.wait_ge(side_high, len(LOWS) * t + LOWS.index(s) + 1)
                    if kind == "turn":
                        j, at = g // 2, (g % 2) * HALF
                        dve.scalar_tensor_tensor(qkT_l[b][:, j, at:at + HALF], bank, qk_scale[:, j:j + 1],
                                                 qkT_h[b][:, j, at:at + HALF], ALU.mult, ALU.subtract).then_inc(side_free, 1)
                    else:
                        four = slice(4 * g, 4 * g + 4)
                        dve.scalar_tensor_tensor(v_l[b][:, four, :].rearrange("p n d -> p (n d)"), bank, 1.0 / WSCALE,
                                                 v_h[b][:, four, :].rearrange("p n d -> p (n d)"),
                                                 ALU.mult, ALU.subtract).then_inc(side_free, 1)

                def squares(t):
                    dve.wait_ge(sq_ready, t + 1)
                    dve.reduce_sum(ss[:, :], sq[:, :, :, :].rearrange("p n j d -> p (n j) d"), AX.X).then_inc(ss_ready, 1)
                    dve.wait_ge(ss_ready, t + 1)
                    dve.tensor_scalar(ss[:, :], ss[:, :], 1.0 / (HD * WSCALE * WSCALE), RMS_EPS0, ALU.mult,
                                      ALU.add).then_inc(var_ready, 1)

                def maxima(t, m):
                    dve.wait_ge(s_ready, QT * t + m + 1)
                    if not (isinstance(t, int) and t == 0 and m < 2):
                        dve.wait_ge(exp_ready, QT * t + m - 1)
                    bank = S_BANK + 2 * (m % 2)
                    dve.tensor_reduce(nmax[:, m % 2:m % 2 + 1], psum[:, bank:bank + 2, :].rearrange("p a b -> p (a b)"),
                                      AX.X, ALU.max, negate=True).then_inc(max_ready, 1)

                def split(t, m):
                    k = m % 2
                    dve.wait_ge(exp_ready, QT * t + m + 1)
                    dve.tensor_scalar(tsc[:, k:k + 1], total[:, k:k + 1], 1.0 / PROB, None, ALU.mult).then_inc(tsc_ready, 1)
                    dve.wait_ge(tsc_ready, QT * t + m + 1)
                    dve.reciprocal(rtot[:, k:k + 1], tsc[:, k:k + 1]).then_inc(rt_ready, 1)
                    dve.wait_ge(rt_ready, QT * t + m + 1)
                    if not (isinstance(t, int) and t == 0 and m < 2):
                        dve.wait_ge(t_ready, QT * t + m - 1)
                    dve.tensor_scalar(pr[k][:, 0, :], ex[k][:, :], rtot[:, k:k + 1], None, ALU.mult).then_inc(ph_ready, 1)
                    dve.wait_ge(ph_ready, QT * t + m + 1)
                    dve.scalar_tensor_tensor(pr[k][:, 1, :], ex[k][:, :], rtot[:, k:k + 1], pr[k][:, 0, :],
                                             ALU.mult, ALU.subtract).then_inc(p_ready, 1)

                def outputs(t, g):
                    dve.wait_ge(o_high, 2 * t + g + 1)
                    at = (slice(None), bass.ds(t, 1), slice(g * HALF, (g + 1) * HALF))
                    dve.scalar_tensor_tensor(oT_l[at], psum[:, O_BANK:O_BANK + 1, :], 1.0 / PROB, oT_h[at],
                                             ALU.mult, ALU.subtract).then_inc(o_free, 1)

                def head(t, b, first, end):
                    nb = 1 - b
                    for m in range(QT):
                        if not first and m in (1, 5):
                            outputs(t - 1, m // 5)
                        if not end:
                            sides(m, 0, lambda u, s: side(u, s, nb), t + 1)
                        if not end and m == NORM_SLOT:
                            squares(t + 1)
                        if m < QT - 1:
                            maxima(t, m + 1)
                        elif not end:
                            maxima(t + 1, 0)
                        if not end:
                            sides(m, 1, lambda u, s: side(u, s, nb), t + 1)
                        if m < QT - 1:
                            split(t, m + 1)
                        elif not end:
                            split(t + 1, 0)

                for s in range(NS):
                    if s == QK_LAST + 1:
                        squares(0)
                    side(0, s, 0)
                maxima(0, 0)
                split(0, 0)
                heads(dve, head)
                outputs(H - 1, 0)
                outputs(H - 1, 1)


def project0(nc, env, w):
    sem, psum = env["sem"], env["psum"]
    oT_h, oT_l, x, gate0 = (env[k] for k in ("oT_h", "oT_l", "x", "gate0"))
    with ExitStack() as local:
        def tmp(name, shape, dt=F32):
            return local.enter_context(nc.sbuf_tensor("p0_" + name, shape, dt))
        HQ = 4
        wf = [tmp(f"wf{b}", [P, HQ, D]) for b in range(2)]
        wo_h, wo_l = tmp("wo_h", [P, H, D], F16), tmp("wo_l", [P, H, D], F16)
        sg = [tmp(f"sg{b}", [P, D]) for b in range(2)]
        loaded = [sem(f"p0_ld{b}") for b in range(2)]
        wh_ready, w_ready, y_ready, sg_ready, x_ready = (sem("p0_" + s) for s in ("wh", "w", "y", "sg", "x"))
        wo = w["L0_attn_wo"].rearrange("h d e -> d h e")
        with nc.Block() as block:
            @block.sync
            def _(sp):
                for q in range(H // HQ):
                    if q >= 2:
                        sp.wait_ge(w_ready, q - 1)
                    sp.dma_start(wf[q % 2][:, :, :], wo[:, q * HQ:(q + 1) * HQ, :]).then_inc(loaded[q % 2], 16)

            @block.scalar
            def _(act):
                for q in range(H // HQ):
                    act.wait_ge(loaded[q % 2], 16 * (q // 2 + 1))
                    act.activation(wo_h[:, q * HQ:(q + 1) * HQ, :], wf[q % 2][:, :, :], ACT.Copy,
                                   scale=WSCALE).then_inc(wh_ready, 1)

            @block.vector
            def _(dve):
                for q in range(H // HQ):
                    dve.wait_ge(wh_ready, q + 1)
                    part = (slice(None), slice(q * HQ, (q + 1) * HQ))
                    dve.scalar_tensor_tensor(wo_l[part], wf[q % 2][:, :, :], WSCALE, wo_h[part],
                                             ALU.mult, ALU.subtract).then_inc(w_ready, 1)
                for n in range(NT):
                    dve.wait_ge(y_ready, n + 1)
                    if n >= 2:
                        dve.wait_ge(x_ready, n - 1)
                    dve.scalar_tensor_tensor(sg[n % 2][:, :], psum[:, n, 0:D], 1.0 / WSCALE, gate0[:, n, :],
                                             ALU.mult, ALU.mult).then_inc(sg_ready, 1)
                    dve.wait_ge(sg_ready, n + 1)
                    dve.tensor_tensor(x[:, n, :], x[:, n, :], sg[n % 2][:, :], ALU.add).then_inc(x_ready, 1)

            @block.tensor
            def _(pe):
                for q in range(H // HQ):
                    pe.wait_ge(w_ready, q + 1)
                    for n in range(NT):
                        for h in range(q * HQ, (q + 1) * HQ):
                            oh, ol = (o[:, h, n * P:(n + 1) * P] for o in (oT_h, oT_l))
                            pe.matmul(psum[:, n, 0:D], oh, wo_h[:, h, :], start=(h == 0), stop=False)
                            pe.matmul(psum[:, n, 0:D], oh, wo_l[:, h, :], start=False, stop=False)
                            last = pe.matmul(psum[:, n, 0:D], ol, wo_h[:, h, :], start=False, stop=(h == H - 1))
                        if q == H // HQ - 1:
                            last.then_inc(y_ready, 1)


def gated_linear_attention(nc, env, w):
    sem, psum, ident = env["sem"], env["psum"], env["ident"]
    spread, gather_h, xn, s1 = (env[k] for k in ("spread", "gather_h", "xn", "s1"))
    KD = GH * GK
    G1 = 16
    FT = -(-HID // P)
    with ExitStack() as outer:
        def keep(name, shape, dt=F32):
            return outer.enter_context(nc.sbuf_tensor("g1_" + name, shape, dt))
        ln = keep("ln", [P, 2, DC])
        ms, inv, sq = keep("ms", [P, NT]), keep("inv", [P, NT]), keep("sq", [P, D])
        silu_g = keep("silu_g", [P, NT, D])
        o = keep("o", [P, NT, D])
        ln_loaded = [sem(f"g1_lnl{i}") for i in range(2)]

        def rms_turned(tag, source, which, xT):
            ss_done, ms_done, rt_done, inv_done, xr_ready, t_ready, evac = (
                sem(tag + s) for s in ("ss", "ms", "rt", "iv", "xr", "t", "e"))
            with ExitStack() as inner:
                xr = inner.enter_context(nc.sbuf_tensor(tag + "_xr", [P, NT, D], F32))
                with nc.Block() as block:
                    @block.vector
                    def _(dve):
                        dve.wait_ge(ss_done, NT)
                        dve.tensor_scalar(ms[:, :], ms[:, :], 1.0 / D, RMS_EPS1, ALU.mult, ALU.add).then_inc(ms_done, 1)
                        dve.wait_ge(rt_done, 1)
                        dve.reciprocal(inv[:, :], inv[:, :]).then_inc(inv_done, 1)
                        dve.wait_ge(inv_done, 1)
                        for n in range(NT):
                            dve.tensor_scalar(xr[:, n, :], source[:, n, :], inv[:, n:n + 1], None, ALU.mult).then_inc(xr_ready, 1)

                    @block.scalar
                    def _(act):
                        for n in range(NT):
                            if n:
                                act.wait_ge(ss_done, n)
                            act.activation(sq[:, :], source[:, n, :], ACT.Square, accum_out=ms[:, n:n + 1]).then_inc(ss_done, 1)
                        act.wait_ge(ms_done, 1)
                        act.activation(inv[:, :], ms[:, :], ACT.Sqrt).then_inc(rt_done, 1)
                        act.wait_ge(ln_loaded[which], 16)
                        for n in range(NT):
                            act.wait_ge(t_ready, n + 1)
                            for c in range(DC):
                                last = act.activation(xT[:, c, n * P:(n + 1) * P], psum[:, n % 2, c * P:(c + 1) * P],
                                                      ACT.Copy, scale=ln[:, which, c:c + 1])
                            last.then_inc(evac, 1)

                    @block.tensor
                    def _(pe):
                        for n in range(NT):
                            pe.wait_ge(xr_ready, n + 1)
                            if n >= 2:
                                pe.wait_ge(evac, n - 1)
                            for c in range(DC):
                                last = pe.transpose(psum[:, n % 2, c * P:(c + 1) * P], xr[:, n, c * P:(c + 1) * P], ident[:, :])
                            last.then_inc(t_ready, 1)

        with ExitStack() as local:
            def tmp(name, shape, dt=F32):
                return local.enter_context(nc.sbuf_tensor("g1_" + name, shape, dt))
            xT = tmp("xT", [P, DC, T])
            wq, wk = tmp("wq", [P, DC, KD]), tmp("wk", [P, DC, KD])
            wg1, wg2, bg2 = tmp("wg1", [P, DC, G1]), tmp("wg2", [G1, KD]), tmp("bg2", [P, 1])
            wv, wg, bg = tmp("wv", [P, DC, D]), tmp("wg", [P, DC, D]), tmp("bg", [P, D])
            wv_dh = tmp("wv_dh", [P, DC, D])
            wv_ready = sem("g1_wv")
            loads = [(wq, w["L1_attn_Wq"]), (wk, w["L1_attn_Wk"]), (wg1, w["L1_attn_Wkg1"]), (wv, w["L1_attn_Wv"]),
                     (wg, w["L1_attn_Wg"])]
            w_loaded = [sem(f"g1_wl{i}") for i in range(len(loads) + 3)]
            with nc.Block() as block:
                @block.sync
                def _(sp):
                    for i, name in enumerate(("L1_attn_ln1_w", "L1_attn_ln2_w")):
                        sp.dma_start(ln[:, i, :], w[name].rearrange("(c p) -> p c", p=P), allow_slow_non_contiguous=True).then_inc(ln_loaded[i], 16)
                    for i, (dst, src) in enumerate(loads):
                        sp.dma_start(dst[:, :, :], src.rearrange("(c p) n -> p c n", p=P)).then_inc(w_loaded[i], 16)
                    sp.dma_start(wg2[:, :], w["L1_attn_Wkg2"]).then_inc(w_loaded[5], 16)
                    sp.dma_start(bg2[:, :], w["L1_attn_bkg2"].rearrange("(p a) -> p a", a=1)).then_inc(w_loaded[6], 16)
                    sp.dma_start(bg[:, :], w["L1_attn_bg"].partition_broadcast(P)).then_inc(w_loaded[7], 16)
            rms_turned("g1_r1", xn, 0, xT)

            qT, kT = tmp("qT", [P, T]), tmp("kT", [P, T])
            mid = tmp("mid", [G1, T])
            z, e, dec = tmp("z", [P, T]), tmp("e", [P, T]), tmp("dec", [P, T])
            v_h, v_l = tmp("v_h", [P, 2, T], F16), tmp("v_l", [P, 2, T], F16)
            q_ready, mid_ready, mid_done, z_ready, v_ready, g_ready = (sem("g1_" + s) for s in ("q", "m", "md", "z", "v", "g"))
            qk_done, act_done, dve_done, vh_done, g_added, g_free, v_free = (sem("g1_" + s) for s in ("qd", "ad", "dd", "vh", "ga", "gf", "vf"))

            def both(pe, banks, lhs, rhs_of, rows=P):
                for half in range(2):
                    for c in range(DC):
                        last = pe.matmul(psum[0:rows, banks + half, :], lhs(c), rhs_of(c, half),
                                         start=(c == 0), stop=(c == DC - 1))
                return last

            with nc.Block() as block:
                @block.tensor
                def _(pe):
                    for i in range(len(loads) + 1):
                        pe.wait_ge(w_loaded[i], 16)

                    def x_of(c, half):
                        return xT[:, c, half * HALF:(half + 1) * HALF]
                    both(pe, 0, lambda c: wg1[:, c, :], x_of, G1).then_inc(mid_ready, 1)
                    both(pe, 2, lambda c: wq[:, c, :], x_of).then_inc(q_ready, 1)
                    both(pe, 4, lambda c: wk[:, c, :], x_of).then_inc(q_ready, 1)
                    pe.wait_ge(mid_done, 1)
                    for half in range(2):
                        last = pe.matmul(psum[:, 6 + half, :], wg2[:, :], mid[:, half * HALF:(half + 1) * HALF],
                                         start=True, stop=True)
                    last.then_inc(z_ready, 1)
                    pe.wait_ge(qk_done, 1)
                    pe.wait_ge(wv_ready, DC)
                    for cv in range(2):
                        both(pe, 2 * cv, lambda c: wv_dh[:, c, cv * P:(cv + 1) * P], x_of).then_inc(v_ready, 1)
                    for n in range(NT):
                        if n == 0:
                            pe.wait_ge(qk_done, 2)
                        if n >= 2:
                            pe.wait_ge(g_added, n - 1)
                        for c in range(DC):
                            last = pe.matmul(psum[:, 4 + n % 2, 0:D], xT[:, c, n * P:(n + 1) * P], wg[:, c, :],
                                             start=(c == 0), stop=(c == DC - 1))
                        last.then_inc(g_ready, 1)

                @block.gpsimd
                def _(pool):
                    pool.wait_ge(w_loaded[3], 16)
                    for c in range(DC):
                        pool.tensor_copy(wv_dh[:, c, :].rearrange("p (c d h) -> p c d h", c=2, d=8),
                                         wv[:, c, :].rearrange("p (h c d) -> p c d h", c=2, d=8)).then_inc(wv_ready, 1)

                def two(bank):
                    return psum[:, bank:bank + 2, :].rearrange("p a b -> p (a b)")

                @block.scalar
                def _(act):
                    chain = Chain(act, act_done)
                    act.wait_ge(mid_ready, 1)
                    act.activation(mid[:, :], psum[0:G1, 0:2, :].rearrange("p a b -> p (a b)"), ACT.Copy).then_inc(mid_done, 1)
                    act.wait_ge(q_ready, 1)
                    act.activation(qT[:, :], two(2), ACT.Copy).then_inc(qk_done, 1)
                    act.wait_ge(q_ready, 2)
                    act.activation(kT[:, :], two(4), ACT.Copy, scale=float(GV) ** -0.5).then_inc(qk_done, 1)
                    act.wait_ge(z_ready, 1)
                    act.wait_ge(w_loaded[6], 16)
                    chain(act.activation(z[:, :], two(6), ACT.Identity, bias=bg2[:, 0:1]))
                    chain(act.activation(e[:, :], z[:, :], ACT.Abs))
                    chain(act.activation(e[:, :], e[:, :], ACT.Exp, scale=-1.0))
                    chain(act.activation(e[:, :], e[:, :], ACT.Ln, bias=1.0))
                    act.wait_ge(dve_done, 1)
                    chain(act.activation(dec[:, :], z[:, :], ACT.Exp, scale=1.0 / GATE_NORM))
                    for cv in range(2):
                        act.wait_ge(v_ready, cv + 1)
                        act.activation(v_h[:, cv, :], two(2 * cv), ACT.Copy).then_inc(vh_done, 1)
                    act.wait_ge(g_added, NT)
                    act.activation(silu_g[:, :, :], silu_g[:, :, :], ACT.Silu).then_inc(g_free, 1)

                @block.vector
                def _(dve):
                    dve.wait_ge(act_done, 4)
                    dve.scalar_tensor_tensor(z[:, :], z[:, :], 0.0, e[:, :], ALU.min, ALU.subtract).then_inc(dve_done, 1)
                    for cv in range(2):
                        dve.wait_ge(vh_done, cv + 1)
                        dve.tensor_tensor(v_l[:, cv, :], two(2 * cv), v_h[:, cv, :], ALU.subtract).then_inc(v_free, 1)
                    dve.wait_ge(w_loaded[7], 16)
                    for n in range(NT):
                        dve.wait_ge(g_ready, n + 1)
                        dve.tensor_tensor(silu_g[:, n, :], psum[:, 4 + n % 2, 0:D], bg[:, :], ALU.add).then_inc(g_added, 1)

            kv = [tmp(f"kv{b}", [P, T]) for b in range(2)]
            state = [tmp(f"state{b}", [P, T]) for b in range(2)]
            qs = [tmp(f"qs{b}", [P, T]) for b in range(2)]
            v_spread, kv_ready, st_ready, qs_ready, o_step = (sem("g2_" + s) for s in ("v", "kv", "st", "qs", "o"))
            oT = tmp("oT", [P, 2, T])
            oT_done = sem("g2_oT")
            STEPS = 2 * GK
            with nc.Block() as block:
                @block.tensor
                def _(pe):
                    def spread_values(s):
                        cv, dd = s // 8, s % 8
                        if s >= 2:
                            pe.wait_ge(kv_ready, s - 1)
                        for half in range(2):
                            cols = slice(half * HALF, (half + 1) * HALF)
                            pe.matmul(psum[:, 2 * (s % 2) + half, :], spread[:, dd, :], v_h[:, cv, cols], start=True, stop=False)
                            last = pe.matmul(psum[:, 2 * (s % 2) + half, :], spread[:, dd, :], v_l[:, cv, cols],
                                             start=False, stop=True)
                        last.then_inc(v_spread, 1)

                    spread_values(0)
                    for s in range(STEPS):
                        if s + 1 < STEPS:
                            spread_values(s + 1)
                        cv, dd = s // 8, s % 8
                        pe.wait_ge(qs_ready, s + 1)
                        for half in range(2):
                            last = pe.matmul(psum[:, 4 + 2 * cv + half, :], gather_h[:, dd, :],
                                             qs[s % 2][:, half * HALF:(half + 1) * HALF], start=(dd == 0), stop=(dd == 7))
                        last.then_inc(o_step, 1)

                @block.vector
                def _(dve):
                    for s in range(STEPS):
                        dve.wait_ge(v_spread, s + 1)
                        if s >= 2:
                            dve.wait_ge(st_ready, s - 1)
                        dve.tensor_tensor(kv[s % 2][:, :], kT[:, :], psum[:, 2 * (s % 2):2 * (s % 2) + 2, :].rearrange("p a b -> p (a b)"),
                                          ALU.mult).then_inc(kv_ready, 1)
                        dve.wait_ge(kv_ready, s + 1)
                        if s >= 2:
                            dve.wait_ge(qs_ready, s - 1)
                        dve.tensor_tensor_scan(state[s % 2][:, :], dec[:, :], kv[s % 2][:, :], 0.0, ALU.mult,
                                               ALU.add).then_inc(st_ready, 1)

                @block.gpsimd
                def _(pool):
                    for s in range(STEPS):
                        pool.wait_ge(st_ready, s + 1)
                        if s >= 2:
                            pool.wait_ge(o_step, s - 1)
                        pool.tensor_tensor(qs[s % 2][:, :], qT[:, :], state[s % 2][:, :], ALU.mult).then_inc(qs_ready, 1)

                @block.scalar
                def _(act):
                    for cv in range(2):
                        act.wait_ge(o_step, 8 * (cv + 1))
                        act.activation(oT[:, cv, :], psum[:, 4 + 2 * cv:6 + 2 * cv, :].rearrange("p a b -> p (a b)"),
                                       ACT.Copy).then_inc(oT_done, 1)

            t_ready, o_done = sem("g3_t"), sem("g3_o")
            with nc.Block() as block:
                @block.tensor
                def _(pe):
                    for n in range(NT):
                        if n >= 2:
                            pe.wait_ge(o_done, n - 1)
                        for cv in range(2):
                            last = pe.transpose(psum[:, n % 2, cv * P:(cv + 1) * P], oT[:, cv, n * P:(n + 1) * P], ident[:, :])
                        last.then_inc(t_ready, 1)

                @block.scalar
                def _(act):
                    for n in range(NT):
                        act.wait_ge(t_ready, n + 1)
                        act.activation(o[:, n, :].rearrange("p (h c d) -> p c d h", c=2, d=8),
                                       psum[:, n % 2, 0:D].rearrange("p (c d h) -> p c d h", c=2, d=8), ACT.Copy).then_inc(o_done, 1)

        with ExitStack() as local:
            def tmp(name, shape, dt=F32):
                return local.enter_context(nc.sbuf_tensor("g4_" + name, shape, dt))
            mean, var, std = (tmp(n, [P, NT * GH]) for n in ("mean", "var", "std"))
            big = tmp("big", [P, NT * GH, GV])
            wo = tmp("wo", [P, DC, D])
            ogT = tmp("ogT", [P, DC, T])
            wo_loaded, dve_done, sq_done, rt_done, og_ready, t_ready, evac, y_ready, s_done = (
                sem("g4_" + s) for s in ("wl", "d", "sq", "rt", "og", "t", "e", "y", "s"))
            oh = o[:, :, :].rearrange("p n (h d) -> p (n h) d", h=GH)
            with nc.Block() as block:
                @block.sync
                def _(sp):
                    sp.dma_start(wo[:, :, :], w["L1_attn_Wo"].rearrange("(c p) n -> p c n", p=P)).then_inc(wo_loaded, 16)

                @block.vector
                def _(dve):
                    chain = Chain(dve, dve_done)
                    chain(dve.reduce_sum(mean[:, :], oh, AX.X))
                    chain(dve.tensor_scalar(mean[:, :], mean[:, :], 1.0 / GV, None, ALU.mult))
                    chain(dve.tensor_tensor(oh, oh, bcast(mean[:, :], 2, GV), ALU.subtract))
                    dve.wait_ge(sq_done, 1)
                    chain(dve.reduce_sum(var[:, :], big[:, :, :], AX.X))
                    chain(dve.tensor_scalar(var[:, :], var[:, :], 1.0 / GV, RMS_EPS1, ALU.mult, ALU.add))
                    dve.wait_ge(rt_done, 1)
                    chain(dve.reciprocal(std[:, :], std[:, :]))
                    chain(dve.tensor_tensor(oh, oh, bcast(std[:, :], 2, GV), ALU.mult))
                    dve.tensor_tensor(o[:, :, :], o[:, :, :], silu_g[:, :, :], ALU.mult).then_inc(og_ready, 1)
                    for n in range(NT):
                        dve.wait_ge(y_ready, n + 1)
                        dve.tensor_tensor(s1[:, n, :], psum[:, 2 + n % 2, 0:D], xn[:, n, :], ALU.add).then_inc(s_done, 1)

                @block.scalar
                def _(act):
                    act.wait_ge(dve_done, 3)
                    act.activation(big[:, :, :], oh, ACT.Square).then_inc(sq_done, 1)
                    act.wait_ge(dve_done, 5)
                    act.activation(std[:, :], var[:, :], ACT.Sqrt).then_inc(rt_done, 1)
                    for n in range(NT):
                        act.wait_ge(t_ready, n + 1)
                        act.activation(ogT[:, :, n * P:(n + 1) * P], psum[:, n % 2, 0:D].rearrange("p (c t) -> p c t", c=DC),
                                       ACT.Copy).then_inc(evac, 1)

                @block.tensor
                def _(pe):
                    pe.wait_ge(og_ready, 1)
                    pe.wait_ge(wo_loaded, 16)
                    for n in range(NT):
                        if n >= 2:
                            pe.wait_ge(evac, n - 1)
                        for c in range(DC):
                            last = pe.transpose(psum[:, n % 2, c * P:(c + 1) * P], o[:, n, c * P:(c + 1) * P], ident[:, :])
                        last.then_inc(t_ready, 1)
                    for n in range(NT):
                        pe.wait_ge(evac, n + 1)
                        if n >= 2:
                            pe.wait_ge(s_done, n - 1)
                        for c in range(DC):
                            last = pe.matmul(psum[:, 2 + n % 2, 0:D], ogT[:, c, n * P:(n + 1) * P], wo[:, c, :],
                                             start=(c == 0), stop=(c == DC - 1))
                        last.then_inc(y_ready, 1)

        with ExitStack() as local:
            def tmp(name, shape, dt=F32):
                return local.enter_context(nc.sbuf_tensor("m1_" + name, shape, dt))
            xT = tmp("xT", [P, DC, T])
            rms_turned("g1_r2", s1, 1, xT)
            w1, w3, w2 = tmp("w1", [P, DC, HID]), tmp("w3", [P, DC, HID]), tmp("w2", [P, FT, D])
            sg = tmp("sg", [P, 2, HALF])
            hT = tmp("hT", [P, FT, T])
            REST = HID - (FT - 1) * P
            loaded = [sem(f"m1_l{i}") for i in range(4)]
            gu_ready, silu_done, h_ready, y_ready, y_done = (sem("m1_" + s) for s in ("gu", "si", "h", "y", "yd"))
            with nc.Block() as block:
                @block.sync
                def _(sp):
                    sp.dma_start(w1[:, :, :], w["L1_attn_W1"].rearrange("(c p) n -> p c n", p=P)).then_inc(loaded[0], 16)
                    sp.dma_start(w3[:, :, :], w["L1_attn_W3"].rearrange("(c p) n -> p c n", p=P)).then_inc(loaded[1], 16)
                    sp.dma_start(w2[:, 0:FT - 1, :], w["L1_attn_W2"][0:(FT - 1) * P, :].rearrange("(f p) n -> p f n", p=P)).then_inc(loaded[2], 16)
                    sp.dma_start(w2[0:REST, FT - 1, :], w["L1_attn_W2"][(FT - 1) * P:HID, :]).then_inc(loaded[3], 16)

                steps = [(f, half) for f in range(FT) for half in range(2)]

                @block.tensor
                def _(pe):
                    pe.wait_ge(loaded[0], 16)
                    pe.wait_ge(loaded[1], 16)
                    for s, (f, half) in enumerate(steps):
                        rows = min(P, HID - f * P)
                        if s >= 2:
                            pe.wait_ge(h_ready, s - 1)
                        for j, wt in enumerate((w1, w3)):
                            for c in range(DC):
                                last = pe.matmul(psum[0:rows, 2 * (s % 2) + j, :], wt[:, c, f * P:f * P + rows],
                                                 xT[:, c, half * HALF:(half + 1) * HALF], start=(c == 0), stop=(c == DC - 1))
                        last.then_inc(gu_ready, 1)
                    pe.wait_ge(h_ready, len(steps))
                    pe.wait_ge(loaded[2], 16)
                    pe.wait_ge(loaded[3], 16)
                    for n in range(NT):
                        if n >= 4:
                            pe.wait_ge(y_done, n - 3)
                        for f in range(FT):
                            rows = min(P, HID - f * P)
                            last = pe.matmul(psum[:, 4 + n % 4, 0:D], hT[0:rows, f, n * P:(n + 1) * P], w2[0:rows, f, :],
                                             start=(f == 0), stop=(f == FT - 1))
                        last.then_inc(y_ready, 1)

                @block.scalar
                def _(act):
                    for s, (f, half) in enumerate(steps):
                        rows = min(P, HID - f * P)
                        act.wait_ge(gu_ready, s + 1)
                        if s >= 2:
                            act.wait_ge(h_ready, s - 1)
                        act.activation(sg[0:rows, s % 2, :], psum[0:rows, 2 * (s % 2), :], ACT.Silu).then_inc(silu_done, 1)

                @block.vector
                def _(dve):
                    for s, (f, half) in enumerate(steps):
                        rows = min(P, HID - f * P)
                        dve.wait_ge(silu_done, s + 1)
                        dve.tensor_tensor(hT[0:rows, f, half * HALF:(half + 1) * HALF], psum[0:rows, 2 * (s % 2) + 1, :],
                                          sg[0:rows, s % 2, :], ALU.mult).then_inc(h_ready, 1)
                    for n in range(NT):
                        dve.wait_ge(y_ready, n + 1)
                        dve.tensor_tensor(s1[:, n, :], s1[:, n, :], psum[:, 4 + n % 4, 0:D], ALU.add).then_inc(y_done, 1)


def route1(nc, env, router_w, router_bias, comb_dram):
    sem, psum, ident, xnT = env["sem"], env["psum"], env["ident"], env["xnT"]
    with ExitStack() as local:
        def tmp(name, shape, dt=F32):
            return local.enter_context(nc.sbuf_tensor("r1_" + name, shape, dt))
        rw, bias = tmp("rw", [P, DC, E1]), tmp("bias", [P, E1])
        es, er, sel = tmp("es", [P, NT, E1 + 8]), tmp("er", [P, NT, E1 + 8]), tmp("sel", [P, NT, E1])
        best, named = tmp("best", [P, NT, 8]), tmp("named", [P, NT, 8])
        shifted, prob, comb = tmp("shifted", [P, NT, E1]), tmp("prob", [P, NT, E1]), tmp("comb", [P, NT, E1])
        top, total = tmp("top", [P, NT]), tmp("total", [P, NT])
        combT = tmp("combT", [E1, T])
        loaded = [sem(f"r1_ld{i}") for i in range(2)]
        logits_ready, dve_done, exp_ready, comb_ready, t_ready, ct_ready, stored = (
            sem("r1_" + s) for s in ("lg", "d", "ex", "cb", "t", "ct", "st"))
        logits = psum[:, 0, :].rearrange("p (n e) -> p n e", n=NT)
        with nc.Block() as block:
            @block.sync
            def _(sp):
                sp.dma_start(rw[:, :, :], router_w.rearrange("(c p) e -> p c e", p=P)).then_inc(loaded[0], 16)
                sp.dma_start(bias[:, :], router_bias.partition_broadcast(P)).then_inc(loaded[1], 16)
                sp.wait_ge(ct_ready, 1)
                sp.dma_start(comb_dram, combT[:, :]).then_inc(stored, 16)
                sp.wait_ge(stored, 16)

            @block.tensor
            def _(pe):
                pe.wait_ge(loaded[0], 16)
                for n in range(NT):
                    for c in range(DC):
                        last = pe.matmul(logits[:, n, :], xnT[:, c, n * P:(n + 1) * P], rw[:, c, :],
                                         start=(c == 0), stop=(c == DC - 1))
                last.then_inc(logits_ready, 1)
                pe.wait_ge(comb_ready, 1)
                for n in range(NT):
                    last = pe.transpose(psum[0:E1, 2 + n // 4, (n % 4) * P:(n % 4 + 1) * P], comb[:, n, :], ident[:, :])
                last.then_inc(t_ready, 1)

            @block.scalar
            def _(act):
                act.wait_ge(dve_done, 2)
                act.activation(prob[:, :, :], shifted[:, :, :], ACT.Exp).then_inc(exp_ready, 1)
                act.wait_ge(t_ready, 1)
                act.activation(combT[:, :], psum[0:E1, 2:4, :].rearrange("p a b -> p (a b)"), ACT.Copy).then_inc(ct_ready, 1)

            @block.vector
            def _(dve):
                chain = Chain(dve, dve_done)
                dve.wait_ge(logits_ready, 1)
                dve.wait_ge(loaded[1], 16)
                chain(dve.reduce_max(top[:, :], logits, AX.X))
                chain(dve.tensor_tensor(shifted[:, :, :], logits, bcast(top[:, :], 2, E1), ALU.subtract))
                chain(dve.memset(es[:, :, :], SENTINEL))
                chain(dve.tensor_tensor(es[:, :, 0:E1], logits, bcast(bias[:, :], 1, NT), ALU.add))
                top_k_mask(dve, chain, es[:, :, :], K1, best[:, :, :], named[:, :, :], er[:, :, :], sel[:, :, :])
                dve.wait_ge(exp_ready, 1)
                chain(dve.reduce_sum(total[:, :], prob[:, :, :], AX.X))
                chain(dve.reciprocal(total[:, :], total[:, :]))
                chain(dve.tensor_tensor(prob[:, :, :], prob[:, :, :], bcast(total[:, :], 2, E1), ALU.mult))
                chain(dve.tensor_tensor(prob[:, :, :], prob[:, :, :], sel[:, :, :], ALU.mult))
                chain(dve.reduce_sum(total[:, :], prob[:, :, :], AX.X))
                chain(dve.reciprocal(total[:, :], total[:, :]))
                dve.tensor_tensor(comb[:, :, :], prob[:, :, :], bcast(total[:, :], 2, E1), ALU.mult).then_inc(comb_ready, 1)


def mixture1(nc, env, w, out):
    sem, psum, ident = env["sem"], env["psum"], env["ident"]
    xnT, x, s1 = env["xnT"], env["x"], env["s1"]
    PAIRS = E1 // 2
    STEPS = PAIRS + SH1 // P
    NW = 3 * DC
    comb_dram = nc.dram_tensor("comb_by_expert", [E1, T], F32, kind="Internal").ap()
    route1(nc, env, w["L1_ffn_router_w"], w["L1_ffn_router_bias"], comb_dram)
    with ExitStack() as local:
        def tmp(name, shape, dt=F32):
            return local.enter_context(nc.sbuf_tensor("e1_" + name, shape, dt))
        xT_h, xT_l = tmp("xTh", [P, DC, T], F16), tmp("xTl", [P, DC, T], F16)
        split16(nc, env, "e1_x", [(xnT[:, :, :], xT_h[:, :, :], xT_l[:, :, :])])
        wf = [tmp(f"wf{b}", [P, NW, P]) for b in range(2)]
        w_h = [tmp(f"wh{b}", [P, NW, P], F16) for b in range(2)]
        w_l = [tmp(f"wl{b}", [P, NW, P], F16) for b in range(2)]
        cb = [tmp(f"cb{b}", [P, T]) for b in range(2)]
        sg = [tmp(f"sg{b}", [P, HALF]) for b in range(2)]
        hf = [tmp(f"hf{b}", [P, HALF]) for b in range(2)]
        h_h = [tmp(f"hh{b}", [P, HALF], F16) for b in range(4)]
        h_l = [tmp(f"hl{b}", [P, HALF], F16) for b in range(4)]
        yT = tmp("yT", [P, DC, T])
        gate1 = [tmp(f"gate{b}", [P, D]) for b in range(2)]
        prod = [tmp(f"prod{b}", [P, D]) for b in range(2)]
        w_loaded = [sem(f"e1_wl{b}") for b in range(2)]
        cb_loaded = [sem(f"e1_cl{b}") for b in range(2)]
        (wh_ready, w_ready, gu_ready, silu_ready, mixed, h_ready, hh_ready, hl_ready, down_done, y_ready,
         t_ready, g_ready, p_ready, x_ready, stored) = (sem("e1_" + s) for s in (
             "wh", "w", "gu", "si", "mi", "h", "hh", "hl", "dn", "y", "t", "g", "p", "x", "st"))
        LOADS = 5 * 16
        wg, wu, wd = (w["L1_ffn_" + k] for k in ("wg", "wu", "wd"))
        swg, swu, swd = (w["L1_ffn_" + k] for k in ("swg", "swu", "swd"))

        def steps(engine, step):
            for s in range(2):
                step(s, s, False)
            with engine.Fori(0, PAIRS // 2) as i:
                for b in range(2):
                    step(2 * i + 2 + b, b, True)
            for s in range(STEPS - 2, STEPS):
                step(s, s % 2, False)

        with nc.Block() as block:
            @block.sync
            def _(sp):
                def load_shared(q, b):
                    e, at = q // 2, (q % 2) * P
                    for j, src in enumerate((swg, swu)):
                        for c in range(DC):
                            sp.dma_start(wf[b][:, DC * j + c, :], src[e, c * P:(c + 1) * P, at:at + P]).then_inc(w_loaded[b], 16)
                    sp.dma_start(wf[b][:, 2 * DC:, :].rearrange("p c d -> p (c d)"), swd[e, at:at + P, :]).then_inc(w_loaded[b], 16)

                def load_routed(pair, b):
                    for j, src in enumerate((wg, wu)):
                        for c in range(DC):
                            sp.dma_start(wf[b][:, DC * j + c, :].rearrange("p (e f) -> p e f", e=2),
                                         src[bass.ds(2 * pair, 2), c * P:(c + 1) * P, :].rearrange("e p f -> p e f"))\
                              .then_inc(w_loaded[b], 16)
                    sp.dma_start(wf[b][:, 2 * DC:, :].rearrange("p c d -> p (c d)"),
                                 wd[bass.ds(2 * pair, 2), :, :].rearrange("e f d -> (e f) d")).then_inc(w_loaded[b], 16)

                def load_comb(pair, b):
                    for e in range(2):
                        sp.dma_start(cb[b][e * F1:(e + 1) * F1, :],
                                     comb_dram[bass.ds(2 * pair + e, 1), :].rearrange("o t -> (o t)").partition_broadcast(F1))\
                          .then_inc(cb_loaded[b], 16)

                for b in range(2):
                    load_shared(b, b)
                    load_comb(b, b)
                for b in range(2):
                    sp.wait_ge(w_ready, b + 1)
                    load_routed(b, b)
                with sp.Fori(0, PAIRS // 2 - 1) as i:
                    for b in range(2):
                        sp.wait_ge(w_ready, 2 * i + b + 3)
                        load_routed(2 * i + b + 2, b)
                        sp.wait_ge(mixed, 2 * (2 * i + b) + 2)
                        load_comb(2 * i + b + 2, b)
                for b in range(2):
                    sp.wait_ge(w_ready, PAIRS + b + 1)
                    load_shared(2 + b, b)

            @block.tensor
            def _(pe):
                def gate_up(s, b, half):
                    hs = 2 * s + half
                    if half == 0:
                        pe.wait_ge(w_ready, s + 1)
                    if not (isinstance(s, int) and hs < 2):
                        pe.wait_ge(h_ready, hs - 1)
                    cols = slice(half * HALF, (half + 1) * HALF)
                    for j in range(2):
                        out = psum[:, 4 + 2 * half + j, :]
                        for c in range(DC):
                            wh, wl = w_h[b][:, DC * j + c, :], w_l[b][:, DC * j + c, :]
                            pe.matmul(out, wh, xT_h[:, c, cols], start=(c == 0), stop=False)
                            pe.matmul(out, wh, xT_l[:, c, cols], start=False, stop=False)
                            last = pe.matmul(out, wl, xT_h[:, c, cols], start=False, stop=(c == DC - 1))
                    last.then_inc(gu_ready, 1)

                def down(s, b, half, first=False, end=False):
                    hs = 2 * s + half
                    pe.wait_ge(hl_ready, hs + 1)
                    hh, hl = h_h[2 * b + half][:, :], h_l[2 * b + half][:, :]
                    for c in range(DC):
                        out = psum[:, 2 * c + half, :]
                        wh, wl = w_h[b][:, 2 * DC + c, :], w_l[b][:, 2 * DC + c, :]
                        pe.matmul(out, wh, hh, start=first, stop=False)
                        pe.matmul(out, wh, hl, start=False, stop=False)
                        last = pe.matmul(out, wl, hh, start=False, stop=end)
                    last.then_inc(down_done, 1)

                def step(s, b, routed):
                    first = isinstance(s, int) and s == 0
                    for half in range(2):
                        gate_up(s, b, half)
                        if not first:
                            down(s - 1, 1 - b, half, isinstance(s, int) and s == 1)
                steps(pe, step)
                for half in range(2):
                    down(STEPS - 1, (STEPS - 1) % 2, half, False, True)
                for n in range(NT):
                    pe.wait_ge(y_ready, n // 4 + 1)
                    if n >= 2:
                        pe.wait_ge(g_ready, n - 1)
                    for c in range(DC):
                        last = pe.transpose(psum[:, 4 + n % 2, c * P:(c + 1) * P], yT[:, c, n * P:(n + 1) * P], ident[:, :])
                    last.then_inc(t_ready, 1)

            @block.scalar
            def _(act):
                def split_high(s, b, loads):
                    act.wait_ge(w_loaded[b], LOADS * loads)
                    if not (isinstance(s, int) and s < 2):
                        act.wait_ge(down_done, 2 * s - 2)
                    act.activation(w_h[b][:, :, :], wf[b][:, :, :], ACT.Copy, scale=WSCALE).then_inc(wh_ready, 1)

                def silu(s, b, half, routed):
                    hs = 2 * s + half
                    act.wait_ge(gu_ready, hs + 1)
                    if not (isinstance(s, int) and hs < 2):
                        act.wait_ge(h_ready, hs - 1)
                    act.activation(sg[half][:, :], psum[:, 4 + 2 * half, :], ACT.Silu, scale=1.0 / WSCALE).then_inc(silu_ready, 1)

                def high(s, b, half):
                    hs = 2 * s + half
                    act.wait_ge(h_ready, hs + 1)
                    if not (isinstance(s, int) and s < 2):
                        act.wait_ge(down_done, hs - 3)
                    act.activation(h_h[2 * b + half][:, :], hf[half][:, :], ACT.Copy).then_inc(hh_ready, 1)

                split_high(0, 0, 1)
                split_high(1, 1, 1)
                for s in range(2):
                    for half in range(2):
                        silu(s, s, half, False)
                        high(s, s, half)
                    split_high(s + 2, s, 2)
                with act.Fori(0, PAIRS // 2) as i:
                    for b in range(2):
                        for half in range(2):
                            silu(2 * i + 2 + b, b, half, True)
                            high(2 * i + 2 + b, b, half)
                        split_high(2 * i + 4 + b, b, i + 3)
                for s in range(STEPS - 2, STEPS):
                    for half in range(2):
                        silu(s, s % 2, half, False)
                        high(s, s % 2, half)
                act.wait_ge(down_done, 2 * STEPS)
                for half in range(2):
                    for c in range(DC):
                        last = act.activation(yT[:, c, half * HALF:(half + 1) * HALF], psum[:, 2 * c + half, :], ACT.Copy,
                                              scale=1.0 / WSCALE)
                    last.then_inc(y_ready, 1)
                for n in range(NT):
                    act.wait_ge(t_ready, n + 1)
                    if n >= 2:
                        act.wait_ge(p_ready, n - 1)
                    act.activation(gate1[n % 2][:, :], psum[:, 4 + n % 2, 0:D], ACT.Silu).then_inc(g_ready, 1)

            @block.gpsimd
            def _(pool):
                with pool.Fori(0, PAIRS // 2) as i:
                    for b in range(2):
                        for half in range(2):
                            pool.wait_ge(silu_ready, 2 * (2 * i + b + 2) + half + 1)
                            if half == 0:
                                pool.wait_ge(cb_loaded[b], 32 * i + 32)
                            pool.tensor_tensor(sg[half][:, :], sg[half][:, :], cb[b][:, half * HALF:(half + 1) * HALF],
                                               ALU.mult).then_inc(mixed, 1)

            @block.vector
            def _(dve):
                def split_low(s, b):
                    dve.wait_ge(wh_ready, s + 1)
                    dve.scalar_tensor_tensor(w_l[b][:, :, :], wf[b][:, :, :], WSCALE, w_h[b][:, :, :],
                                             ALU.mult, ALU.subtract).then_inc(w_ready, 1)

                def hidden(s, b, half, routed):
                    hs = 2 * s + half
                    if routed:
                        dve.wait_ge(mixed, hs - 3)
                    else:
                        dve.wait_ge(silu_ready, hs + 1)
                    if not (isinstance(s, int) and s == 0):
                        dve.wait_ge(hl_ready, hs - 1)
                    dve.scalar_tensor_tensor(hf[half][:, :], psum[:, 5 + 2 * half, :], 1.0 / WSCALE, sg[half][:, :],
                                             ALU.mult, ALU.mult).then_inc(h_ready, 1)

                def low(s, b, half):
                    hs = 2 * s + half
                    dve.wait_ge(hh_ready, hs + 1)
                    dve.tensor_tensor(h_l[2 * b + half][:, :], hf[half][:, :], h_h[2 * b + half][:, :],
                                      ALU.subtract).then_inc(hl_ready, 1)

                split_low(0, 0)
                split_low(1, 1)

                def step(s, b, routed):
                    for half in range(2):
                        hidden(s, b, half, routed)
                        low(s, b, half)
                    if not isinstance(s, int) or s < STEPS - 2:
                        split_low(s + 2, b)
                steps(dve, step)
                for n in range(NT):
                    dve.wait_ge(g_ready, n + 1)
                    dve.tensor_tensor(prod[n % 2][:, :], gate1[n % 2][:, :], s1[:, n, :], ALU.mult).then_inc(p_ready, 1)
                    dve.wait_ge(p_ready, n + 1)
                    dve.tensor_tensor(x[:, n, :], x[:, n, :], prod[n % 2][:, :], ALU.add).then_inc(x_ready, 1)

    store_tokens(nc, env, "out", out, x)


def program(nc, w, out):
    with ExitStack() as ctx:
        def sb(name, shape, dt):
            return ctx.enter_context(nc.sbuf_tensor(name, shape, dt))

        in_use = []

        def sem(name):
            in_use.append(nc.alloc_semaphore(name=name))
            return in_use[-1]

        env = {"sem": sem, "sb": sb}
        env["psum"] = ctx.enter_context(nc.psum_tensor("psum", [P, 8, HALF], F32))
        env["x"] = x = sb("x", [P, NT, D], F32)
        env["x_loaded"] = x_loaded = env["sem"]("x_loaded")
        with nc.Block() as block:
            @block.sync
            def _(sp):
                sp.dma_start(x[:, :, :], w["L0_attn_x"][0].rearrange("(n p) d -> p n d", p=P)).then_inc(x_loaded, 16)
        constants(nc, env)
        with ExitStack() as layer0:
            def tmp(name, shape, dt):
                return layer0.enter_context(nc.sbuf_tensor(name, shape, dt))
            env["gate0"] = tmp("gate0", [P, NT, D], F32)
            env["xT_h"], env["xT_l"] = tmp("xT_h", [P, DC, T], F16), tmp("xT_l", [P, DC, T], F16)
            with ExitStack() as norm:
                env["xn"] = norm.enter_context(nc.sbuf_tensor("xn0", [P, NT, D], F32))
                env["xnT"] = xnT = norm.enter_context(nc.sbuf_tensor("xnT0", [P, DC, T], F32))
                layer_norm(nc, env, "ln0", x, env["xn"], xnT)
                split16(nc, env, "xT0", [(xnT[:, :, :], env["xT_h"][:, :, :], env["xT_l"][:, :, :])])
                mixture0(nc, env, w)
            env["oT_h"], env["oT_l"] = tmp("oT_h", [P, H, T], F16), tmp("oT_l", [P, H, T], F16)
            attention0(nc, env, w)
            project0(nc, env, w)
        nc.clear_and_free_semaphores(in_use)
        nc.all_engine_barrier()
        env["xn"], env["xnT"] = sb("xn1", [P, NT, D], F32), sb("xnT1", [P, DC, T], F32)
        env["s1"] = sb("s1", [P, NT, D], F32)
        layer_norm(nc, env, "ln1", x, env["xn"], env["xnT"])
        gated_linear_attention(nc, env, w)
        mixture1(nc, env, w, out)


_INS = ["L0_attn_x"] + ["L0_attn_" + k for k in ("wq", "wk", "wv", "wo", "q_scale", "k_scale")] \
    + ["L0_ffn_" + k for k in ("router_w", "e_bias", "W_gate", "W_up", "W_down", "shared_gate", "shared_up", "shared_down")] \
    + ["L1_attn_" + k for k in ("Wq", "Wk", "Wkg1", "Wkg2", "bkg2", "Wv", "Wg", "bg", "Wo", "ln1_w", "ln2_w", "W1", "W3", "W2")] \
    + ["L1_ffn_" + k for k in ("router_w", "router_bias", "wg", "wu", "wd", "swg", "swu", "swd")]


def kernel(**inputs):
    import concourse.bacc as bacc
    from concourse.bass_utils import run_bass_kernel_spmd

    nc = bacc.Bacc("TRN2", target_bir_lowering=False, num_devices=1)
    arrays, aps = {}, {}
    for name in _INS:
        a = np.ascontiguousarray(inputs[name])
        arrays["in_" + name] = a
        aps[name] = nc.dram_tensor("in_" + name, a.shape, mybir.dt.from_np(a.dtype), kind="ExternalInput").ap()
    out = nc.dram_tensor("out", [1, T, D], F32, kind="ExternalOutput").ap()
    program(nc, aps, out[0])
    r = run_bass_kernel_spmd(nc, [arrays], core_ids=[0])
    return r.results[0]["out"]
```

```python
import concourse.bass as bass
import numpy as np
from concourse import mybir
from contextlib import ExitStack

F32 = mybir.dt.float32
F16 = mybir.dt.float16
ALU = mybir.AluOpType
ACT = mybir.ActivationFunctionType
AX = mybir.AxisListType

P = 128
T = 1024
NT = T // P
D = 256
DC = D // P
HALF = 512
LN_EPS = 1e-5

H, HD = 16, 128
RMS_EPS0 = 1e-6
WSCALE = 64.0

E0, NG0, GE0, TKG0, K0, I0 = 32, 8, 4, 3, 4, 128
CAP = int(np.ceil(1.25 * T / E0))
SLOTS = E0 * CAP
ST = SLOTS // P
ROUTE_SCALE = 2.5
IS = 256

GH, GK, GV = 16, 8, 16
RMS_EPS1 = 1e-5
GATE_NORM = 16.0
HID = 704
E1, F1, K1 = 64, 64, 4
SH1 = 512

SENTINEL = -1.0e30
TAKEN = -3.0e38


class Chain:

    def __init__(self, engine, done):
        self.engine, self.done, self.count = engine, done, 0

    def __call__(self, instruction):
        self.count += 1
        instruction.then_inc(self.done, 1)
        self.engine.wait_ge(self.done, self.count)


def bcast(ap, axis, n):
    a = ap.unsqueeze(axis)
    shape = list(a.shape)
    shape[axis] = n
    return a.to_broadcast(shape)


def identities(nc, env):
    ident, ident16 = env["sb"]("ident", [P, P], F32), env["sb"]("ident16", [P, P], F16)
    env.update(ident=ident, ident16=ident16)
    done = env["sem"]("ident_done")
    with nc.Block() as block:
        @block.gpsimd
        def _(pool):
            chain = Chain(pool, done)
            for m in (ident, ident16):
                chain(pool.memset(m[:, :], 0.0))
                chain(pool.affine_select(out=m[:, :], in_=m[:, :], compare_op=ALU.not_equal, fill=1.0,
                                         base=0, pattern=[[-1, P]], channel_multiplier=1))


def band(pool, chain, out, first, pattern, channel_multiplier, width):
    chain(pool.memset(out, 1.0))
    chain(pool.affine_select(out=out, in_=out, compare_op=ALU.is_ge, fill=0.0, base=first, pattern=pattern,
                             channel_multiplier=channel_multiplier))
    chain(pool.affine_select(out=out, in_=out, compare_op=ALU.is_ge, fill=0.0, base=width - 1 - first,
                             pattern=[[-step, n] for step, n in pattern], channel_multiplier=-channel_multiplier))


def mixture_masks(nc, env, sb):
    ones16 = sb("ones16", [P, P], F16)
    upper16 = sb("upper16", [P, P], F16)
    steps = sb("steps", [P, CAP], F32)
    slot_expert = sb("slot_expert", [P, ST, E0], F32)
    env.update(ones16=ones16, upper16=upper16, steps=steps, slot_expert=slot_expert)
    done = env["sem"]("masks_done")
    with nc.Block() as block:
        @block.gpsimd
        def _(pool):
            chain = Chain(pool, done)
            chain(pool.memset(ones16[:, :], 1.0))
            chain(pool.affine_select(out=upper16[:, :], in_=ones16[:, :], compare_op=ALU.is_gt, fill=0.0,
                                     base=0, pattern=[[1, P]], channel_multiplier=-1))
            chain(pool.iota(steps[:, :], [[1, CAP]], base=1, channel_multiplier=0,
                            allow_small_or_imprecise_dtypes=True))
            band(pool, chain, slot_expert[:, :, :], 0, [[P, ST], [-CAP, E0]], 1, CAP)


def head_masks(nc, env, sb):
    spread = sb("spread", [P, GK, P], F16)
    gather_h = sb("gather_h", [P, GK, P], F32)
    env.update(spread=spread, gather_h=gather_h)
    done = env["sem"]("head_masks_done")
    with nc.Block() as block:
        @block.gpsimd
        def _(pool):
            chain = Chain(pool, done)
            band(pool, chain, spread[:, :, :], 0, [[GH * GK, GK], [1, P]], -GK, GK)
            band(pool, chain, gather_h[:, :, :], 0, [[GH * GK, GK], [-GK, P]], 1, GK)


def layer_norm(nc, env, tag, x, xn, xnT, interleaved=False):
    sem, ident, psum = env["sem"], env["ident"], env["psum"]
    with ExitStack() as local:
        stats = local.enter_context(nc.sbuf_tensor(tag + "_stats", [P, NT, 6], F32))
        mv = local.enter_context(nc.sbuf_tensor(tag + "_mv", [P, NT, 2], F32))
        var = local.enter_context(nc.sbuf_tensor(tag + "_var", [P, NT], F32))
        std = local.enter_context(nc.sbuf_tensor(tag + "_std", [P, NT], F32))
        inv = local.enter_context(nc.sbuf_tensor(tag + "_inv", [P, NT], F32))
        stats_done, mv_done, var_ready, std_ready = (sem(tag + s) for s in ("_st", "_mv", "_var", "_std"))
        inv_done, xn_ready, xT_ready, evac_done = (sem(tag + s) for s in ("_inv", "_xn", "_xT", "_ev"))
        with nc.Block() as block:
            @block.vector
            def _(dve):
                if "x_loaded" in env and tag == "ln0":
                    dve.wait_ge(env["x_loaded"], 16)
                for n in range(NT):
                    dve.bn_stats(stats[:, n, :], x[:, n, :]).then_inc(stats_done, 1)
                for n in range(NT):
                    dve.wait_ge(stats_done, n + 1)
                    dve.bn_aggr(mv[:, n, :], stats[:, n, :]).then_inc(mv_done, 1)
                dve.wait_ge(mv_done, NT)
                dve.tensor_scalar(var[:, :], mv[:, :, 1], LN_EPS, None, ALU.add).then_inc(var_ready, 1)
                dve.wait_ge(std_ready, 1)
                dve.reciprocal(inv[:, :], std[:, :]).then_inc(inv_done, 1)
                dve.wait_ge(inv_done, 1)
                for n in range(NT):
                    dve.tensor_scalar(xn[:, n, :], x[:, n, :], mv[:, n, 0:1], inv[:, n:n + 1],
                                      ALU.subtract, ALU.mult).then_inc(xn_ready, 1)

            @block.scalar
            def _(act):
                act.wait_ge(var_ready, 1)
                act.activation(std[:, :], var[:, :], ACT.Sqrt).then_inc(std_ready, 1)
                for n in range(NT):
                    act.wait_ge(xT_ready, n + 1)
                    act.activation(xnT[:, :, n * P:(n + 1) * P],
                                   psum[:, n % 2, 0:D].rearrange("p (c t) -> p c t", c=DC),
                                   ACT.Copy).then_inc(evac_done, 1)

            @block.tensor
            def _(pe):
                for n in range(NT):
                    pe.wait_ge(xn_ready, n + 1)
                    if n >= 2:
                        pe.wait_ge(evac_done, n - 1)
                    for c in range(DC):
                        channels = xn[:, n, c::DC] if interleaved else xn[:, n, c * P:(c + 1) * P]
                        last = pe.transpose(psum[:, n % 2, c * P:(c + 1) * P], channels, ident[:, :])
                    last.then_inc(xT_ready, 1)


def split16(nc, env, tag, pairs):
    done = env["sem"](tag + "_high")
    with nc.Block() as block:
        @block.vector
        def _(dve):
            for i, (x, high, low) in enumerate(pairs):
                dve.tensor_copy(high, x).then_inc(done, 1)
                dve.wait_ge(done, i + 1)
                dve.tensor_tensor(low, x, high, ALU.subtract)


def top_k_mask(dve, chain, scores, k, best, named, replaced, mask):
    m = scores.shape[2] - 8
    chain(dve.memset(named, SENTINEL))
    for n in range(NT):
        chain(dve.max(best[:, n, :], scores[:, n, 0:m]))
    chain(dve.tensor_copy(named[:, :, 0:k], best[:, :, 0:k]))
    for n in range(NT):
        chain(dve.match_replace(replaced[:, n, :], named[:, n, :], scores[:, n, :], TAKEN))
    chain(dve.tensor_scalar(mask, replaced[:, :, 0:m], TAKEN / 2, None, ALU.is_lt))


def route0(nc, env, router_w, e_bias):
    sem, psum, ident = env["sem"], env["psum"], env["ident"]
    xnT, ones16, upper16, steps = env["xnT"], env["ones16"], env["upper16"], env["steps"]
    member, wk_h, wk_l = env["member"], env["wk_h"], env["wk_l"]
    with ExitStack() as local:
        def tmp(name, shape, dt=F32):
            return local.enter_context(nc.sbuf_tensor("r0_" + name, shape, dt))
        rw, rwT, bias = tmp("rw", [E0, D]), tmp("rwT", [P, DC, E0]), tmp("bias", [P, E0])
        prob, sc = tmp("prob", [P, NT, E0]), tmp("sc", [P, NT, E0])
        hi2, lo2, sums = tmp("hi2", [P, NT * NG0, 2]), tmp("lo2", [P, NT * NG0, 2]), tmp("sums", [P, NT * NG0, 2])
        gs, gr, gm = tmp("gs", [P, NT, NG0 + 8]), tmp("gr", [P, NT, NG0 + 8]), tmp("gm", [P, NT, NG0])
        es, er, sel = tmp("es", [P, NT, E0 + 8]), tmp("er", [P, NT, E0 + 8]), tmp("sel", [P, NT, E0])
        best, named = tmp("best", [P, NT, 8]), tmp("named", [P, NT, 8])
        sel16 = tmp("sel16", [P, NT, E0], F16)
        w, wsum, winv = tmp("w", [P, NT, E0]), tmp("wsum", [P, NT]), tmp("winv", [P, NT])
        keep, place = tmp("keep", [P, NT, E0]), tmp("place", [P, NT, E0])
        loaded = [sem("r0_ld0"), sem("r0_ld1")]
        rwT_ready, rwT_done, logits_ready, prob_ready = (sem("r0_" + s) for s in ("rwT", "rwTd", "lg", "pr"))
        sel_ready, pos_ready, dve_done = (sem("r0_" + s) for s in ("sel", "pos", "dve"))
        logits = psum[:, 0, 0:NT * E0].rearrange("p (n e) -> p n e", n=NT)
        pos = psum[:, 1, 0:NT * E0].rearrange("p (n e) -> p n e", n=NT)
        turned = psum[:, 2, 0:DC * E0].rearrange("p (c e) -> p c e", c=DC)
        with nc.Block() as block:
            @block.sync
            def _(sp):
                sp.dma_start(rw[:, :], router_w).then_inc(loaded[0], 16)
                sp.dma_start(bias[:, :], e_bias.partition_broadcast(P)).then_inc(loaded[1], 16)

            @block.tensor
            def _(pe):
                pe.wait_ge(loaded[0], 16)
                for c in range(DC):
                    last = pe.transpose(turned[:, c, :], rw[:, c * P:(c + 1) * P], ident[0:E0, 0:E0])
                last.then_inc(rwT_ready, 1)
                pe.wait_ge(rwT_done, 1)
                for n in range(NT):
                    for c in range(DC):
                        last = pe.matmul(logits[:, n, :], xnT[:, c, n * P:(n + 1) * P], rwT[:, c, :],
                                         start=(c == 0), stop=(c == DC - 1))
                last.then_inc(logits_ready, 1)
                pe.wait_ge(sel_ready, 1)
                for n in range(NT):
                    for i in range(n):
                        pe.matmul(pos[:, n, :], ones16[:, :], sel16[:, i, :], start=(i == 0), stop=False)
                    last = pe.matmul(pos[:, n, :], upper16[:, :], sel16[:, n, :], start=(n == 0), stop=True)
                last.then_inc(pos_ready, 1)

            @block.scalar
            def _(act):
                act.wait_ge(rwT_ready, 1)
                act.activation(rwT[:, :, :], turned, ACT.Copy).then_inc(rwT_done, 1)
                act.wait_ge(logits_ready, 1)
                act.activation(prob[:, :, :], logits, ACT.Sigmoid).then_inc(prob_ready, 1)

            @block.vector
            def _(dve):
                chain = Chain(dve, dve_done)
                dve.wait_ge(prob_ready, 1)
                dve.wait_ge(loaded[1], 16)
                chain(dve.tensor_tensor(sc[:, :, :], prob[:, :, :], bcast(bias[:, :], 1, NT), ALU.add))
                pair = sc[:, :, :].rearrange("p n (g a b) -> p (n g) a b", a=2, b=2)
                chain(dve.tensor_tensor(hi2[:, :, :], pair[:, :, :, 0], pair[:, :, :, 1], ALU.max))
                chain(dve.tensor_tensor(lo2[:, :, :], pair[:, :, :, 0], pair[:, :, :, 1], ALU.min))
                chain(dve.tensor_tensor(sums[:, :, :], hi2[:, :, :], lo2[:, :, :], ALU.add))
                chain(dve.tensor_tensor(lo2[:, :, 0], hi2[:, :, 0], hi2[:, :, 1], ALU.add))
                chain(dve.tensor_tensor(lo2[:, :, 1], sums[:, :, 0], sums[:, :, 1], ALU.max))
                chain(dve.memset(gs[:, :, :], SENTINEL))
                chain(dve.tensor_tensor(gs[:, :, 0:NG0], lo2[:, :, 0].rearrange("p (n g) -> p n g", n=NT),
                                        lo2[:, :, 1].rearrange("p (n g) -> p n g", n=NT), ALU.max))
                top_k_mask(dve, chain, gs[:, :, :], TKG0, best[:, :, :], named[:, :, :], gr[:, :, :], gm[:, :, :])
                chain(dve.memset(es[:, :, :], SENTINEL))
                for a in range(GE0):
                    chain(dve.tensor_tensor(es[:, :, a:E0:GE0], sc[:, :, a:E0:GE0], gm[:, :, :], ALU.mult))
                chain(dve.tensor_scalar(es[:, :, 0:E0], es[:, :, 0:E0], 0.0, None, ALU.add))
                top_k_mask(dve, chain, es[:, :, :], K0, best[:, :, :], named[:, :, :], er[:, :, :], sel[:, :, :])
                dve.tensor_copy(sel16[:, :, :], sel[:, :, :]).then_inc(sel_ready, 1)
                chain(dve.tensor_tensor(w[:, :, :], prob[:, :, :], sel[:, :, :], ALU.mult))
                chain(dve.reduce_sum(wsum[:, :], w[:, :, :], AX.X))
                chain(dve.tensor_scalar(wsum[:, :], wsum[:, :], 1e-20, None, ALU.add))
                chain(dve.reciprocal(winv[:, :], wsum[:, :]))
                chain(dve.scalar_tensor_tensor(w[:, :, :], w[:, :, :], ROUTE_SCALE, bcast(winv[:, :], 2, E0),
                                               ALU.mult, ALU.mult))
                dve.wait_ge(pos_ready, 1)
                chain(dve.scalar_tensor_tensor(keep[:, :, :], pos, float(CAP), sel[:, :, :], ALU.is_lt, ALU.mult))
                chain(dve.scalar_tensor_tensor(place[:, :, :], pos, 1.0, keep[:, :, :], ALU.add, ALU.mult))
                chain(dve.tensor_tensor(w[:, :, :], w[:, :, :], keep[:, :, :], ALU.mult))
                chain(dve.tensor_copy(wk_h[:, :, :], w[:, :, :]))
                chain(dve.tensor_tensor(wk_l[:, :, :], w[:, :, :], wk_h[:, :, :], ALU.subtract))
                for n in range(NT):
                    chain(dve.tensor_tensor(member[:, n, :, :], bcast(place[:, n, :], 2, CAP),
                                            bcast(steps[:, :], 1, E0), ALU.is_equal))


def experts0(nc, env, w_gate, w_up, w_down):
    sem, psum = env["sem"], env["psum"]
    xn_h, xn_l, member, wk_h, wk_l = (env[k] for k in ("xn_h", "xn_l", "member", "wk_h", "wk_l"))
    slot_expert, yT = env["slot_expert"], env["yT"]
    w_slot = env["w_slot"]
    cuts = [(0, 512), (512, 512), (1024, 256)]
    with ExitStack() as local:
        def tmp(name, shape, dt=F32):
            return local.enter_context(nc.sbuf_tensor("e0_" + name, shape, dt))
        xgT = tmp("xgT", [P, DC, SLOTS])
        wmask = tmp("wmask", [P, ST, E0])
        gathered, xg_done, ws_ready, wm_done = (sem("e0_" + s) for s in ("ga", "xg", "ws", "wm"))
        ws = psum[:, 7, 0:ST * E0].rearrange("p (s e) -> p s e", s=ST)
        with nc.Block() as block:
            @block.tensor
            def _(pe):
                for c in range(DC):
                    for k, (at, size) in enumerate(cuts):
                        bank = c * len(cuts) + k
                        for n in range(NT):
                            slots = member[:, n, :, :].rearrange("p e c -> p (e c)")[:, at:at + size]
                            pe.matmul(psum[:, bank, 0:size], xn_h[:, n, c * P:(c + 1) * P], slots,
                                      start=(n == 0), stop=False)
                            last = pe.matmul(psum[:, bank, 0:size], xn_l[:, n, c * P:(c + 1) * P], slots,
                                             start=False, stop=(n == NT - 1))
                        last.then_inc(gathered, 1)
                for s in range(ST):
                    for n in range(NT):
                        slots = member[:, n, :, :].rearrange("p e c -> p (e c)")[:, s * P:(s + 1) * P]
                        pe.matmul(ws[:, s, :], slots, wk_h[:, n, :], start=(n == 0), stop=False)
                        last = pe.matmul(ws[:, s, :], slots, wk_l[:, n, :], start=False, stop=(n == NT - 1))
                last.then_inc(ws_ready, 1)

            @block.scalar
            def _(act):
                for c in range(DC):
                    for k, (at, size) in enumerate(cuts):
                        bank = c * len(cuts) + k
                        act.wait_ge(gathered, bank + 1)
                        act.activation(xgT[:, c, at:at + size], psum[:, bank, 0:size], ACT.Copy).then_inc(xg_done, 1)

            @block.vector
            def _(dve):
                dve.wait_ge(ws_ready, 1)
                dve.tensor_tensor(wmask[:, :, :], ws, slot_expert[:, :, :], ALU.mult).then_inc(wm_done, 1)
                dve.wait_ge(wm_done, 1)
                dve.reduce_sum(w_slot[:, :], wmask[:, :, :], AX.X).then_inc(wm_done, 1)

        wgu = [tmp(f"wgu{b}", [P, DC, 2, I0]) for b in range(2)]
        wd = [tmp(f"wd{b}", [P, D]) for b in range(2)]
        sg = [tmp(f"sg{b}", [P, CAP]) for b in range(2)]
        hT = [tmp(f"hT{b}", [P, CAP]) for b in range(2)]
        gate_loaded = [sem(f"e0_lg{b}") for b in range(2)]
        up_loaded = [sem(f"e0_lu{b}") for b in range(2)]
        down_loaded = [sem(f"e0_ld{b}") for b in range(2)]
        gu_ready, silu_done, h_ready, y_ready, y_done = (sem("e0_" + s) for s in ("gu", "si", "h", "y", "yd"))
        with nc.Block() as block:
            @block.sync
            def _(sp):
                def load(e, b):
                    for j, (src, got) in enumerate(((w_gate, gate_loaded), (w_up, up_loaded))):
                        sp.dma_start(wgu[b][:, :, j, :],
                                     src[bass.ds(e, 1), :, :].rearrange("o (c p) i -> p (o c) i", p=P)).then_inc(got[b], 16)
                    sp.dma_start(wd[b][:, :], src2(e)).then_inc(down_loaded[b], 16)

                def src2(e):
                    return w_down[bass.ds(e, 1), :, :].rearrange("o i d -> (o i) d")
                for b in range(2):
                    load(b, b)
                with sp.Fori(0, E0 // 2 - 1) as i:
                    for b in range(2):
                        sp.wait_ge(y_ready, 2 * i + b + 1)
                        load(2 * i + b + 2, b)

            @block.tensor
            def _(pe):
                with pe.Fori(0, E0 // 2) as i:
                    for b in range(2):
                        e = 2 * i + b
                        pe.wait_ge(gate_loaded[b], 16 * i + 16)
                        pe.wait_ge(up_loaded[b], 16 * i + 16)
                        for j in range(2):
                            for c in range(DC):
                                last = pe.matmul(psum[:, b, j * CAP:(j + 1) * CAP], wgu[b][:, c, j, :],
                                                 xgT[:, c, bass.ds(e * CAP, CAP)], start=(c == 0), stop=(c == DC - 1))
                        last.then_inc(gu_ready, 1)
                    for b in range(2):
                        e = 2 * i + b
                        pe.wait_ge(down_loaded[b], 16 * i + 16)
                        pe.wait_ge(h_ready, e + 1)
                        for c in range(DC):
                            last = pe.matmul(psum[:, 2 + b, c * CAP:(c + 1) * CAP], wd[b][:, c * P:(c + 1) * P],
                                             hT[b][:, :], start=True, stop=True)
                        last.then_inc(y_ready, 1)

            @block.scalar
            def _(act):
                with act.Fori(0, E0 // 2) as i:
                    for b in range(2):
                        act.wait_ge(gu_ready, 2 * i + b + 1)
                        act.activation(sg[b][:, :], psum[:, b, 0:CAP], ACT.Silu).then_inc(silu_done, 1)

            @block.vector
            def _(dve):
                with dve.Fori(0, E0 // 2) as i:
                    for b in range(2):
                        dve.wait_ge(silu_done, 2 * i + b + 1)
                        dve.tensor_tensor(hT[b][:, :], psum[:, b, CAP:2 * CAP], sg[b][:, :], ALU.mult).then_inc(h_ready, 1)
                    for b in range(2):
                        dve.wait_ge(y_ready, 2 * i + b + 1)
                        dve.tensor_copy(yT[:, :, bass.ds((2 * i + b) * CAP, CAP)],
                                        psum[:, 2 + b, 0:DC * CAP].rearrange("p (c s) -> p c s", c=DC)).then_inc(y_done, 1)


def combine0(nc, env, shared_gate, shared_up, shared_down):
    sem, psum, ident = env["sem"], env["psum"], env["ident"]
    member, yT, w_slot, xnT, gate0 = (env[k] for k in ("member", "yT", "w_slot", "xnT", "gate0"))
    ident16 = env["ident16"]
    IC = IS // P
    with ExitStack() as local:
        def tmp(name, shape, dt=F32):
            return local.enter_context(nc.sbuf_tensor("c0_" + name, shape, dt))
        w3 = [tmp(f"w{i}", [P, 2, D]) for i in range(3)]
        w3T = [tmp(f"wT{i}", [P, 2, D]) for i in range(3)]
        sg = tmp("sg", [P, 2, HALF])
        hT = tmp("hT", [P, IC, T])
        loaded = [sem(f"c0_ld{i}") for i in range(3)]
        wT_ready, wT_done, gu_ready, silu_done, h_ready = (sem("c0_" + s) for s in ("wT", "wTd", "gu", "si", "h"))
        with nc.Block() as block:
            @block.sync
            def _(sp):
                for i, src in enumerate((shared_gate, shared_up, shared_down)):
                    sp.dma_start(w3[i][:, :, :], src.rearrange("(a p) d -> p a d", p=P)).then_inc(loaded[i], 16)

            @block.tensor
            def _(pe):
                for i in range(3):
                    pe.wait_ge(loaded[i], 16)
                    for a in range(2):
                        for c in range(2):
                            last = pe.transpose(psum[:, i, (c * 2 + a) * P:(c * 2 + a + 1) * P],
                                                w3[i][:, a, c * P:(c + 1) * P], ident[:, :])
                    last.then_inc(wT_ready, 1)
                pe.wait_ge(wT_done, 3)
                for step in range(2 * IC):
                    t, ic = step // IC, step % IC
                    bank = 4 + 2 * (step % 2)
                    if step >= 2:
                        pe.wait_ge(h_ready, step - 1)
                    for j in range(2):
                        for c in range(DC):
                            last = pe.matmul(psum[:, bank + j, :], w3T[j][:, c, ic * P:(ic + 1) * P],
                                             xnT[:, c, t * HALF:(t + 1) * HALF], start=(c == 0), stop=(c == DC - 1))
                    last.then_inc(gu_ready, 1)

            @block.scalar
            def _(act):
                for i in range(3):
                    act.wait_ge(wT_ready, i + 1)
                    act.activation(w3T[i][:, :, :], psum[:, i, :].rearrange("p (c x) -> p c x", c=2),
                                   ACT.Copy).then_inc(wT_done, 1)
                for step in range(2 * IC):
                    act.wait_ge(gu_ready, step + 1)
                    if step >= 2:
                        act.wait_ge(h_ready, step - 1)
                    act.activation(sg[:, step % 2, :], psum[:, 4 + 2 * (step % 2), :], ACT.Silu).then_inc(silu_done, 1)

            @block.vector
            def _(dve):
                for step in range(2 * IC):
                    t, ic = step // IC, step % IC
                    dve.wait_ge(silu_done, step + 1)
                    dve.tensor_tensor(hT[:, ic, t * HALF:(t + 1) * HALF], psum[:, 5 + 2 * (step % 2), :],
                                      sg[:, step % 2, :], ALU.mult).then_inc(h_ready, 1)

        yw_h, yw_l = tmp("yw_h", [P, ST, D], F16), tmp("yw_l", [P, ST, D], F16)
        turned = [tmp(f"turned{b}", [P, ST, P], F16) for b in range(2)]
        y_ready, yh_done, yl_done, m_ready, m_done, o_ready, o_done = (
            sem("c1_" + s) for s in ("y", "yh", "yl", "m", "md", "o", "od"))
        mcuts = [(0, 8), (8, ST - 8)]
        with nc.Block() as block:
            @block.tensor
            def _(pe):
                for s in range(ST):
                    if s >= 2:
                        pe.wait_ge(yl_done, s - 1)
                    for c in range(DC):
                        last = pe.transpose(psum[:, s % 2, c * P:(c + 1) * P], yT[:, c, s * P:(s + 1) * P], ident[:, :])
                    last.then_inc(y_ready, 1)
                for n in range(NT):
                    slots = member[:, n, :, :].rearrange("p e c -> p (e c)")
                    for k, (at, size) in enumerate(mcuts):
                        step = 2 * n + k
                        if step >= 2:
                            pe.wait_ge(m_done, step - 1)
                        for s in range(at, at + size):
                            out = psum[:, 2 + k, :].bitcast(F16)[:, (s - at) * P:(s - at + 1) * P]
                            last = pe.transpose(out, slots[:, s * P:(s + 1) * P], ident16[:, :])
                        last.then_inc(m_ready, 1)
                    pe.wait_ge(m_done, 2 * n + 2)
                    if n == 0:
                        pe.wait_ge(yl_done, ST)
                    if n >= 2:
                        pe.wait_ge(o_done, n - 1)
                    out = psum[:, 4 + n % 2, 0:D]
                    for s in range(ST):
                        pe.matmul(out, turned[n % 2][:, s, :], yw_h[:, s, :], start=(s == 0), stop=False)
                        pe.matmul(out, turned[n % 2][:, s, :], yw_l[:, s, :], start=False, stop=False)
                    for ic in range(IC):
                        last = pe.matmul(out, hT[:, ic, n * P:(n + 1) * P], w3T[2][:, ic, :],
                                         start=False, stop=(ic == IC - 1))
                    last.then_inc(o_ready, 1)

            @block.scalar
            def _(act):
                for n in range(NT):
                    for k, (at, size) in enumerate(mcuts):
                        act.wait_ge(m_ready, 2 * n + k + 1)
                        if n >= 2:
                            act.wait_ge(o_ready, n - 1)
                        act.copy(turned[n % 2][:, at:at + size, :].rearrange("p s x -> p (s x)").bitcast(F32),
                                 psum[:, 2 + k, 0:size * P // 2]).then_inc(m_done, 1)
                for n in range(NT):
                    act.wait_ge(o_done, n + 1)
                    act.activation(gate0[:, n, :], gate0[:, n, :], ACT.Silu)

            @block.vector
            def _(dve):
                for s in range(ST):
                    dve.wait_ge(y_ready, s + 1)
                    dve.tensor_scalar(yw_h[:, s, :], psum[:, s % 2, 0:D], w_slot[:, s:s + 1], None,
                                      ALU.mult).then_inc(yh_done, 1)
                    dve.wait_ge(yh_done, s + 1)
                    dve.scalar_tensor_tensor(yw_l[:, s, :], psum[:, s % 2, 0:D], w_slot[:, s:s + 1], yw_h[:, s, :],
                                             ALU.mult, ALU.subtract).then_inc(yl_done, 1)
                for n in range(NT):
                    dve.wait_ge(o_ready, n + 1)
                    dve.tensor_copy(gate0[:, n, :], psum[:, 4 + n % 2, 0:D]).then_inc(o_done, 1)


def mixture0(nc, env, w):
    with ExitStack() as local:
        def tmp(name, shape, dt=F32):
            return local.enter_context(nc.sbuf_tensor(name, shape, dt))
        mixture_masks(nc, env, tmp)
        env["member"] = tmp("member", [P, NT, E0, CAP], F16)
        env["wk_h"], env["wk_l"] = tmp("wk_h", [P, NT, E0], F16), tmp("wk_l", [P, NT, E0], F16)
        env["yT"] = tmp("yT", [P, DC, SLOTS])
        env["w_slot"] = tmp("w_slot", [P, ST])
        xn_h, xn_l = tmp("xn_h", [P, NT, D], F16), tmp("xn_l", [P, NT, D], F16)
        env["xn_h"], env["xn_l"] = xn_h, xn_l
        split16(nc, env, "xn0tok", [(env["xn"][:, :, :], xn_h[:, :, :], xn_l[:, :, :])])
        route0(nc, env, w["L0_ffn_router_w"], w["L0_ffn_e_bias"])
        experts0(nc, env, w["L0_ffn_W_gate"], w["L0_ffn_W_up"], w["L0_ffn_W_down"])
        combine0(nc, env, w["L0_ffn_shared_gate"], w["L0_ffn_shared_up"], w["L0_ffn_shared_down"])


def store_tokens(nc, env, tag, out, tile):
    stored = env["sem"](tag + "_stored")
    with nc.Block() as block:
        @block.sync
        def _(sp):
            sp.dma_start(out.rearrange("(n p) d -> p n d", p=P), tile[:, :, :]).then_inc(stored, 16)
            sp.wait_ge(stored, 16)


def attention0(nc, env, w):
    sem, psum, ident, ident16 = env["sem"], env["psum"], env["ident"], env["ident16"]
    xT_h, xT_l, oT_h, oT_l = (env[k] for k in ("xT_h", "xT_l", "oT_h", "oT_l"))
    wq, wk, wv = (w["L0_attn_" + k].rearrange("(c p) h d -> p c h d", p=P) for k in ("wq", "wk", "wv"))
    SIDE = [("qk", 0), ("qk", 1), ("qk", 2), ("qk", 3), ("turn", 0), ("turn", 1), ("v", 0), ("turn", 2),
            ("turn", 3), ("v", 1)]
    PLAN = {0: ([0], [1]), 1: ([2], [3]), 2: ([], []), 3: ([], []), 4: ([4, 5], [6]), 5: ([7, 8], [9]),
            6: ([], []), 7: ([], [])}
    VALUES = {2: [(1, 0), (1, 1)], 3: [(1, 2), (1, 3)], 6: [(0, 0), (0, 1)], 7: [(0, 2), (0, 3)]}
    NORM_SLOT = 2
    NS = len(SIDE)
    QK_LAST = SIDE.index(("qk", 3))
    TURN_LAST = SIDE.index(("turn", 3))
    V_LAST = SIDE.index(("v", 1))
    TURN_1 = SIDE.index(("turn", 1))
    QT = NT
    KT = NT
    PROB = 4096.0
    S_BANK, T_BANK, O_BANK, SIDE_BANKS = 0, 4, 6, (7, 6)
    with ExitStack() as local:
        def tmp(name, shape, dt=F32):
            return local.enter_context(nc.sbuf_tensor("a0_" + name, shape, dt))
        wf = [tmp(f"wf{b}", [P, DC, 3, HD]) for b in range(2)]
        w_h = [tmp(f"wh{b}", [P, DC, 3, HD], F16) for b in range(2)]
        w_l = [tmp(f"wl{b}", [P, DC, 3, HD], F16) for b in range(2)]
        qk = tmp("qk", [P, NT, 2, HD])
        sq = tmp("sq", [P, NT, 2, HD])
        qkT_f = tmp("qkTf", [P, 2, T])
        v_f = tmp("vf", [P, NT, HD])
        ss, power, rnorm = tmp("ss", [P, NT * 2]), tmp("power", [P, NT * 2]), tmp("rnorm", [P, NT * 2])
        qkT_h = [tmp(f"qkTh{b}", [P, 2, T], F16) for b in range(2)]
        qkT_l = [tmp(f"qkTl{b}", [P, 2, T], F16) for b in range(2)]
        v_h = [tmp(f"vh{b}", [P, NT, HD], F16) for b in range(2)]
        v_l = [tmp(f"vl{b}", [P, NT, HD], F16) for b in range(2)]
        lifts = tmp("lifts", [P, 3])
        scales = tmp("scales", [P, 2])
        qk_scale = tmp("qk_scale", [P, 2])
        nmax, total, tsc, rtot = (tmp(n, [P, 2]) for n in ("nmax", "total", "tsc", "rtot"))
        ex = [tmp(f"ex{b}", [P, T]) for b in range(2)]
        pr = [tmp(f"pr{b}", [P, 2, T], F16) for b in range(2)]
        pT = [tmp(f"pT{b}", [P, 2, KT, HALF], F16) for b in range(2)]

        w_loaded = [sem(f"a0_wld{b}") for b in range(2)]
        scale_loaded = [sem(f"a0_sld{b}") for b in range(2)]
        (scale_ready, w_scaled, w_high, w_ready, side_ready, qkT_ready, side_free, sq_ready, ss_ready,
         var_ready, v_ready, part_high, pow_ready, r_ready, qkn_ready, s_ready, max_ready, exp_ready, tsc_ready, rt_ready, ph_ready,
         p_ready, t_ready, pT_ready, pv_ready, o_high, o_free) = (sem("a0_" + s) for s in (
             "sc", "ws", "wh", "wr", "sr", "kt", "sf", "sq", "ss", "vr", "vv", "hi", "pw", "rr", "qn", "s", "mx", "ex",
             "ts", "rt", "ph", "p", "t", "pT", "pv", "oh", "of"))

        def heads(engine, head):
            head(0, 0, True, False)
            with engine.Fori(0, (H - 2) // 2) as i:
                for b in range(2):
                    head(2 * i + 1 + b, (1 + b) % 2, False, False)
            head(H - 1, (H - 1) % 2, False, True)

        def sides(m, part, job, t):
            for s in PLAN[m][part]:
                job(t, s)

        with nc.Block() as block:
            @block.sync
            def _(sp):
                for i, name in enumerate(("L0_attn_q_scale", "L0_attn_k_scale")):
                    sp.dma_start(scales[:, i:i + 1], w[name].rearrange("(p a) -> p a", a=1)).then_inc(scale_loaded[i], 16)

                def load(h, b):
                    for j, src in enumerate((wq, wk, wv)):
                        sp.dma_start(wf[b][:, :, j, :], src[:, :, bass.ds(h, 1), :].rearrange("p c o d -> p c (o d)"))\
                          .then_inc(w_loaded[b], 16)
                load(0, 0)
                load(1, 1)
                with sp.Fori(0, (H - 2) // 2) as i:
                    for b in range(2):
                        sp.wait_ge(w_ready, 2 * i + b + 1)
                        load(2 * i + b + 2, b)

            @block.gpsimd
            def _(pool):
                pool.memset(power[:, :], -0.5).then_inc(pow_ready, 1)
                pool.memset(lifts[:, 0:1], WSCALE).then_inc(pow_ready, 1)
                pool.memset(lifts[:, 1:2], 1.0 / WSCALE).then_inc(pow_ready, 1)
                pool.memset(lifts[:, 2:3], 1.0).then_inc(pow_ready, 1)
                pool.wait_ge(scale_loaded[0], 16)
                pool.wait_ge(scale_loaded[1], 16)
                pool.tensor_tensor(qk_scale[:, 0:1], scales[:, 0:1], scales[:, 1:2], ALU.mult).then_inc(scale_ready, 1)
                pool.memset(qk_scale[:, 1:2], 1.0).then_inc(scale_ready, 1)
                pool.wait_ge(pow_ready, 4)

                def split_weights(t, b, loads):
                    pool.wait_ge(w_loaded[b], 48 * loads)
                    if not isinstance(t, int) or t >= 2:
                        pool.wait_ge(side_ready, NS * (t - 2) + V_LAST + 1)
                    lift = lifts[:, 0:1].to_broadcast([P, DC * 3 * HD])
                    flat, high = (x.rearrange("p c j d -> p (c j d)") for x in (wf[b][:, :, :, :], w_h[b][:, :, :, :]))
                    pool.tensor_tensor(high, flat, lift, ALU.mult).then_inc(w_high, 1)
                    pool.wait_ge(w_high, t + 1)
                    pool.tensor_tensor(flat, flat, lift, ALU.mult).then_inc(w_scaled, 1)
                    pool.wait_ge(w_scaled, t + 1)
                    pool.tensor_tensor(w_l[b][:, :, :, :], wf[b][:, :, :, :], w_h[b][:, :, :, :],
                                       ALU.subtract).then_inc(w_ready, 1)

                def normalise(t):
                    pool.wait_ge(side_free, NS * t + QK_LAST + 1)
                    pool.wait_ge(var_ready, t + 1)
                    pool.tensor_tensor(rnorm[:, :], ss[:, :], power[:, :], ALU.pow).then_inc(r_ready, 1)
                    pool.wait_ge(r_ready, 2 * t + 1)
                    pool.tensor_tensor(rnorm[:, :], rnorm[:, :], lifts[:, 1:2].to_broadcast([P, NT * 2]),
                                       ALU.mult).then_inc(r_ready, 1)
                    pool.wait_ge(r_ready, 2 * t + 2)
                    flat = qk[:, :, :, :].rearrange("p n j d -> p (n j) d")
                    pool.tensor_tensor(flat, flat, bcast(rnorm[:, :], 2, HD), ALU.mult).then_inc(qkn_ready, 1)

                def split_parts(t, b):
                    later = not isinstance(t, int) or t >= 2
                    kinds = [(i, kind, g) for i, (kind, g) in enumerate(SIDE) if kind != "qk"]
                    for k, (i, kind, g) in enumerate(kinds):
                        pool.wait_ge(side_free, NS * t + i + 1)
                        if kind == "turn":
                            if g == 0 and later:
                                pool.wait_ge(s_ready, QT * (t - 1))
                            at = (slice(None), g // 2, slice((g % 2) * HALF, (g % 2 + 1) * HALF))
                            whole, high, low = qkT_f[at], qkT_h[b][at], qkT_l[b][at]
                        else:
                            if g == 0 and later:
                                pool.wait_ge(pv_ready, 2 * t - 2)
                            whole, high, low = (x[:, 4 * g:4 * g + 4, :].rearrange("p n d -> p (n d)")
                                                for x in (v_f, v_h[b], v_l[b]))
                        pool.tensor_tensor(high, whole, lifts[:, 2:3].to_broadcast([P, HALF]), ALU.mult).then_inc(part_high, 1)
                        pool.wait_ge(part_high, len(kinds) * t + k + 1)
                        pool.tensor_tensor(low, whole, high, ALU.subtract).then_inc(qkT_ready if kind == "turn" else v_ready, 1)

                split_weights(0, 0, 1)
                normalise(0)
                split_parts(0, 0)
                split_weights(1, 1, 1)
                with pool.Fori(0, (H - 2) // 2) as i:
                    for b in range(2):
                        normalise(2 * i + b + 1)
                        split_parts(2 * i + b + 1, (b + 1) % 2)
                        split_weights(2 * i + b + 2, b, i + 2)
                normalise(H - 1)
                split_parts(H - 1, (H - 1) % 2)

            @block.tensor
            def _(pe):
                def side(t, s, b):
                    kind, g = SIDE[s]
                    later = not isinstance(t, int)
                    if later or t > 0 or s >= 2:
                        pe.wait_ge(side_free, NS * t + s - 1)
                    if s in (1, TURN_1) and (later or t >= 2):
                        pe.wait_ge(o_free, 2 * t - (3 if s == 1 else 2))
                    out = psum[:, SIDE_BANKS[s % 2], :]
                    if kind == "turn":
                        if g == 0:
                            pe.wait_ge(qkn_ready, t + 1)
                        for k in range(4):
                            last = pe.transpose(out[:, k * P:(k + 1) * P], qk[:, 4 * (g % 2) + k, g // 2, :], ident[:, :])
                    else:
                        if s == 0:
                            pe.wait_ge(w_ready, t + 1)
                        tiles, j0, j1 = (2, 0, 2) if kind == "qk" else (4, 2, 3)
                        cols = (j1 - j0) * HD
                        for k in range(tiles):
                            n = g * tiles + k
                            dst = out[:, k * cols:(k + 1) * cols]
                            for c in range(DC):
                                xh, xl = (x[:, c, n * P:(n + 1) * P] for x in (xT_h, xT_l))
                                wh, wl = (x[b][:, c, j0:j1, :].rearrange("p j d -> p (j d)") for x in (w_h, w_l))
                                pe.matmul(dst, xh, wh, start=(c == 0), stop=False)
                                pe.matmul(dst, xh, wl, start=False, stop=False)
                                last = pe.matmul(dst, xl, wh, start=False, stop=(c == DC - 1))
                    last.then_inc(side_ready, 1)

                def scores(t, m, b):
                    if m == 0:
                        pe.wait_ge(qkT_ready, 4 * t + 4)
                    if not (isinstance(t, int) and t == 0 and m < 2):
                        pe.wait_ge(exp_ready, QT * t + m - 1)
                    qh, ql = (x[b][:, 0, m * P:(m + 1) * P] for x in (qkT_h, qkT_l))
                    bank = S_BANK + 2 * (m % 2)
                    kh, kl = ([x[b][:, 1, f * HALF:(f + 1) * HALF] for f in range(2)] for x in (qkT_h, qkT_l))
                    for f in range(2):
                        pe.matmul(psum[:, bank + f, :], qh, kh[f], start=True, stop=False)
                    for f in range(2):
                        pe.matmul(psum[:, bank + f, :], qh, kl[f], start=False, stop=False)
                    for f in range(2):
                        last = pe.matmul(psum[:, bank + f, :], ql, kh[f], start=False, stop=True)
                    last.then_inc(s_ready, 1)

                def turn(t, m):
                    pe.wait_ge(p_ready, QT * t + m + 1)
                    if not (isinstance(t, int) and t == 0 and m == 0):
                        pe.wait_ge(pT_ready, QT * t + m)
                    for part in range(2):
                        for k in range(KT):
                            out = psum[:, T_BANK + part, :].bitcast(F16)[:, k * P:(k + 1) * P]
                            last = pe.transpose(out, pr[m % 2][:, part, k * P:(k + 1) * P], ident16[:, :])
                    last.then_inc(t_ready, 1)

                def values(t, g, piece, b, end):
                    if piece == 0:
                        pe.wait_ge(pT_ready, QT * t + 4 * g + 4)
                        pe.wait_ge(v_ready, 2 * t + 2)
                        if not end:
                            pe.wait_ge(side_free, NS * (t + 2) + QK_LAST + 1 if g else NS * (t + 1) + NS)
                        if not (isinstance(t, int) and t == 0 and g == 0):
                            pe.wait_ge(o_free, 2 * t + g)
                    out = psum[:, O_BANK, :]
                    for k in (2 * piece, 2 * piece + 1):
                        ph, pl = (pT[g][:, part, k, :] for part in range(2))
                        pe.matmul(out, v_h[b][:, k, :], ph, start=(k == 0), stop=False)
                        pe.matmul(out, v_h[b][:, k, :], pl, start=False, stop=False)
                        last = pe.matmul(out, v_l[b][:, k, :], ph, start=False, stop=(k == KT - 1))
                    if piece == 3:
                        last.then_inc(pv_ready, 1)

                def head(t, b, first, end):
                    nb = 1 - b
                    for m in range(QT):
                        if not end:
                            sides(m, 0, lambda u, s: side(u, s, nb), t + 1)
                        if m > 0:
                            turn(t, m - 1)
                        elif not first:
                            turn(t - 1, QT - 1)
                        if m < QT - 2:
                            scores(t, m + 2, b)
                        elif not end:
                            scores(t + 1, m + 2 - QT, nb)
                        if not end:
                            sides(m, 1, lambda u, s: side(u, s, nb), t + 1)
                        for g, piece in VALUES.get(m, []):
                            if g == 0:
                                values(t, g, piece, b, end)
                            elif not first:
                                values(t - 1, g, piece, nb, end)

                for s in range(NS):
                    side(0, s, 0)
                scores(0, 0, 0)
                scores(0, 1, 0)
                heads(pe, head)
                turn(H - 1, QT - 1)
                for piece in range(4):
                    values(H - 1, 1, piece, (H - 1) % 2, True)

            @block.scalar
            def _(act):
                def side(t, s, b):
                    kind, g = SIDE[s]
                    act.wait_ge(side_ready, NS * t + s + 1)
                    bank = psum[:, SIDE_BANKS[s % 2], :]
                    later = not isinstance(t, int)
                    if kind == "qk":
                        if s == 0 and (later or t > 0):
                            act.wait_ge(side_ready, NS * (t - 1) + TURN_LAST + 1)
                            act.wait_ge(ss_ready, t)
                        two = slice(2 * g, 2 * g + 2)
                        act.activation(sq[:, two, :, :].rearrange("p n j d -> p (n j d)"), bank, ACT.Square).then_inc(sq_ready, 1)
                        act.activation(qk[:, two, :, :].rearrange("p n j d -> p (n j d)"), bank,
                                       ACT.Copy).then_inc(side_free, 1)
                    elif kind == "turn":
                        j, at = g // 2, (g % 2) * HALF
                        if g == 0 and (later or t > 0):
                            act.wait_ge(qkT_ready, 4 * t)
                        act.activation(qkT_f[:, j, at:at + HALF], bank, ACT.Copy,
                                       scale=qk_scale[:, j:j + 1]).then_inc(side_free, 1)
                    else:
                        if g == 0 and (later or t > 0):
                            act.wait_ge(v_ready, 2 * t)
                        act.activation(v_f[:, 4 * g:4 * g + 4, :].rearrange("p n d -> p (n d)"), bank, ACT.Copy,
                                       scale=1.0 / WSCALE).then_inc(side_free, 1)

                def exps(t, m):
                    act.wait_ge(max_ready, QT * t + m + 1)
                    if not (isinstance(t, int) and t == 0 and m < 2):
                        act.wait_ge(p_ready, QT * t + m - 1)
                    bank = S_BANK + 2 * (m % 2)
                    act.activation(ex[m % 2][:, :], psum[:, bank:bank + 2, :].rearrange("p a b -> p (a b)"), ACT.Exp,
                                   bias=nmax[:, m % 2:m % 2 + 1], accum_out=total[:, m % 2:m % 2 + 1]).then_inc(exp_ready, 1)

                def turned(t, m):
                    act.wait_ge(t_ready, QT * t + m + 1)
                    if m % 4 == 0 and (not isinstance(t, int) or t > 0):
                        act.wait_ge(pv_ready, 2 * (t - 1) + m // 4 + 1)
                    dst = pT[m // 4][:, :, :, (m % 4) * P:(m % 4 + 1) * P].bitcast(F32)
                    src = psum[:, T_BANK:T_BANK + 2, :].rearrange("p a (k q) -> p a k q", k=KT)
                    act.copy(dst, src).then_inc(pT_ready, 1)

                def outputs(t, g):
                    act.wait_ge(pv_ready, 2 * t + g + 1)
                    act.activation(oT_h[:, bass.ds(t, 1), g * HALF:(g + 1) * HALF],
                                   psum[:, O_BANK:O_BANK + 1, :], ACT.Copy, scale=1.0 / PROB).then_inc(o_high, 1)

                def head(t, b, first, end):
                    nb = 1 - b
                    for m in range(QT):
                        if not end:
                            sides(m, 0, lambda u, s: side(u, s, nb), t + 1)
                        if m > 0:
                            turned(t, m - 1)
                        elif not first:
                            turned(t - 1, QT - 1)
                        if m < QT - 1:
                            exps(t, m + 1)
                        elif not end:
                            exps(t + 1, 0)
                        if not end:
                            sides(m, 1, lambda u, s: side(u, s, nb), t + 1)
                        if not first and m == 3:
                            outputs(t - 1, 1)
                        if m == 7:
                            outputs(t, 0)

                act.wait_ge(scale_ready, 2)
                for s in range(NS):
                    side(0, s, 0)
                exps(0, 0)
                heads(act, head)
                turned(H - 1, QT - 1)
                outputs(H - 1, 1)

            @block.vector
            def _(dve):
                def squares(t):
                    dve.wait_ge(sq_ready, 4 * t + 4)
                    dve.reduce_sum(ss[:, :], sq[:, :, :, :].rearrange("p n j d -> p (n j) d"), AX.X).then_inc(ss_ready, 1)
                    dve.wait_ge(ss_ready, t + 1)
                    dve.tensor_scalar(ss[:, :], ss[:, :], 1.0 / (HD * WSCALE * WSCALE), RMS_EPS0, ALU.mult,
                                      ALU.add).then_inc(var_ready, 1)

                def maxima(t, m):
                    dve.wait_ge(s_ready, QT * t + m + 1)
                    if not (isinstance(t, int) and t == 0 and m < 2):
                        dve.wait_ge(exp_ready, QT * t + m - 1)
                    bank = S_BANK + 2 * (m % 2)
                    dve.tensor_reduce(nmax[:, m % 2:m % 2 + 1], psum[:, bank:bank + 2, :].rearrange("p a b -> p (a b)"),
                                      AX.X, ALU.max, negate=True).then_inc(max_ready, 1)

                def split(t, m):
                    k = m % 2
                    dve.wait_ge(exp_ready, QT * t + m + 1)
                    dve.tensor_scalar(tsc[:, k:k + 1], total[:, k:k + 1], 1.0 / PROB, None, ALU.mult).then_inc(tsc_ready, 1)
                    dve.wait_ge(tsc_ready, QT * t + m + 1)
                    dve.reciprocal(rtot[:, k:k + 1], tsc[:, k:k + 1]).then_inc(rt_ready, 1)
                    dve.wait_ge(rt_ready, QT * t + m + 1)
                    if not (isinstance(t, int) and t == 0 and m < 2):
                        dve.wait_ge(t_ready, QT * t + m - 1)
                    dve.tensor_scalar(pr[k][:, 0, :], ex[k][:, :], rtot[:, k:k + 1], None, ALU.mult).then_inc(ph_ready, 1)
                    dve.wait_ge(ph_ready, QT * t + m + 1)
                    dve.scalar_tensor_tensor(pr[k][:, 1, :], ex[k][:, :], rtot[:, k:k + 1], pr[k][:, 0, :],
                                             ALU.mult, ALU.subtract).then_inc(p_ready, 1)

                def outputs(t, g):
                    dve.wait_ge(o_high, 2 * t + g + 1)
                    at = (slice(None), bass.ds(t, 1), slice(g * HALF, (g + 1) * HALF))
                    dve.scalar_tensor_tensor(oT_l[at], psum[:, O_BANK:O_BANK + 1, :], 1.0 / PROB, oT_h[at],
                                             ALU.mult, ALU.subtract).then_inc(o_free, 1)

                def head(t, b, first, end):
                    nb = 1 - b
                    for m in range(QT):
                        if not first and m in (0, 4):
                            outputs(t - 1, m // 4)
                        if not end and m == NORM_SLOT:
                            squares(t + 1)
                        if m < QT - 1:
                            maxima(t, m + 1)
                        elif not end:
                            maxima(t + 1, 0)
                        split(t, m)

                squares(0)
                maxima(0, 0)
                heads(dve, head)
                outputs(H - 1, 0)
                outputs(H - 1, 1)


def project0(nc, env, w):
    sem, psum = env["sem"], env["psum"]
    oT_h, oT_l, x, gate0 = (env[k] for k in ("oT_h", "oT_l", "x", "gate0"))
    with ExitStack() as local:
        def tmp(name, shape, dt=F32):
            return local.enter_context(nc.sbuf_tensor("p0_" + name, shape, dt))
        HQ = 4
        wf = [tmp(f"wf{b}", [P, HQ, D]) for b in range(2)]
        wo_h, wo_l = tmp("wo_h", [P, H, D], F16), tmp("wo_l", [P, H, D], F16)
        sg = [tmp(f"sg{b}", [P, D]) for b in range(2)]
        loaded = [sem(f"p0_ld{b}") for b in range(2)]
        wh_ready, w_ready, y_ready, sg_ready, x_ready = (sem("p0_" + s) for s in ("wh", "w", "y", "sg", "x"))
        wo = w["L0_attn_wo"].rearrange("h d e -> d h e")
        with nc.Block() as block:
            @block.sync
            def _(sp):
                for q in range(H // HQ):
                    if q >= 2:
                        sp.wait_ge(w_ready, q - 1)
                    sp.dma_start(wf[q % 2][:, :, :], wo[:, q * HQ:(q + 1) * HQ, :]).then_inc(loaded[q % 2], 16)

            @block.scalar
            def _(act):
                for q in range(H // HQ):
                    act.wait_ge(loaded[q % 2], 16 * (q // 2 + 1))
                    act.activation(wo_h[:, q * HQ:(q + 1) * HQ, :], wf[q % 2][:, :, :], ACT.Copy,
                                   scale=WSCALE).then_inc(wh_ready, 1)

            @block.vector
            def _(dve):
                for q in range(H // HQ):
                    dve.wait_ge(wh_ready, q + 1)
                    part = (slice(None), slice(q * HQ, (q + 1) * HQ))
                    dve.scalar_tensor_tensor(wo_l[part], wf[q % 2][:, :, :], WSCALE, wo_h[part],
                                             ALU.mult, ALU.subtract).then_inc(w_ready, 1)
                for n in range(NT):
                    dve.wait_ge(y_ready, n + 1)
                    if n >= 2:
                        dve.wait_ge(x_ready, n - 1)
                    dve.scalar_tensor_tensor(sg[n % 2][:, :], psum[:, n, 0:D], 1.0 / WSCALE, gate0[:, n, :],
                                             ALU.mult, ALU.mult).then_inc(sg_ready, 1)
                    dve.wait_ge(sg_ready, n + 1)
                    dve.tensor_tensor(x[:, n, :], x[:, n, :], sg[n % 2][:, :], ALU.add).then_inc(x_ready, 1)

            @block.tensor
            def _(pe):
                for q in range(H // HQ):
                    pe.wait_ge(w_ready, q + 1)
                    for n in range(NT):
                        for h in range(q * HQ, (q + 1) * HQ):
                            oh, ol = (o[:, h, n * P:(n + 1) * P] for o in (oT_h, oT_l))
                            pe.matmul(psum[:, n, 0:D], oh, wo_h[:, h, :], start=(h == 0), stop=False)
                            pe.matmul(psum[:, n, 0:D], oh, wo_l[:, h, :], start=False, stop=False)
                            last = pe.matmul(psum[:, n, 0:D], ol, wo_h[:, h, :], start=False, stop=(h == H - 1))
                        if q == H // HQ - 1:
                            last.then_inc(y_ready, 1)


def gated_linear_attention(nc, env, w):
    sem, psum, ident = env["sem"], env["psum"], env["ident"]
    xn, s1 = env["xn"], env["s1"]
    KD = GH * GK
    G1 = 16
    FT = -(-HID // P)
    with ExitStack() as outer:
        def keep(name, shape, dt=F32):
            return outer.enter_context(nc.sbuf_tensor("g1_" + name, shape, dt))
        head_masks(nc, env, keep)
        spread, gather_h = env["spread"], env["gather_h"]
        ln = keep("ln", [P, 2, DC])
        ms, inv, sq = keep("ms", [P, NT]), keep("inv", [P, NT]), keep("sq", [P, D])
        silu_g = keep("silu_g", [P, NT, D])
        o = keep("o", [P, NT, D])
        ln_loaded = [sem(f"g1_lnl{i}") for i in range(2)]

        def rms_turned(tag, source, which, xT):
            ss_done, ms_done, rt_done, inv_done, xr_ready, t_ready, evac = (
                sem(tag + s) for s in ("ss", "ms", "rt", "iv", "xr", "t", "e"))
            with ExitStack() as inner:
                xr = inner.enter_context(nc.sbuf_tensor(tag + "_xr", [P, NT, D], F32))
                with nc.Block() as block:
                    @block.vector
                    def _(dve):
                        dve.wait_ge(ss_done, NT)
                        dve.tensor_scalar(ms[:, :], ms[:, :], 1.0 / D, RMS_EPS1, ALU.mult, ALU.add).then_inc(ms_done, 1)
                        dve.wait_ge(rt_done, 1)
                        dve.reciprocal(inv[:, :], inv[:, :]).then_inc(inv_done, 1)
                        dve.wait_ge(inv_done, 1)
                        for n in range(NT):
                            dve.tensor_scalar(xr[:, n, :], source[:, n, :], inv[:, n:n + 1], None, ALU.mult).then_inc(xr_ready, 1)

                    @block.scalar
                    def _(act):
                        for n in range(NT):
                            if n:
                                act.wait_ge(ss_done, n)
                            act.activation(sq[:, :], source[:, n, :], ACT.Square, accum_out=ms[:, n:n + 1]).then_inc(ss_done, 1)
                        act.wait_ge(ms_done, 1)
                        act.activation(inv[:, :], ms[:, :], ACT.Sqrt).then_inc(rt_done, 1)
                        act.wait_ge(ln_loaded[which], 16)
                        for n in range(NT):
                            act.wait_ge(t_ready, n + 1)
                            for c in range(DC):
                                last = act.activation(xT[:, c, n * P:(n + 1) * P], psum[:, n % 2, c * P:(c + 1) * P],
                                                      ACT.Copy, scale=ln[:, which, c:c + 1])
                            last.then_inc(evac, 1)

                    @block.tensor
                    def _(pe):
                        for n in range(NT):
                            pe.wait_ge(xr_ready, n + 1)
                            if n >= 2:
                                pe.wait_ge(evac, n - 1)
                            for c in range(DC):
                                last = pe.transpose(psum[:, n % 2, c * P:(c + 1) * P], xr[:, n, c * P:(c + 1) * P], ident[:, :])
                            last.then_inc(t_ready, 1)

        with ExitStack() as local:
            def tmp(name, shape, dt=F32):
                return local.enter_context(nc.sbuf_tensor("g1_" + name, shape, dt))
            xT = tmp("xT", [P, DC, T])
            wq, wk = tmp("wq", [P, DC, KD]), tmp("wk", [P, DC, KD])
            wg1, wg2, bg2 = tmp("wg1", [P, DC, G1]), tmp("wg2", [G1, KD]), tmp("bg2", [P, 1])
            wv, wg, bg = tmp("wv", [P, DC, D]), tmp("wg", [P, DC, D]), tmp("bg", [P, D])
            wv_dh = tmp("wv_dh", [P, DC, D])
            wv_ready = sem("g1_wv")
            loads = [(wq, w["L1_attn_Wq"]), (wk, w["L1_attn_Wk"]), (wg1, w["L1_attn_Wkg1"]), (wv, w["L1_attn_Wv"]),
                     (wg, w["L1_attn_Wg"])]
            w_loaded = [sem(f"g1_wl{i}") for i in range(len(loads) + 3)]
            with nc.Block() as block:
                @block.sync
                def _(sp):
                    for i, name in enumerate(("L1_attn_ln1_w", "L1_attn_ln2_w")):
                        sp.dma_start(ln[:, i, :], w[name].rearrange("(c p) -> p c", p=P), allow_slow_non_contiguous=True).then_inc(ln_loaded[i], 16)
                    for i, (dst, src) in enumerate(loads):
                        sp.dma_start(dst[:, :, :], src.rearrange("(c p) n -> p c n", p=P)).then_inc(w_loaded[i], 16)
                    sp.dma_start(wg2[:, :], w["L1_attn_Wkg2"]).then_inc(w_loaded[5], 16)
                    sp.dma_start(bg2[:, :], w["L1_attn_bkg2"].rearrange("(p a) -> p a", a=1)).then_inc(w_loaded[6], 16)
                    sp.dma_start(bg[:, :], w["L1_attn_bg"].partition_broadcast(P)).then_inc(w_loaded[7], 16)
            rms_turned("g1_r1", xn, 0, xT)

            qT, kT = tmp("qT", [P, T]), tmp("kT", [P, T])
            mid = tmp("mid", [G1, T])
            z, e, dec = tmp("z", [P, T]), tmp("e", [P, T]), tmp("dec", [P, T])
            v_h, v_l = tmp("v_h", [P, 2, T], F16), tmp("v_l", [P, 2, T], F16)
            q_ready, mid_ready, mid_done, z_ready, v_ready, g_ready = (sem("g1_" + s) for s in ("q", "m", "md", "z", "v", "g"))
            qk_done, act_done, dve_done, vh_done, g_added, g_free, v_free = (sem("g1_" + s) for s in ("qd", "ad", "dd", "vh", "ga", "gf", "vf"))

            def both(pe, banks, lhs, rhs_of, rows=P):
                for half in range(2):
                    for c in range(DC):
                        last = pe.matmul(psum[0:rows, banks + half, :], lhs(c), rhs_of(c, half),
                                         start=(c == 0), stop=(c == DC - 1))
                return last

            with nc.Block() as block:
                @block.tensor
                def _(pe):
                    for i in range(len(loads) + 1):
                        pe.wait_ge(w_loaded[i], 16)

                    def x_of(c, half):
                        return xT[:, c, half * HALF:(half + 1) * HALF]
                    both(pe, 0, lambda c: wg1[:, c, :], x_of, G1).then_inc(mid_ready, 1)
                    both(pe, 2, lambda c: wq[:, c, :], x_of).then_inc(q_ready, 1)
                    both(pe, 4, lambda c: wk[:, c, :], x_of).then_inc(q_ready, 1)
                    pe.wait_ge(mid_done, 1)
                    for half in range(2):
                        last = pe.matmul(psum[:, 6 + half, :], wg2[:, :], mid[:, half * HALF:(half + 1) * HALF],
                                         start=True, stop=True)
                    last.then_inc(z_ready, 1)
                    pe.wait_ge(qk_done, 1)
                    pe.wait_ge(wv_ready, DC)
                    for cv in range(2):
                        both(pe, 2 * cv, lambda c: wv_dh[:, c, cv * P:(cv + 1) * P], x_of).then_inc(v_ready, 1)
                    for n in range(NT):
                        if n == 0:
                            pe.wait_ge(qk_done, 2)
                        if n >= 2:
                            pe.wait_ge(g_added, n - 1)
                        for c in range(DC):
                            last = pe.matmul(psum[:, 4 + n % 2, 0:D], xT[:, c, n * P:(n + 1) * P], wg[:, c, :],
                                             start=(c == 0), stop=(c == DC - 1))
                        last.then_inc(g_ready, 1)

                @block.gpsimd
                def _(pool):
                    pool.wait_ge(w_loaded[3], 16)
                    for c in range(DC):
                        pool.tensor_copy(wv_dh[:, c, :].rearrange("p (c d h) -> p c d h", c=2, d=8),
                                         wv[:, c, :].rearrange("p (h c d) -> p c d h", c=2, d=8)).then_inc(wv_ready, 1)

                def two(bank):
                    return psum[:, bank:bank + 2, :].rearrange("p a b -> p (a b)")

                @block.scalar
                def _(act):
                    chain = Chain(act, act_done)
                    act.wait_ge(mid_ready, 1)
                    act.activation(mid[:, :], psum[0:G1, 0:2, :].rearrange("p a b -> p (a b)"), ACT.Copy).then_inc(mid_done, 1)
                    act.wait_ge(q_ready, 1)
                    act.activation(qT[:, :], two(2), ACT.Copy).then_inc(qk_done, 1)
                    act.wait_ge(q_ready, 2)
                    act.activation(kT[:, :], two(4), ACT.Copy, scale=float(GV) ** -0.5).then_inc(qk_done, 1)
                    act.wait_ge(z_ready, 1)
                    act.wait_ge(w_loaded[6], 16)
                    chain(act.activation(z[:, :], two(6), ACT.Identity, bias=bg2[:, 0:1]))
                    chain(act.activation(e[:, :], z[:, :], ACT.Abs))
                    chain(act.activation(e[:, :], e[:, :], ACT.Exp, scale=-1.0))
                    chain(act.activation(e[:, :], e[:, :], ACT.Ln, bias=1.0))
                    act.wait_ge(dve_done, 1)
                    chain(act.activation(dec[:, :], z[:, :], ACT.Exp, scale=1.0 / GATE_NORM))
                    for cv in range(2):
                        act.wait_ge(v_ready, cv + 1)
                        act.activation(v_h[:, cv, :], two(2 * cv), ACT.Copy).then_inc(vh_done, 1)
                    act.wait_ge(g_added, NT)
                    act.activation(silu_g[:, :, :], silu_g[:, :, :], ACT.Silu).then_inc(g_free, 1)

                @block.vector
                def _(dve):
                    dve.wait_ge(act_done, 4)
                    dve.scalar_tensor_tensor(z[:, :], z[:, :], 0.0, e[:, :], ALU.min, ALU.subtract).then_inc(dve_done, 1)
                    for cv in range(2):
                        dve.wait_ge(vh_done, cv + 1)
                        dve.tensor_tensor(v_l[:, cv, :], two(2 * cv), v_h[:, cv, :], ALU.subtract).then_inc(v_free, 1)
                    dve.wait_ge(w_loaded[7], 16)
                    for n in range(NT):
                        dve.wait_ge(g_ready, n + 1)
                        dve.tensor_tensor(silu_g[:, n, :], psum[:, 4 + n % 2, 0:D], bg[:, :], ALU.add).then_inc(g_added, 1)

            kv = [tmp(f"kv{b}", [P, T]) for b in range(2)]
            state = [tmp(f"state{b}", [P, T]) for b in range(2)]
            qs = [tmp(f"qs{b}", [P, T]) for b in range(2)]
            v_spread, kv_ready, st_ready, qs_ready, o_step = (sem("g2_" + s) for s in ("v", "kv", "st", "qs", "o"))
            oT = tmp("oT", [P, 2, T])
            oT_done = sem("g2_oT")
            STEPS = 2 * GK
            with nc.Block() as block:
                @block.tensor
                def _(pe):
                    def spread_values(s):
                        cv, dd = s // 8, s % 8
                        if s >= 2:
                            pe.wait_ge(kv_ready, s - 1)
                        for half in range(2):
                            cols = slice(half * HALF, (half + 1) * HALF)
                            pe.matmul(psum[:, 2 * (s % 2) + half, :], spread[:, dd, :], v_h[:, cv, cols], start=True, stop=False)
                            last = pe.matmul(psum[:, 2 * (s % 2) + half, :], spread[:, dd, :], v_l[:, cv, cols],
                                             start=False, stop=True)
                        last.then_inc(v_spread, 1)

                    spread_values(0)
                    for s in range(STEPS):
                        if s + 1 < STEPS:
                            spread_values(s + 1)
                        cv, dd = s // 8, s % 8
                        pe.wait_ge(qs_ready, s + 1)
                        for half in range(2):
                            last = pe.matmul(psum[:, 4 + 2 * cv + half, :], gather_h[:, dd, :],
                                             qs[s % 2][:, half * HALF:(half + 1) * HALF], start=(dd == 0), stop=(dd == 7))
                        last.then_inc(o_step, 1)

                @block.vector
                def _(dve):
                    for s in range(STEPS):
                        dve.wait_ge(v_spread, s + 1)
                        if s >= 2:
                            dve.wait_ge(st_ready, s - 1)
                        dve.tensor_tensor(kv[s % 2][:, :], kT[:, :], psum[:, 2 * (s % 2):2 * (s % 2) + 2, :].rearrange("p a b -> p (a b)"),
                                          ALU.mult).then_inc(kv_ready, 1)
                        dve.wait_ge(kv_ready, s + 1)
                        if s >= 2:
                            dve.wait_ge(qs_ready, s - 1)
                        dve.tensor_tensor_scan(state[s % 2][:, :], dec[:, :], kv[s % 2][:, :], 0.0, ALU.mult,
                                               ALU.add).then_inc(st_ready, 1)

                @block.gpsimd
                def _(pool):
                    for s in range(STEPS):
                        pool.wait_ge(st_ready, s + 1)
                        if s >= 2:
                            pool.wait_ge(o_step, s - 1)
                        pool.tensor_tensor(qs[s % 2][:, :], qT[:, :], state[s % 2][:, :], ALU.mult).then_inc(qs_ready, 1)

                @block.scalar
                def _(act):
                    for cv in range(2):
                        act.wait_ge(o_step, 8 * (cv + 1))
                        act.activation(oT[:, cv, :], psum[:, 4 + 2 * cv:6 + 2 * cv, :].rearrange("p a b -> p (a b)"),
                                       ACT.Copy).then_inc(oT_done, 1)

            t_ready, o_done = sem("g3_t"), sem("g3_o")
            with nc.Block() as block:
                @block.tensor
                def _(pe):
                    for n in range(NT):
                        if n >= 2:
                            pe.wait_ge(o_done, n - 1)
                        for cv in range(2):
                            last = pe.transpose(psum[:, n % 2, cv * P:(cv + 1) * P], oT[:, cv, n * P:(n + 1) * P], ident[:, :])
                        last.then_inc(t_ready, 1)

                @block.scalar
                def _(act):
                    for n in range(NT):
                        act.wait_ge(t_ready, n + 1)
                        act.activation(o[:, n, :].rearrange("p (h c d) -> p c d h", c=2, d=8),
                                       psum[:, n % 2, 0:D].rearrange("p (c d h) -> p c d h", c=2, d=8), ACT.Copy).then_inc(o_done, 1)

        with ExitStack() as local:
            def tmp(name, shape, dt=F32):
                return local.enter_context(nc.sbuf_tensor("g4_" + name, shape, dt))
            mean, var, std = (tmp(n, [P, NT * GH]) for n in ("mean", "var", "std"))
            big = tmp("big", [P, NT * GH, GV])
            wo = tmp("wo", [P, DC, D])
            ogT = tmp("ogT", [P, DC, T])
            wo_loaded, dve_done, sq_done, rt_done, og_ready, t_ready, evac, y_ready, s_done = (
                sem("g4_" + s) for s in ("wl", "d", "sq", "rt", "og", "t", "e", "y", "s"))
            oh = o[:, :, :].rearrange("p n (h d) -> p (n h) d", h=GH)
            with nc.Block() as block:
                @block.sync
                def _(sp):
                    sp.dma_start(wo[:, :, :], w["L1_attn_Wo"].rearrange("(c p) n -> p c n", p=P)).then_inc(wo_loaded, 16)

                @block.vector
                def _(dve):
                    chain = Chain(dve, dve_done)
                    chain(dve.reduce_sum(mean[:, :], oh, AX.X))
                    chain(dve.tensor_scalar(mean[:, :], mean[:, :], 1.0 / GV, None, ALU.mult))
                    chain(dve.tensor_tensor(oh, oh, bcast(mean[:, :], 2, GV), ALU.subtract))
                    dve.wait_ge(sq_done, 1)
                    chain(dve.reduce_sum(var[:, :], big[:, :, :], AX.X))
                    chain(dve.tensor_scalar(var[:, :], var[:, :], 1.0 / GV, RMS_EPS1, ALU.mult, ALU.add))
                    dve.wait_ge(rt_done, 1)
                    chain(dve.reciprocal(std[:, :], std[:, :]))
                    chain(dve.tensor_tensor(oh, oh, bcast(std[:, :], 2, GV), ALU.mult))
                    dve.tensor_tensor(o[:, :, :], o[:, :, :], silu_g[:, :, :], ALU.mult).then_inc(og_ready, 1)
                    for n in range(NT):
                        dve.wait_ge(y_ready, n + 1)
                        dve.tensor_tensor(s1[:, n, :], psum[:, 2 + n % 2, 0:D], xn[:, n, :], ALU.add).then_inc(s_done, 1)

                @block.scalar
                def _(act):
                    act.wait_ge(dve_done, 3)
                    act.activation(big[:, :, :], oh, ACT.Square).then_inc(sq_done, 1)
                    act.wait_ge(dve_done, 5)
                    act.activation(std[:, :], var[:, :], ACT.Sqrt).then_inc(rt_done, 1)
                    for n in range(NT):
                        act.wait_ge(t_ready, n + 1)
                        act.activation(ogT[:, :, n * P:(n + 1) * P], psum[:, n % 2, 0:D].rearrange("p (c t) -> p c t", c=DC),
                                       ACT.Copy).then_inc(evac, 1)

                @block.tensor
                def _(pe):
                    pe.wait_ge(og_ready, 1)
                    pe.wait_ge(wo_loaded, 16)
                    for n in range(NT):
                        if n >= 2:
                            pe.wait_ge(evac, n - 1)
                        for c in range(DC):
                            last = pe.transpose(psum[:, n % 2, c * P:(c + 1) * P], o[:, n, c * P:(c + 1) * P], ident[:, :])
                        last.then_inc(t_ready, 1)
                    for n in range(NT):
                        pe.wait_ge(evac, n + 1)
                        if n >= 2:
                            pe.wait_ge(s_done, n - 1)
                        for c in range(DC):
                            last = pe.matmul(psum[:, 2 + n % 2, 0:D], ogT[:, c, n * P:(n + 1) * P], wo[:, c, :],
                                             start=(c == 0), stop=(c == DC - 1))
                        last.then_inc(y_ready, 1)

        with ExitStack() as local:
            def tmp(name, shape, dt=F32):
                return local.enter_context(nc.sbuf_tensor("m1_" + name, shape, dt))
            xT = tmp("xT", [P, DC, T])
            rms_turned("g1_r2", s1, 1, xT)
            w1, w3, w2 = tmp("w1", [P, DC, HID]), tmp("w3", [P, DC, HID]), tmp("w2", [P, FT, D])
            sg = tmp("sg", [P, 2, HALF])
            hT = tmp("hT", [P, FT, T])
            REST = HID - (FT - 1) * P
            loaded = [sem(f"m1_l{i}") for i in range(4)]
            gu_ready, silu_done, h_ready, y_ready, y_done = (sem("m1_" + s) for s in ("gu", "si", "h", "y", "yd"))
            with nc.Block() as block:
                @block.sync
                def _(sp):
                    sp.dma_start(w1[:, :, :], w["L1_attn_W1"].rearrange("(c p) n -> p c n", p=P)).then_inc(loaded[0], 16)
                    sp.dma_start(w3[:, :, :], w["L1_attn_W3"].rearrange("(c p) n -> p c n", p=P)).then_inc(loaded[1], 16)
                    sp.dma_start(w2[:, 0:FT - 1, :], w["L1_attn_W2"][0:(FT - 1) * P, :].rearrange("(f p) n -> p f n", p=P)).then_inc(loaded[2], 16)
                    sp.dma_start(w2[0:REST, FT - 1, :], w["L1_attn_W2"][(FT - 1) * P:HID, :]).then_inc(loaded[3], 16)

                steps = [(f, half) for f in range(FT) for half in range(2)]

                @block.tensor
                def _(pe):
                    pe.wait_ge(loaded[0], 16)
                    pe.wait_ge(loaded[1], 16)
                    for s, (f, half) in enumerate(steps):
                        rows = min(P, HID - f * P)
                        if s >= 2:
                            pe.wait_ge(h_ready, s - 1)
                        for j, wt in enumerate((w1, w3)):
                            for c in range(DC):
                                last = pe.matmul(psum[0:rows, 2 * (s % 2) + j, :], wt[:, c, f * P:f * P + rows],
                                                 xT[:, c, half * HALF:(half + 1) * HALF], start=(c == 0), stop=(c == DC - 1))
                        last.then_inc(gu_ready, 1)
                    pe.wait_ge(h_ready, len(steps))
                    pe.wait_ge(loaded[2], 16)
                    pe.wait_ge(loaded[3], 16)
                    for n in range(NT):
                        if n >= 4:
                            pe.wait_ge(y_done, n - 3)
                        for f in range(FT):
                            rows = min(P, HID - f * P)
                            last = pe.matmul(psum[:, 4 + n % 4, 0:D], hT[0:rows, f, n * P:(n + 1) * P], w2[0:rows, f, :],
                                             start=(f == 0), stop=(f == FT - 1))
                        last.then_inc(y_ready, 1)

                @block.scalar
                def _(act):
                    for s, (f, half) in enumerate(steps):
                        rows = min(P, HID - f * P)
                        act.wait_ge(gu_ready, s + 1)
                        if s >= 2:
                            act.wait_ge(h_ready, s - 1)
                        act.activation(sg[0:rows, s % 2, :], psum[0:rows, 2 * (s % 2), :], ACT.Silu).then_inc(silu_done, 1)

                @block.vector
                def _(dve):
                    for s, (f, half) in enumerate(steps):
                        rows = min(P, HID - f * P)
                        dve.wait_ge(silu_done, s + 1)
                        dve.tensor_tensor(hT[0:rows, f, half * HALF:(half + 1) * HALF], psum[0:rows, 2 * (s % 2) + 1, :],
                                          sg[0:rows, s % 2, :], ALU.mult).then_inc(h_ready, 1)
                    for n in range(NT):
                        dve.wait_ge(y_ready, n + 1)
                        dve.tensor_tensor(s1[:, n, :], s1[:, n, :], psum[:, 4 + n % 4, 0:D], ALU.add).then_inc(y_done, 1)


def route1(nc, env, router_w, router_bias, comb_dram):
    sem, psum, ident, xnT = env["sem"], env["psum"], env["ident"], env["xnT"]
    with ExitStack() as local:
        def tmp(name, shape, dt=F32):
            return local.enter_context(nc.sbuf_tensor("r1_" + name, shape, dt))
        rw, bias = tmp("rw", [P, DC, E1]), tmp("bias", [P, E1])
        es, er, sel = tmp("es", [P, NT, E1 + 8]), tmp("er", [P, NT, E1 + 8]), tmp("sel", [P, NT, E1])
        best, named = tmp("best", [P, NT, 8]), tmp("named", [P, NT, 8])
        shifted, prob, comb = tmp("shifted", [P, NT, E1]), tmp("prob", [P, NT, E1]), tmp("comb", [P, NT, E1])
        top, total = tmp("top", [P, NT]), tmp("total", [P, NT])
        combT = tmp("combT", [E1, T])
        loaded = [sem(f"r1_ld{i}") for i in range(2)]
        logits_ready, dve_done, exp_ready, comb_ready, t_ready, ct_ready, stored = (
            sem("r1_" + s) for s in ("lg", "d", "ex", "cb", "t", "ct", "st"))
        logits = psum[:, 0, :].rearrange("p (n e) -> p n e", n=NT)
        with nc.Block() as block:
            @block.sync
            def _(sp):
                sp.dma_start(rw[:, :, :], router_w.rearrange("(p c) e -> p c e", p=P)).then_inc(loaded[0], 16)
                sp.dma_start(bias[:, :], router_bias.partition_broadcast(P)).then_inc(loaded[1], 16)
                sp.wait_ge(ct_ready, 1)
                sp.dma_start(comb_dram, combT[:, :]).then_inc(stored, 16)
                sp.wait_ge(stored, 16)

            @block.tensor
            def _(pe):
                pe.wait_ge(loaded[0], 16)
                for n in range(NT):
                    for c in range(DC):
                        last = pe.matmul(logits[:, n, :], xnT[:, c, n * P:(n + 1) * P], rw[:, c, :],
                                         start=(c == 0), stop=(c == DC - 1))
                last.then_inc(logits_ready, 1)
                pe.wait_ge(comb_ready, 1)
                for n in range(NT):
                    last = pe.transpose(psum[0:E1, 2 + n // 4, (n % 4) * P:(n % 4 + 1) * P], comb[:, n, :], ident[:, :])
                last.then_inc(t_ready, 1)

            @block.scalar
            def _(act):
                act.wait_ge(dve_done, 2)
                act.activation(prob[:, :, :], shifted[:, :, :], ACT.Exp).then_inc(exp_ready, 1)
                act.wait_ge(t_ready, 1)
                act.activation(combT[:, :], psum[0:E1, 2:4, :].rearrange("p a b -> p (a b)"), ACT.Copy).then_inc(ct_ready, 1)

            @block.vector
            def _(dve):
                chain = Chain(dve, dve_done)
                dve.wait_ge(logits_ready, 1)
                dve.wait_ge(loaded[1], 16)
                chain(dve.reduce_max(top[:, :], logits, AX.X))
                chain(dve.tensor_tensor(shifted[:, :, :], logits, bcast(top[:, :], 2, E1), ALU.subtract))
                chain(dve.memset(es[:, :, :], SENTINEL))
                chain(dve.tensor_tensor(es[:, :, 0:E1], logits, bcast(bias[:, :], 1, NT), ALU.add))
                top_k_mask(dve, chain, es[:, :, :], K1, best[:, :, :], named[:, :, :], er[:, :, :], sel[:, :, :])
                dve.wait_ge(exp_ready, 1)
                chain(dve.reduce_sum(total[:, :], prob[:, :, :], AX.X))
                chain(dve.reciprocal(total[:, :], total[:, :]))
                chain(dve.tensor_tensor(prob[:, :, :], prob[:, :, :], bcast(total[:, :], 2, E1), ALU.mult))
                chain(dve.tensor_tensor(prob[:, :, :], prob[:, :, :], sel[:, :, :], ALU.mult))
                chain(dve.reduce_sum(total[:, :], prob[:, :, :], AX.X))
                chain(dve.reciprocal(total[:, :], total[:, :]))
                dve.tensor_tensor(comb[:, :, :], prob[:, :, :], bcast(total[:, :], 2, E1), ALU.mult).then_inc(comb_ready, 1)


def mixture1(nc, env, w, out):
    sem, psum, ident = env["sem"], env["psum"], env["ident"]
    xnT, x, s1 = env["xnT"], env["x"], env["s1"]
    PAIRS = E1 // 2
    STEPS = PAIRS + SH1 // P
    comb_dram = nc.dram_tensor("comb_by_expert", [E1, T], F32, kind="Internal").ap()
    route1(nc, env, w["L1_ffn_router_w"], w["L1_ffn_router_bias"], comb_dram)
    with ExitStack() as local:
        def tmp(name, shape, dt=F32):
            return local.enter_context(nc.sbuf_tensor("e1_" + name, shape, dt))
        xT_h, xT_l = tmp("xTh", [P, DC, T], F16), tmp("xTl", [P, DC, T], F16)
        split16(nc, env, "e1_x", [(xnT[:, :, :], xT_h[:, :, :], xT_l[:, :, :])])
        gu_f = [tmp(f"guf{b}", [P, 2, 2, DC, F1]) for b in range(2)]
        gu_h = [tmp(f"guh{b}", [P, 2, DC, P], F16) for b in range(2)]
        gu_l = [tmp(f"gul{b}", [P, 2, DC, P], F16) for b in range(2)]
        dn_f = [tmp(f"dnf{b}", [P, DC, P]) for b in range(2)]
        dn_h = [tmp(f"dnh{b}", [P, DC, P], F16) for b in range(2)]
        dn_l = [tmp(f"dnl{b}", [P, DC, P], F16) for b in range(2)]
        cb = [tmp(f"cb{b}", [P, T]) for b in range(2)]
        sg = [tmp(f"sg{b}", [P, HALF]) for b in range(2)]
        hf = [tmp(f"hf{b}", [P, HALF]) for b in range(2)]
        h_h = [tmp(f"hh{b}", [P, HALF], F16) for b in range(4)]
        h_l = [tmp(f"hl{b}", [P, HALF], F16) for b in range(4)]
        yT = tmp("yT", [P, DC, T])
        gate1 = [tmp(f"gate{b}", [P, D]) for b in range(2)]
        prod = [tmp(f"prod{b}", [P, D]) for b in range(2)]
        gu_loaded = [sem(f"e1_gl{b}") for b in range(2)]
        dn_loaded = [sem(f"e1_dl{b}") for b in range(2)]
        cb_loaded = [sem(f"e1_cl{b}") for b in range(2)]
        (guh_ready, gul_ready, dnh_ready, dnl_ready, gu_ready, silu_ready, mixed, h_ready, hh_ready, hl_ready,
         down_done, y_ready, t_ready, g_ready, p_ready, x_ready) = (sem("e1_" + s) for s in (
             "gh", "gl", "dh", "dl", "gu", "si", "mi", "h", "hh", "hl", "dn", "y", "t", "g", "p", "x"))
        GU_LOADS = 2 * 16
        wg, wu, wd = (w["L1_ffn_" + k] for k in ("wg", "wu", "wd"))
        swg, swu, swd = (w["L1_ffn_" + k] for k in ("swg", "swu", "swd"))

        with nc.Block() as block:
            @block.sync
            def _(sp):
                def load_shared_gate_up(q, b):
                    e, at = q // 2, (q % 2) * P
                    for j, src in enumerate((swg, swu)):
                        sp.dma_start(gu_f[b][:, j, :, :, :].rearrange("p e c f -> p (e c f)").rearrange("p (c f) -> p c f", c=DC),
                                     src[e, :, at:at + P].rearrange("(p c) f -> p c f", p=P)).then_inc(gu_loaded[b], 16)

                def load_shared_down(q, b):
                    e, at = q // 2, (q % 2) * P
                    sp.dma_start(dn_f[b][:, :, :].rearrange("p c d -> p (c d)"), swd[e, at:at + P, :]).then_inc(dn_loaded[b], 16)

                def load_gate_up(pair, b):
                    for j, src in enumerate((wg, wu)):
                        sp.dma_start(gu_f[b][:, j, :, :, :].rearrange("p e c f -> p e (c f)"),
                                     src[bass.ds(2 * pair, 2), :, :].rearrange("e (p c) f -> p e (c f)", p=P))\
                          .then_inc(gu_loaded[b], 16)

                def load_down(pair, b):
                    sp.dma_start(dn_f[b][:, :, :].rearrange("p c d -> p (c d)"),
                                 wd[bass.ds(2 * pair, 2), :, :].rearrange("e f d -> (e f) d")).then_inc(dn_loaded[b], 16)

                def load_comb(pair, b):
                    for e in range(2):
                        sp.dma_start(cb[b][e * F1:(e + 1) * F1, :],
                                     comb_dram[bass.ds(2 * pair + e, 1), :].rearrange("o t -> (o t)").partition_broadcast(F1))\
                          .then_inc(cb_loaded[b], 16)

                for b in range(2):
                    load_shared_gate_up(b, b)
                    load_shared_down(b, b)
                for b in range(2):
                    load_comb(b, b)

                def loads(pair, b, comb=True):
                    sp.wait_ge(gul_ready, pair + 1)
                    load_gate_up(pair, b)
                    if comb:
                        sp.wait_ge(mixed, 2 * pair - 4)
                        load_comb(pair - 1, 1 - b)
                    sp.wait_ge(dnl_ready, pair + 1)
                    load_down(pair, b)

                for pair in range(3):
                    loads(pair, pair % 2, comb=False)
                with sp.Fori(0, PAIRS // 2 - 2) as i:
                    loads(2 * i + 3, 1)
                    loads(2 * i + 4, 0)
                loads(PAIRS - 1, 1)
                for b in range(2):
                    sp.wait_ge(gul_ready, PAIRS + b + 1)
                    load_shared_gate_up(2 + b, b)
                    if b == 0:
                        sp.wait_ge(mixed, 2 * PAIRS - 4)
                        load_comb(PAIRS - 1, 1)
                    sp.wait_ge(dnl_ready, PAIRS + b + 1)
                    load_shared_down(2 + b, b)

            @block.tensor
            def _(pe):
                def gate_up(s, b, half):
                    hs = 2 * s + half
                    if half == 0:
                        pe.wait_ge(gul_ready, s + 1)
                    if not (isinstance(s, int) and s == 0):
                        pe.wait_ge(h_ready, hs - 1)
                    cols = slice(half * HALF, (half + 1) * HALF)
                    for j in range(2):
                        out = psum[:, 4 + 2 * half + j, :]
                        for c in range(DC):
                            wh, wl = gu_h[b][:, j, c, :], gu_l[b][:, j, c, :]
                            pe.matmul(out, wh, xT_h[:, c, cols], start=(c == 0), stop=False)
                            pe.matmul(out, wh, xT_l[:, c, cols], start=False, stop=False)
                            last = pe.matmul(out, wl, xT_h[:, c, cols], start=False, stop=(c == DC - 1))
                    last.then_inc(gu_ready, 1)

                def down(s, b, half, first=False, end=False):
                    hs = 2 * s + half
                    if half == 0:
                        pe.wait_ge(dnl_ready, s + 1)
                    pe.wait_ge(hl_ready, hs + 1)
                    hh, hl = h_h[2 * b + half][:, :], h_l[2 * b + half][:, :]
                    for c in range(DC):
                        out = psum[:, 2 * c + half, :]
                        wh, wl = dn_h[b][:, c, :], dn_l[b][:, c, :]
                        pe.matmul(out, wh, hh, start=first, stop=False)
                        pe.matmul(out, wh, hl, start=False, stop=False)
                        last = pe.matmul(out, wl, hh, start=False, stop=end)
                    last.then_inc(down_done, 1)

                gate_up(0, 0, 0)
                gate_up(0, 0, 1)
                for half in range(2):
                    gate_up(1, 1, half)
                    down(0, 0, half, first=True)
                with pe.Fori(0, PAIRS // 2) as i:
                    for b in range(2):
                        for half in range(2):
                            gate_up(2 * i + 2 + b, b, half)
                            down(2 * i + 1 + b, 1 - b, half)
                for s in range(STEPS - 2, STEPS):
                    for half in range(2):
                        gate_up(s, s % 2, half)
                        down(s - 1, (s - 1) % 2, half)
                for half in range(2):
                    down(STEPS - 1, (STEPS - 1) % 2, half, end=True)
                for n in range(NT):
                    pe.wait_ge(y_ready, n // 4 + 1)
                    if n >= 2:
                        pe.wait_ge(g_ready, n - 1)
                    for c in range(DC):
                        last = pe.transpose(psum[:, 4 + n % 2, c * P:(c + 1) * P], yT[:, c, n * P:(n + 1) * P], ident[:, :])
                    last.then_inc(t_ready, 1)

            @block.scalar
            def _(act):
                def gate_up_high(s, b, loads, routed):
                    act.wait_ge(gu_loaded[b], GU_LOADS * loads)
                    if not (isinstance(s, int) and s < 2):
                        act.wait_ge(gu_ready, 2 * s - 2)
                    if routed:
                        for j in range(2):
                            last = act.activation(gu_h[b][:, j, :, :].rearrange("p c (e f) -> p e c f", e=2), gu_f[b][:, j, :, :, :],
                                                  ACT.Copy, scale=WSCALE)
                    else:
                        last = act.activation(gu_h[b][:, :, :, :].rearrange("p j c n -> p (j c n)"),
                                              gu_f[b][:, :, :, :, :].rearrange("p j e c f -> p (j e c f)"), ACT.Copy, scale=WSCALE)
                    last.then_inc(guh_ready, 1)

                def down_high(s, b, loads):
                    act.wait_ge(dn_loaded[b], 16 * loads)
                    if not (isinstance(s, int) and s < 2):
                        act.wait_ge(down_done, 2 * s - 2)
                    act.activation(dn_h[b][:, :, :], dn_f[b][:, :, :], ACT.Copy, scale=WSCALE).then_inc(dnh_ready, 1)

                def silu(s, b, half):
                    hs = 2 * s + half
                    act.wait_ge(gu_ready, hs + 1)
                    if not (isinstance(s, int) and s == 0):
                        act.wait_ge(h_ready, hs - 1)
                    act.activation(sg[half][:, :], psum[:, 4 + 2 * half, :], ACT.Silu, scale=1.0 / WSCALE).then_inc(silu_ready, 1)

                def high(s, b, half):
                    hs = 2 * s + half
                    act.wait_ge(h_ready, hs + 1)
                    if not (isinstance(s, int) and s < 2):
                        act.wait_ge(down_done, hs - 3)
                    act.activation(h_h[2 * b + half][:, :], hf[half][:, :], ACT.Copy).then_inc(hh_ready, 1)

                def step(s, b, gate_up=None, down=None):
                    silu(s, b, 0)
                    high(s, b, 0)
                    silu(s, b, 1)
                    if gate_up is not None:
                        gate_up_high(s + 2, b, *gate_up)
                    high(s, b, 1)
                    if down is not None:
                        down_high(s + 1, 1 - b, down)

                gate_up_high(0, 0, 1, False)
                down_high(0, 0, 1)
                gate_up_high(1, 1, 1, False)
                step(0, 0, (2, True), 1)
                step(1, 1, (2, True), 2)
                with act.Fori(0, PAIRS // 2 - 1) as i:
                    step(2 * i + 2, 0, (i + 3, True), i + 2)
                    step(2 * i + 3, 1, (i + 3, True), i + 3)
                LAST = PAIRS // 2 + 2
                step(STEPS - 4, 0, (LAST, False), LAST - 1)
                step(STEPS - 3, 1, (LAST, False), LAST)
                step(STEPS - 2, 0, None, LAST)
                step(STEPS - 1, 1)
                act.wait_ge(down_done, 2 * STEPS)
                for half in range(2):
                    for c in range(DC):
                        last = act.activation(yT[:, c, half * HALF:(half + 1) * HALF], psum[:, 2 * c + half, :], ACT.Copy,
                                              scale=1.0 / WSCALE)
                    last.then_inc(y_ready, 1)
                for n in range(NT):
                    act.wait_ge(t_ready, n + 1)
                    if n >= 2:
                        act.wait_ge(p_ready, n - 1)
                    act.activation(gate1[n % 2][:, :], psum[:, 4 + n % 2, 0:D], ACT.Silu).then_inc(g_ready, 1)

            @block.gpsimd
            def _(pool):
                with pool.Fori(0, PAIRS // 2) as i:
                    for b in range(2):
                        for half in range(2):
                            pool.wait_ge(silu_ready, 2 * (2 * i + b + 2) + half + 1)
                            if half == 0:
                                pool.wait_ge(cb_loaded[b], 32 * i + 32)
                            pool.tensor_tensor(sg[half][:, :], sg[half][:, :], cb[b][:, half * HALF:(half + 1) * HALF],
                                               ALU.mult).then_inc(mixed, 1)

            @block.vector
            def _(dve):
                def gate_up_low(s, b, routed):
                    dve.wait_ge(guh_ready, s + 1)
                    if routed:
                        by_expert = "p (e f) -> p e f"
                        for j in range(2):
                            for c in range(DC):
                                last = dve.scalar_tensor_tensor(
                                    gu_l[b][:, j, c, :].rearrange(by_expert, e=2), gu_f[b][:, j, :, c, :], WSCALE,
                                    gu_h[b][:, j, c, :].rearrange(by_expert, e=2), ALU.mult, ALU.subtract)
                    else:
                        last = dve.scalar_tensor_tensor(gu_l[b][:, :, :, :].rearrange("p j c n -> p (j c n)"),
                                                        gu_f[b][:, :, :, :, :].rearrange("p j e c f -> p (j e c f)"), WSCALE,
                                                        gu_h[b][:, :, :, :].rearrange("p j c n -> p (j c n)"), ALU.mult, ALU.subtract)
                    last.then_inc(gul_ready, 1)

                def down_low(s, b):
                    dve.wait_ge(dnh_ready, s + 1)
                    dve.scalar_tensor_tensor(dn_l[b][:, :, :], dn_f[b][:, :, :], WSCALE, dn_h[b][:, :, :],
                                             ALU.mult, ALU.subtract).then_inc(dnl_ready, 1)

                def hidden(s, b, half, routed):
                    hs = 2 * s + half
                    if routed:
                        dve.wait_ge(mixed, hs - 3)
                    else:
                        dve.wait_ge(silu_ready, hs + 1)
                    if not (isinstance(s, int) and s == 0):
                        dve.wait_ge(hl_ready, hs - 1)
                    dve.scalar_tensor_tensor(hf[half][:, :], psum[:, 5 + 2 * half, :], 1.0 / WSCALE, sg[half][:, :],
                                             ALU.mult, ALU.mult).then_inc(h_ready, 1)

                def low(s, b, half):
                    hs = 2 * s + half
                    dve.wait_ge(hh_ready, hs + 1)
                    dve.tensor_tensor(h_l[2 * b + half][:, :], hf[half][:, :], h_h[2 * b + half][:, :],
                                      ALU.subtract).then_inc(hl_ready, 1)

                def step(s, b, routed, gate_up=None, down=True):
                    hidden(s, b, 0, routed)
                    low(s, b, 0)
                    if gate_up is not None:
                        gate_up_low(s + 2, b, gate_up)
                    hidden(s, b, 1, routed)
                    low(s, b, 1)
                    if down:
                        down_low(s + 1, 1 - b)

                gate_up_low(0, 0, False)
                down_low(0, 0)
                gate_up_low(1, 1, False)
                step(0, 0, False, True)
                step(1, 1, False, True)
                with dve.Fori(0, PAIRS // 2 - 1) as i:
                    step(2 * i + 2, 0, True, True)
                    step(2 * i + 3, 1, True, True)
                step(STEPS - 4, 0, True, False)
                step(STEPS - 3, 1, True, False)
                step(STEPS - 2, 0, False)
                step(STEPS - 1, 1, False, down=False)
                for n in range(NT):
                    dve.wait_ge(g_ready, n + 1)
                    dve.tensor_tensor(prod[n % 2][:, :], gate1[n % 2][:, :], s1[:, n, :], ALU.mult).then_inc(p_ready, 1)
                    dve.wait_ge(p_ready, n + 1)
                    dve.tensor_tensor(x[:, n, :], x[:, n, :], prod[n % 2][:, :], ALU.add).then_inc(x_ready, 1)

    store_tokens(nc, env, "out", out, x)


def program(nc, w, out):
    with ExitStack() as ctx:
        def sb(name, shape, dt):
            return ctx.enter_context(nc.sbuf_tensor(name, shape, dt))

        in_use = []

        def sem(name):
            in_use.append(nc.alloc_semaphore(name=name))
            return in_use[-1]

        env = {"sem": sem, "sb": sb}
        env["psum"] = ctx.enter_context(nc.psum_tensor("psum", [P, 8, HALF], F32))
        env["x"] = x = sb("x", [P, NT, D], F32)
        env["x_loaded"] = x_loaded = env["sem"]("x_loaded")
        with nc.Block() as block:
            @block.sync
            def _(sp):
                sp.dma_start(x[:, :, :], w["L0_attn_x"][0].rearrange("(n p) d -> p n d", p=P)).then_inc(x_loaded, 16)
        identities(nc, env)
        with ExitStack() as layer0:
            def tmp(name, shape, dt):
                return layer0.enter_context(nc.sbuf_tensor(name, shape, dt))
            env["gate0"] = tmp("gate0", [P, NT, D], F32)
            env["xT_h"], env["xT_l"] = tmp("xT_h", [P, DC, T], F16), tmp("xT_l", [P, DC, T], F16)
            with ExitStack() as norm:
                env["xn"] = norm.enter_context(nc.sbuf_tensor("xn0", [P, NT, D], F32))
                env["xnT"] = xnT = norm.enter_context(nc.sbuf_tensor("xnT0", [P, DC, T], F32))
                layer_norm(nc, env, "ln0", x, env["xn"], xnT)
                split16(nc, env, "xT0", [(xnT[:, :, :], env["xT_h"][:, :, :], env["xT_l"][:, :, :])])
                mixture0(nc, env, w)
            env["oT_h"], env["oT_l"] = tmp("oT_h", [P, H, T], F16), tmp("oT_l", [P, H, T], F16)
            attention0(nc, env, w)
            project0(nc, env, w)
        nc.clear_and_free_semaphores(in_use)
        nc.all_engine_barrier()
        env["xn"], env["xnT"] = sb("xn1", [P, NT, D], F32), sb("xnT1", [P, DC, T], F32)
        env["s1"] = sb("s1", [P, NT, D], F32)
        layer_norm(nc, env, "ln1", x, env["xn"], env["xnT"], interleaved=True)
        gated_linear_attention(nc, env, w)
        mixture1(nc, env, w, out)


_INS = ["L0_attn_x"] + ["L0_attn_" + k for k in ("wq", "wk", "wv", "wo", "q_scale", "k_scale")] \
    + ["L0_ffn_" + k for k in ("router_w", "e_bias", "W_gate", "W_up", "W_down", "shared_gate", "shared_up", "shared_down")] \
    + ["L1_attn_" + k for k in ("Wq", "Wk", "Wkg1", "Wkg2", "bkg2", "Wv", "Wg", "bg", "Wo", "ln1_w", "ln2_w", "W1", "W3", "W2")] \
    + ["L1_ffn_" + k for k in ("router_w", "router_bias", "wg", "wu", "wd", "swg", "swu", "swd")]


def kernel(**inputs):
    import concourse.bacc as bacc
    from concourse.bass_utils import run_bass_kernel_spmd

    nc = bacc.Bacc("TRN2", target_bir_lowering=False, num_devices=1)
    arrays, aps = {}, {}
    for name in _INS:
        a = np.ascontiguousarray(inputs[name])
        arrays["in_" + name] = a
        aps[name] = nc.dram_tensor("in_" + name, a.shape, mybir.dt.from_np(a.dtype), kind="ExternalInput").ap()
    out = nc.dram_tensor("out", [1, T, D], F32, kind="ExternalOutput").ap()
    program(nc, aps, out[0])
    r = run_bass_kernel_spmd(nc, [arrays], core_ids=[0])
    return r.results[0]["out"]
```

```python
import concourse.bass as bass
import numpy as np
from concourse import mybir
from contextlib import ExitStack

F32 = mybir.dt.float32
F16 = mybir.dt.float16
ALU = mybir.AluOpType
ACT = mybir.ActivationFunctionType
AX = mybir.AxisListType

P = 128
T = 1024
NT = T // P
D = 256
DC = D // P
HALF = 512
LN_EPS = 1e-5
X_TILES = 2

H, HD = 16, 128
RMS_EPS0 = 1e-6
WSCALE = 64.0

E0, NG0, GE0, TKG0, K0, I0 = 32, 8, 4, 3, 4, 128
CAP = int(np.ceil(1.25 * T / E0))
SLOTS = E0 * CAP
ST = SLOTS // P
ROUTE_SCALE = 2.5
IS = 256

GH, GK, GV = 16, 8, 16
RMS_EPS1 = 1e-5
GATE_NORM = 16.0
HID = 704
E1, F1, K1 = 64, 64, 4
SH1 = 512

SENTINEL = -1.0e30
TAKEN = -3.0e38


class Chain:

    def __init__(self, engine, done):
        self.engine, self.done, self.count = engine, done, 0

    def __call__(self, instruction):
        self.count += 1
        instruction.then_inc(self.done, 1)
        self.engine.wait_ge(self.done, self.count)


def bcast(ap, axis, n):
    a = ap.unsqueeze(axis)
    shape = list(a.shape)
    shape[axis] = n
    return a.to_broadcast(shape)


def identities(nc, env):
    ident, ident16 = env["sb"]("ident", [P, P], F32), env["sb"]("ident16", [P, P], F16)
    env.update(ident=ident, ident16=ident16)
    done = env["sem"]("ident_done")
    with nc.Block() as block:
        @block.gpsimd
        def _(pool):
            chain = Chain(pool, done)
            for m in (ident, ident16):
                chain(pool.memset(m[:, :], 0.0))
                chain(pool.affine_select(out=m[:, :], in_=m[:, :], compare_op=ALU.not_equal, fill=1.0,
                                         base=0, pattern=[[-1, P]], channel_multiplier=1))


def band(pool, chain, out, first, pattern, channel_multiplier, width):
    chain(pool.memset(out, 1.0))
    chain(pool.affine_select(out=out, in_=out, compare_op=ALU.is_ge, fill=0.0, base=first, pattern=pattern,
                             channel_multiplier=channel_multiplier))
    chain(pool.affine_select(out=out, in_=out, compare_op=ALU.is_ge, fill=0.0, base=width - 1 - first,
                             pattern=[[-step, n] for step, n in pattern], channel_multiplier=-channel_multiplier))


def mixture_masks(nc, env, sb):
    ones16 = sb("ones16", [P, P], F16)
    upper16 = sb("upper16", [P, P], F16)
    steps = sb("steps", [P, CAP], F32)
    slot_expert = sb("slot_expert", [P, ST, E0], F32)
    env.update(ones16=ones16, upper16=upper16, steps=steps, slot_expert=slot_expert)
    done = env["sem"]("masks_done")

    def fill(pool):
        chain = Chain(pool, done)
        chain(pool.memset(ones16[:, :], 1.0))
        chain(pool.affine_select(out=upper16[:, :], in_=ones16[:, :], compare_op=ALU.is_gt, fill=0.0,
                                 base=0, pattern=[[1, P]], channel_multiplier=-1))
        chain(pool.iota(steps[:, :], [[1, CAP]], base=1, channel_multiplier=0,
                        allow_small_or_imprecise_dtypes=True))
        band(pool, chain, slot_expert[:, :, :], 0, [[P, ST], [-CAP, E0]], 1, CAP)
    return fill


def head_masks(nc, env, sb):
    spread = sb("spread", [P, GK, P], F16)
    gather_h = sb("gather_h", [P, GK, P], F32)
    env.update(spread=spread, gather_h=gather_h)
    done = env["sem"]("head_masks_done")

    def fill(pool):
        chain = Chain(pool, done)
        band(pool, chain, spread[:, :, :], 0, [[GH * GK, GK], [1, P]], -GK, GK)
        band(pool, chain, gather_h[:, :, :], 0, [[GH * GK, GK], [-GK, P]], 1, GK)
    return fill


def layer_norm(nc, env, tag, x, xn, xnT, interleaved=False, loads=None, side=None, stats=None,
               squares=None):
    sem, ident, psum = env["sem"], env["ident"], env["psum"]
    with ExitStack() as local:
        if stats is None:
            raw = local.enter_context(nc.sbuf_tensor(tag + "_stats", [P, NT, 6], F32))
            mv = local.enter_context(nc.sbuf_tensor(tag + "_mv", [P, NT, 2], F32))
        else:
            mv = stats
        var = local.enter_context(nc.sbuf_tensor(tag + "_var", [P, NT], F32))
        std = local.enter_context(nc.sbuf_tensor(tag + "_std", [P, NT], F32))
        inv = local.enter_context(nc.sbuf_tensor(tag + "_inv", [P, NT], F32))
        stats_done, mv_done, var_ready, std_ready = (sem(tag + s) for s in ("_st", "_mv", "_var", "_std"))
        inv_done, xn_ready, xT_ready, evac_done = (sem(tag + s) for s in ("_inv", "_xn", "_xT", "_ev"))
        with nc.Block() as block:
            if loads:
                block.sync(loads)
            if side:
                block.gpsimd(side)

            @block.vector
            def _(dve):
                if stats is None:
                    for n in range(NT):
                        if n % X_TILES == 0:
                            dve.wait_ge(env["x_loaded"][n // X_TILES], 16)
                        dve.bn_stats(raw[:, n, :], x[:, n, :]).then_inc(stats_done, 1)
                    for n in range(NT):
                        dve.wait_ge(stats_done, n + 1)
                        dve.bn_aggr(mv[:, n, :], raw[:, n, :]).then_inc(mv_done, 1)
                    dve.wait_ge(mv_done, NT)
                dve.tensor_scalar(var[:, :], mv[:, :, 1], LN_EPS, None, ALU.add).then_inc(var_ready, 1)
                dve.wait_ge(std_ready, 1)
                dve.reciprocal(inv[:, :], std[:, :]).then_inc(inv_done, 1)
                dve.wait_ge(inv_done, 1)
                for n in range(NT):
                    dve.tensor_scalar(xn[:, n, :], x[:, n, :], mv[:, n, 0:1], inv[:, n:n + 1],
                                      ALU.subtract, ALU.mult).then_inc(xn_ready, 1)

            @block.scalar
            def _(act):
                act.wait_ge(var_ready, 1)
                act.activation(std[:, :], var[:, :], ACT.Sqrt).then_inc(std_ready, 1)
                for n in range(NT):
                    act.wait_ge(xT_ready, n + 1)
                    act.activation(xnT[:, :, n * P:(n + 1) * P],
                                   psum[:, n % 2, 0:D].rearrange("p (c t) -> p c t", c=DC),
                                   ACT.Copy).then_inc(evac_done, 1)
                    if squares:
                        act.wait_ge(xn_ready, n + 1)
                        squares(act, n)

            @block.tensor
            def _(pe):
                for n in range(NT):
                    pe.wait_ge(xn_ready, n + 1)
                    if n >= 2:
                        pe.wait_ge(evac_done, n - 1)
                    for c in range(DC):
                        channels = xn[:, n, c::DC] if interleaved else xn[:, n, c * P:(c + 1) * P]
                        last = pe.transpose(psum[:, n % 2, c * P:(c + 1) * P], channels, ident[:, :])
                    last.then_inc(xT_ready, 1)


def top_k_mask(dve, chain, scores, k, best, named, replaced, mask):
    m = scores.shape[2] - 8
    chain(dve.memset(named, SENTINEL))
    for n in range(NT):
        chain(dve.max(best[:, n, :], scores[:, n, 0:m]))
    chain(dve.tensor_copy(named[:, :, 0:k], best[:, :, 0:k]))
    for n in range(NT):
        chain(dve.match_replace(replaced[:, n, :], named[:, n, :], scores[:, n, :], TAKEN))
    chain(dve.tensor_scalar(mask, replaced[:, :, 0:m], TAKEN / 2, None, ALU.is_lt))


def route0(nc, env, router_w, e_bias):
    sem, psum, ident = env["sem"], env["psum"], env["ident"]
    xnT, ones16, upper16, steps = env["xnT"], env["ones16"], env["upper16"], env["steps"]
    member, wk_h, wk_l, xn_h, xn_l = (env[k] for k in ("member", "wk_h", "wk_l", "xn_h", "xn_l"))
    xg_h, xg_l, w_slot, slot_expert = env["xg_h"], env["xg_l"], env["w_slot"], env["slot_expert"]
    with ExitStack() as local:
        def tmp(name, shape, dt=F32):
            return local.enter_context(nc.sbuf_tensor("r0_" + name, shape, dt))
        rw, rwT, bias = tmp("rw", [E0, D]), tmp("rwT", [P, DC, E0]), tmp("bias", [P, E0])
        prob, sc = tmp("prob", [P, NT, E0]), tmp("sc", [P, NT, E0])
        hi2, lo2, sums = tmp("hi2", [P, NT * NG0, 2]), tmp("lo2", [P, NT * NG0, 2]), tmp("sums", [P, NT * NG0, 2])
        gs, gr, gm = tmp("gs", [P, NT, NG0 + 8]), tmp("gr", [P, NT, NG0 + 8]), tmp("gm", [P, NT, NG0])
        es, er, sel = tmp("es", [P, NT, E0 + 8]), tmp("er", [P, NT, E0 + 8]), tmp("sel", [P, NT, E0])
        best, named = tmp("best", [P, NT, 8]), tmp("named", [P, NT, 8])
        sel16 = tmp("sel16", [P, NT, E0], F16)
        w, wsum, winv = tmp("w", [P, NT, E0]), tmp("wsum", [P, NT]), tmp("winv", [P, NT])
        keep, place = tmp("keep", [P, NT, E0]), tmp("place", [P, NT, E0])
        wmask = tmp("wmask", [P, ST, E0])
        IC = IS // P
        w3T, hT = env["shared_wT"], env["shared_hT"]
        w3 = [tmp(f"w{i}", [P, 2, D]) for i in range(3)]
        sg, up = tmp("sg", [P, 2, HALF]), tmp("up", [P, 2, HALF])
        w3_loaded = [sem(f"r0_w3_{i}") for i in range(3)]
        wT_ready, wT_done, gu_ready, silu_done, up_done, h_ready = (sem("r0_" + s) for s in ("wT", "wTd", "gu", "si", "up", "h"))
        loaded = [sem("r0_ld0"), sem("r0_ld1")]
        member_ready, gathered, xg_done, ws_ready, wm_done = (sem("r0_" + s) for s in ("me", "ga", "xg", "ws", "wm"))
        high_done, xn_split = (sem("r0_" + s) for s in ("hi", "xn"))
        wf, w_h, w_l, w_high, w_ready = (env[k] for k in ("wf", "w_h", "w_l", "w_high", "w_ready"))
        cuts = [(0, 512), (512, 512), (1024, 256)]
        rwT_ready, rwT_done, logits_ready, prob_ready = (sem("r0_" + s) for s in ("rwT", "rwTd", "lg", "pr"))
        sel_ready, pos_ready, dve_done = (sem("r0_" + s) for s in ("sel", "pos", "dve"))
        logits = psum[:, 6, 0:NT * E0].rearrange("p (n e) -> p n e", n=NT)
        pos = psum[:, 7, 0:NT * E0].rearrange("p (n e) -> p n e", n=NT)
        turned = psum[:, 7, 0:DC * E0].rearrange("p (c e) -> p c e", c=DC)
        ws = psum[:, 6, 0:ST * E0].rearrange("p (s e) -> p s e", s=ST)

        def load_first(sp):
            sp.dma_start(rw[:, :], router_w).then_inc(loaded[0], 16)
            sp.dma_start(bias[:, :], e_bias.partition_broadcast(P)).then_inc(loaded[1], 16)
            for i, src in enumerate(env["shared_weights"]):
                sp.dma_start(w3[i][:, :, :], src.rearrange("(a p) d -> p a d", p=P)).then_inc(w3_loaded[i], 16)
        layer_norm(nc, env, "ln0", env["x"], env["xn"], xnT, loads=load_first, side=env["fill_masks"])

        with nc.Block() as block:
            @block.sync
            def _(sp):
                for e in range(EB):
                    load_expert(sp, env, e, e)
                for b in range(EB):
                    sp.wait_ge(w_ready, b + 1)
                    load_expert(sp, env, EB + b, b)

            @block.tensor
            def _(pe):
                pe.wait_ge(loaded[0], 16)
                for c in range(DC):
                    last = pe.transpose(turned[:, c, :], rw[:, c * P:(c + 1) * P], ident[0:E0, 0:E0])
                last.then_inc(rwT_ready, 1)
                pe.wait_ge(rwT_done, 1)
                for n in range(NT):
                    for c in range(DC):
                        last = pe.matmul(logits[:, n, :], xnT[:, c, n * P:(n + 1) * P], rwT[:, c, :],
                                         start=(c == 0), stop=(c == DC - 1))
                last.then_inc(logits_ready, 1)
                for i in range(3):
                    pe.wait_ge(w3_loaded[i], 16)
                    for a in range(2):
                        for c in range(2):
                            last = pe.transpose(psum[:, i, (c * 2 + a) * P:(c * 2 + a + 1) * P],
                                                w3[i][:, a, c * P:(c + 1) * P], ident[:, :])
                    last.then_inc(wT_ready, 1)
                pe.wait_ge(wT_done, 3)

                def shared_gate_up(step):
                    t, ic = step // IC, step % IC
                    if step >= 2:
                        pe.wait_ge(up_done, step - 1)
                    for j in range(2):
                        for c in range(DC):
                            last = pe.matmul(psum[:, 2 * (step % 2) + j, :], w3T[j][:, c, ic * P:(ic + 1) * P],
                                             xnT[:, c, t * HALF:(t + 1) * HALF], start=(c == 0), stop=(c == DC - 1))
                    last.then_inc(gu_ready, 1)

                for step in range(2 * IC - 2):
                    shared_gate_up(step)
                pe.wait_ge(sel_ready, 1)
                for n in range(NT):
                    for i in range(n):
                        pe.matmul(pos[:, n, :], ones16[:, :], sel16[:, i, :], start=(i == 0), stop=False)
                    last = pe.matmul(pos[:, n, :], upper16[:, :], sel16[:, n, :], start=(n == 0), stop=True)
                last.then_inc(pos_ready, 1)
                for step in range(2 * IC - 2, 2 * IC):
                    shared_gate_up(step)
                pe.wait_ge(up_done, 2 * IC)
                pe.wait_ge(xn_split, 1)
                for n in range(NT):
                    pe.wait_ge(member_ready, n + 1)
                    for c in range(DC):
                        for k, (at, size) in enumerate(cuts):
                            bank = c * len(cuts) + k
                            slots = member[:, n, :, :].rearrange("p e c -> p (e c)")[:, at:at + size]
                            pe.matmul(psum[:, bank, 0:size], xn_h[:, n, c::DC], slots,
                                      start=(n == 0), stop=False)
                            last = pe.matmul(psum[:, bank, 0:size], xn_l[:, n, c::DC], slots,
                                             start=False, stop=(n == NT - 1))
                            if n == NT - 1:
                                last.then_inc(gathered, 1)
                for s in range(ST):
                    for n in range(NT):
                        slots = member[:, n, :, :].rearrange("p e c -> p (e c)")[:, s * P:(s + 1) * P]
                        pe.matmul(ws[:, s, :], slots, wk_h[:, n, :], start=(n == 0), stop=False)
                        last = pe.matmul(ws[:, s, :], slots, wk_l[:, n, :], start=False, stop=(n == NT - 1))
                last.then_inc(ws_ready, 1)

            @block.scalar
            def _(act):
                act.wait_ge(rwT_ready, 1)
                act.activation(rwT[:, :, :], turned, ACT.Copy).then_inc(rwT_done, 1)
                act.wait_ge(logits_ready, 1)
                act.activation(prob[:, :, :], logits, ACT.Sigmoid).then_inc(prob_ready, 1)
                for i in range(3):
                    act.wait_ge(wT_ready, i + 1)
                    act.activation(w3T[i][:, :, :], psum[:, i, :].rearrange("p (c x) -> p c x", c=2),
                                   ACT.Copy).then_inc(wT_done, 1)

                def weights_high(e):
                    act.wait_ge(env["expert_loaded"][e], 48)
                    act.activation(w_h[e][:, :, :], wf[e][:, :, :], ACT.Copy, scale=WSCALE).then_inc(w_high, 1)
                    act.wait_ge(w_high, 2 * e + 1)
                    act.activation(wf[e][:, :, :], wf[e][:, :, :], ACT.Copy, scale=WSCALE).then_inc(w_high, 1)

                for step in range(2 * IC):
                    act.wait_ge(gu_ready, step + 1)
                    if step >= 2:
                        act.wait_ge(h_ready, step - 1)
                    bank = 2 * (step % 2)
                    act.activation(sg[:, step % 2, :], psum[:, bank, :], ACT.Silu).then_inc(silu_done, 1)
                    act.activation(up[:, step % 2, :], psum[:, bank + 1, :], ACT.Copy).then_inc(up_done, 1)
                    weights_high(step)
                for e in range(2 * IC, EB):
                    weights_high(e)
                for c in range(DC):
                    for k, (at, size) in enumerate(cuts):
                        bank = c * len(cuts) + k
                        act.wait_ge(gathered, bank + 1)
                        act.activation(xg_h[:, c, at:at + size], psum[:, bank, 0:size], ACT.Copy).then_inc(xg_done, 1)

            @block.gpsimd
            def _(pool):
                def weights_low(e):
                    pool.wait_ge(w_high, 2 * e + 2)
                    pool.tensor_tensor(w_l[e][:, :, :], wf[e][:, :, :], w_h[e][:, :, :], ALU.subtract).then_inc(w_ready, 1)

                xn = env["xn"]
                pool.tensor_copy(xn_h[:, :, :], xn[:, :, :]).then_inc(high_done, 1)
                pool.wait_ge(high_done, 1)
                pool.tensor_tensor(xn_l[:, :, :], xn[:, :, :], xn_h[:, :, :], ALU.subtract).then_inc(xn_split, 1)
                for step in range(2 * IC):
                    t, ic = step // IC, step % IC
                    pool.wait_ge(silu_done, step + 1)
                    pool.wait_ge(up_done, step + 1)
                    pool.tensor_tensor(hT[:, ic, t * HALF:(t + 1) * HALF], up[:, step % 2, :], sg[:, step % 2, :],
                                       ALU.mult).then_inc(h_ready, 1)
                    weights_low(step)
                for e in range(2 * IC, EB):
                    weights_low(e)

            @block.vector
            def _(dve):
                chain = Chain(dve, dve_done)
                dve.wait_ge(prob_ready, 1)
                dve.wait_ge(loaded[1], 16)
                chain(dve.tensor_tensor(sc[:, :, :], prob[:, :, :], bcast(bias[:, :], 1, NT), ALU.add))
                pair = sc[:, :, :].rearrange("p n (g a b) -> p (n g) a b", a=2, b=2)
                chain(dve.tensor_tensor(hi2[:, :, :], pair[:, :, :, 0], pair[:, :, :, 1], ALU.max))
                chain(dve.tensor_tensor(lo2[:, :, :], pair[:, :, :, 0], pair[:, :, :, 1], ALU.min))
                chain(dve.tensor_tensor(sums[:, :, :], hi2[:, :, :], lo2[:, :, :], ALU.add))
                chain(dve.tensor_tensor(lo2[:, :, 0], hi2[:, :, 0], hi2[:, :, 1], ALU.add))
                chain(dve.tensor_tensor(lo2[:, :, 1], sums[:, :, 0], sums[:, :, 1], ALU.max))
                chain(dve.memset(gs[:, :, :], SENTINEL))
                chain(dve.tensor_tensor(gs[:, :, 0:NG0], lo2[:, :, 0].rearrange("p (n g) -> p n g", n=NT),
                                        lo2[:, :, 1].rearrange("p (n g) -> p n g", n=NT), ALU.max))
                top_k_mask(dve, chain, gs[:, :, :], TKG0, best[:, :, :], named[:, :, :], gr[:, :, :], gm[:, :, :])
                chain(dve.memset(es[:, :, :], SENTINEL))
                for a in range(GE0):
                    chain(dve.tensor_tensor(es[:, :, a:E0:GE0], sc[:, :, a:E0:GE0], gm[:, :, :], ALU.mult))
                chain(dve.tensor_scalar(es[:, :, 0:E0], es[:, :, 0:E0], 0.0, None, ALU.add))
                top_k_mask(dve, chain, es[:, :, :], K0, best[:, :, :], named[:, :, :], er[:, :, :], sel[:, :, :])
                dve.tensor_copy(sel16[:, :, :], sel[:, :, :]).then_inc(sel_ready, 1)
                chain(dve.tensor_tensor(w[:, :, :], prob[:, :, :], sel[:, :, :], ALU.mult))
                chain(dve.reduce_sum(wsum[:, :], w[:, :, :], AX.X))
                chain(dve.tensor_scalar(wsum[:, :], wsum[:, :], 1e-20, None, ALU.add))
                chain(dve.reciprocal(winv[:, :], wsum[:, :]))
                chain(dve.scalar_tensor_tensor(w[:, :, :], w[:, :, :], ROUTE_SCALE, bcast(winv[:, :], 2, E0),
                                               ALU.mult, ALU.mult))
                dve.wait_ge(pos_ready, 1)
                chain(dve.scalar_tensor_tensor(keep[:, :, :], pos, float(CAP), sel[:, :, :], ALU.is_lt, ALU.mult))
                chain(dve.scalar_tensor_tensor(place[:, :, :], pos, 1.0, keep[:, :, :], ALU.add, ALU.mult))
                chain(dve.tensor_tensor(w[:, :, :], w[:, :, :], keep[:, :, :], ALU.mult))
                chain(dve.tensor_copy(wk_h[:, :, :], w[:, :, :]))
                chain(dve.tensor_tensor(wk_l[:, :, :], w[:, :, :], wk_h[:, :, :], ALU.subtract))
                for n in range(NT):
                    dve.tensor_tensor(member[:, n, :, :], bcast(place[:, n, :], 2, CAP),
                                      bcast(steps[:, :], 1, E0), ALU.is_equal).then_inc(member_ready, 1)
                for c in range(DC):
                    for k, (at, size) in enumerate(cuts):
                        bank = c * len(cuts) + k
                        dve.wait_ge(xg_done, bank + 1)
                        dve.tensor_tensor(xg_l[:, c, at:at + size], psum[:, bank, 0:size], xg_h[:, c, at:at + size], ALU.subtract)
                dve.wait_ge(ws_ready, 1)
                dve.tensor_tensor(wmask[:, :, :], ws, slot_expert[:, :, :], ALU.mult).then_inc(wm_done, 1)
                dve.wait_ge(wm_done, 1)
                dve.reduce_sum(w_slot[:, :], wmask[:, :, :], AX.X).then_inc(wm_done, 1)


EB = 8


def load_expert(sp, env, e, b):
    w_gate, w_up, w_down = env["expert_weights"]
    wf, loaded = env["wf"][b], env["expert_loaded"][b]
    for j, src in enumerate((w_gate, w_up)):
        sp.dma_start(wf[:, DC * j:DC * (j + 1), :].rearrange("p c i -> p (c i)"),
                     src[bass.ds(e, 1), :, :].rearrange("o (p c) i -> p (o c i)", p=P)).then_inc(loaded, 16)
    sp.dma_start(wf[:, 2 * DC:, :].rearrange("p c d -> p (c d)"),
                 w_down[bass.ds(e, 1), :, :].rearrange("o i d -> (o i) d")).then_inc(loaded, 16)


def experts0(nc, env):
    sem, psum, xg_h, xg_l, yT, wf, loaded = (env[k] for k in ("sem", "psum", "xg_h", "xg_l", "yT", "wf", "expert_loaded"))
    w_h, w_l, w_ready, xnT = (env[k] for k in ("w_h", "w_l", "w_ready", "xnT"))
    with ExitStack() as local:
        def tmp(name, shape, dt=F32):
            return local.enter_context(nc.sbuf_tensor("e0_" + name, shape, dt))
        BANKS = 4
        sg, hf = ([tmp(f"{n}{b}", [P, CAP]) for b in range(BANKS)] for n in ("sg", "hf"))
        h_h, h_l = ([tmp(f"{n}{b}", [P, CAP], F16) for b in range(BANKS)] for n in ("hh", "hl"))
        wh_ready, gu_ready, silu_done, h_ready, hh_ready, hl_ready, y_ready, y_done, x_high = (
            sem("e0_" + s) for s in ("nwh", "gu", "si", "h", "hh", "hl", "y", "yd", "xh"))

        def rounds(engine, *jobs):
            def one(i, last):
                for b in range(EB + max(late for late, _, _ in jobs)):
                    for late, do, prepares in jobs:
                        if 0 <= b - late < EB and not (last and prepares):
                            do(i, b - late)
            with engine.Fori(0, E0 // EB - 1) as i:
                one(i, False)
            one(E0 // EB - 1, True)

        with nc.Block() as block:
            @block.sync
            def _(sp):
                with sp.Fori(0, E0 // EB - 2) as i:
                    for b in range(EB):
                        sp.wait_ge(w_ready, EB * i + EB + b + 1)
                        load_expert(sp, env, EB * i + 2 * EB + b, b)

            @block.tensor
            def _(pe):
                def gate_up(i, b):
                    pe.wait_ge(w_ready, EB * i + b + 1)
                    slots = bass.ds((EB * i + b) * CAP, CAP)
                    for j in range(2):
                        out = psum[:, b % BANKS, j * CAP:(j + 1) * CAP]
                        for c in range(DC):
                            wh, wl = w_h[b][:, DC * j + c, :], w_l[b][:, DC * j + c, :]
                            pe.matmul(out, wh, xg_h[:, c, slots], start=(c == 0), stop=False)
                            pe.matmul(out, wh, xg_l[:, c, slots], start=False, stop=False)
                            last = pe.matmul(out, wl, xg_h[:, c, slots], start=False, stop=(c == DC - 1))
                    last.then_inc(gu_ready, 1)

                def down(i, b):
                    pe.wait_ge(hl_ready, EB * i + b + 1)
                    hh, hl = h_h[b % BANKS][:, :], h_l[b % BANKS][:, :]
                    for c in range(DC):
                        out = psum[:, BANKS + b % BANKS, c * CAP:(c + 1) * CAP]
                        wh, wl = w_h[b][:, 2 * DC + c, :], w_l[b][:, 2 * DC + c, :]
                        pe.matmul(out, wh, hh, start=True, stop=False)
                        pe.matmul(out, wh, hl, start=False, stop=False)
                        last = pe.matmul(out, wl, hh, start=False, stop=True)
                    last.then_inc(y_ready, 1)
                rounds(pe, (3, down, False), (0, gate_up, False))

            @block.scalar
            def _(act):
                def silu(i, b):
                    act.wait_ge(gu_ready, EB * i + b + 1)
                    act.activation(sg[b % BANKS][:, :], psum[:, b % BANKS, 0:CAP], ACT.Silu,
                                   scale=1.0 / WSCALE).then_inc(silu_done, 1)

                def hidden_high(i, b):
                    act.wait_ge(h_ready, EB * i + b + 1)
                    act.activation(h_h[b % BANKS][:, :], hf[b % BANKS][:, :], ACT.Copy).then_inc(hh_ready, 1)

                def next_high(i, b):
                    act.wait_ge(y_ready, EB * i + b + 1)
                    act.wait_ge(loaded[b], 48 * i + 96)
                    act.activation(w_h[b][:, :, :], wf[b][:, :, :], ACT.Copy, scale=WSCALE).then_inc(wh_ready, 1)
                rounds(act, (0, silu, False), (3, next_high, True), (0, hidden_high, False))

            @block.vector
            def _(dve):
                def hidden(i, b):
                    dve.wait_ge(silu_done, EB * i + b + 1)
                    dve.scalar_tensor_tensor(hf[b % BANKS][:, :], psum[:, b % BANKS, CAP:2 * CAP], 1.0 / WSCALE,
                                             sg[b % BANKS][:, :], ALU.mult, ALU.mult).then_inc(h_ready, 1)

                def hidden_low(i, b):
                    dve.wait_ge(hh_ready, EB * i + b + 1)
                    dve.tensor_tensor(h_l[b % BANKS][:, :], hf[b % BANKS][:, :], h_h[b % BANKS][:, :],
                                      ALU.subtract).then_inc(hl_ready, 1)

                def outputs(i, b):
                    dve.wait_ge(y_ready, EB * i + b + 1)
                    dve.tensor_scalar(yT[:, :, bass.ds((EB * i + b) * CAP, CAP)],
                                      psum[:, BANKS + b % BANKS, 0:DC * CAP].rearrange("p (c s) -> p c s", c=DC),
                                      1.0 / WSCALE, None, ALU.mult).then_inc(y_done, 1)

                def next_low(i, b):
                    dve.wait_ge(wh_ready, EB * i + b + 1)
                    dve.scalar_tensor_tensor(w_l[b][:, :, :], wf[b][:, :, :], WSCALE, w_h[b][:, :, :],
                                             ALU.mult, ALU.subtract).then_inc(w_ready, 1)
                rounds(dve, (0, hidden, False), (3, next_low, True), (0, hidden_low, False), (3, outputs, False))

            @block.gpsimd
            def _(pool):
                high, low = env["xT_h"], env["xT_l"]
                pool.tensor_copy(high[:, :, :], xnT[:, :, :]).then_inc(x_high, 1)
                pool.wait_ge(x_high, 1)
                pool.tensor_tensor(low[:, :, :], xnT[:, :, :], high[:, :, :], ALU.subtract)


def combine0(nc, env):
    sem, psum, ident, ident16 = (env[k] for k in ("sem", "psum", "ident", "ident16"))
    member, yT, w_slot, gate0, hT, w3T = (env[k] for k in ("member", "yT", "w_slot", "gate0", "shared_hT", "shared_wT"))
    IC = IS // P
    with ExitStack() as local:
        def tmp(name, shape, dt=F32):
            return local.enter_context(nc.sbuf_tensor("c0_" + name, shape, dt))
        yw_h, yw_l = tmp("yw_h", [P, ST, D], F16), tmp("yw_l", [P, ST, D], F16)
        turned = [tmp(f"turned{b}", [P, ST, P], F16) for b in range(2)]
        y_ready, yh_done, yl_done, m_ready, m_done, o_ready, o_done = (
            sem("c1_" + s) for s in ("y", "yh", "yl", "m", "md", "o", "od"))
        mcuts = [(0, 8), (8, ST - 8)]
        with nc.Block() as block:
            block.sync(env["head_weights"].load_first)
            block.gpsimd(env["head_weights"].split_first)

            @block.tensor
            def _(pe):
                def turn_members(n):
                    slots = member[:, n, :, :].rearrange("p e c -> p (e c)")
                    for k, (at, size) in enumerate(mcuts):
                        step = 2 * n + k
                        if step >= 2:
                            pe.wait_ge(m_done, step - 1)
                        for s in range(at, at + size):
                            out = psum[:, 2 + k, :].bitcast(F16)[:, (s - at) * P:(s - at + 1) * P]
                            last = pe.transpose(out, slots[:, s * P:(s + 1) * P], ident16[:, :])
                        last.then_inc(m_ready, 1)

                turn_members(0)
                for s in range(ST):
                    if s >= 2:
                        pe.wait_ge(yl_done, s - 1)
                    for c in range(DC):
                        last = pe.transpose(psum[:, s % 2, c * P:(c + 1) * P], yT[:, c, s * P:(s + 1) * P], ident[:, :])
                    last.then_inc(y_ready, 1)
                for n in range(NT):
                    if n + 1 < NT:
                        turn_members(n + 1)
                    pe.wait_ge(m_done, 2 * n + 2)
                    if n == 0:
                        pe.wait_ge(yl_done, ST)
                    if n >= 2:
                        pe.wait_ge(o_done, n - 1)
                    out = psum[:, 4 + n % 2, 0:D]
                    for s in range(ST):
                        pe.matmul(out, turned[n % 2][:, s, :], yw_h[:, s, :], start=(s == 0), stop=False)
                        pe.matmul(out, turned[n % 2][:, s, :], yw_l[:, s, :], start=False, stop=False)
                    for ic in range(IC):
                        last = pe.matmul(out, hT[:, ic, n * P:(n + 1) * P], w3T[2][:, ic, :],
                                         start=False, stop=(ic == IC - 1))
                    last.then_inc(o_ready, 1)

            @block.scalar
            def _(act):
                for n in range(NT):
                    for k, (at, size) in enumerate(mcuts):
                        act.wait_ge(m_ready, 2 * n + k + 1)
                        if n >= 2:
                            act.wait_ge(o_ready, n - 1)
                        act.copy(turned[n % 2][:, at:at + size, :].rearrange("p s x -> p (s x)").bitcast(F32),
                                 psum[:, 2 + k, 0:size * P // 2]).then_inc(m_done, 1)
                for n in range(NT):
                    act.wait_ge(o_done, n + 1)
                    act.activation(gate0[:, n, :], gate0[:, n, :], ACT.Silu)

            @block.vector
            def _(dve):
                for s in range(ST):
                    dve.wait_ge(y_ready, s + 1)
                    dve.tensor_scalar(yw_h[:, s, :], psum[:, s % 2, 0:D], w_slot[:, s:s + 1], None,
                                      ALU.mult).then_inc(yh_done, 1)
                    dve.wait_ge(yh_done, s + 1)
                    dve.scalar_tensor_tensor(yw_l[:, s, :], psum[:, s % 2, 0:D], w_slot[:, s:s + 1], yw_h[:, s, :],
                                             ALU.mult, ALU.subtract).then_inc(yl_done, 1)
                for n in range(NT):
                    dve.wait_ge(o_ready, n + 1)
                    dve.tensor_copy(gate0[:, n, :], psum[:, 4 + n % 2, 0:D]).then_inc(o_done, 1)


def mixture0(nc, env, w):
    with ExitStack() as local:
        def tmp(name, shape, dt=F32):
            return local.enter_context(nc.sbuf_tensor(name, shape, dt))
        env["fill_masks"] = mixture_masks(nc, env, tmp)
        env["member"] = tmp("member", [P, NT, E0, CAP], F16)
        env["wk_h"], env["wk_l"] = tmp("wk_h", [P, NT, E0], F16), tmp("wk_l", [P, NT, E0], F16)
        env["yT"] = tmp("yT", [P, DC, SLOTS])
        env["w_slot"] = tmp("w_slot", [P, ST])
        env["shared_weights"] = [w["L0_ffn_shared_" + k] for k in ("gate", "up", "down")]
        env["shared_wT"] = [tmp(f"shared_wT{i}", [P, 2, D]) for i in range(3)]
        env["shared_hT"] = tmp("shared_hT", [P, IS // P, T])
        xn_h, xn_l = tmp("xn_h", [P, NT, D], F16), tmp("xn_l", [P, NT, D], F16)
        env["xn_h"], env["xn_l"] = xn_h, xn_l
        with ExitStack() as experts:
            def part(name, shape, dt=F32):
                return experts.enter_context(nc.sbuf_tensor(name, shape, dt))
            env["xg_h"], env["xg_l"] = part("xg_h", [P, DC, SLOTS], F16), part("xg_l", [P, DC, SLOTS], F16)
            env["wf"] = [part(f"wf{b}", [P, 3 * DC, P]) for b in range(EB)]
            env["w_h"], env["w_l"] = ([part(f"w{x}{b}", [P, 3 * DC, P], F16) for b in range(EB)] for x in "hl")
            env["w_high"], env["w_ready"] = env["sem"]("e0_wh"), env["sem"]("e0_w")
            env["expert_loaded"] = [env["sem"](f"expert_loaded{b}") for b in range(EB)]
            env["expert_weights"] = [w["L0_ffn_" + k] for k in ("W_gate", "W_up", "W_down")]
            route0(nc, env, w["L0_ffn_router_w"], w["L0_ffn_e_bias"])
            experts0(nc, env)
        combine0(nc, env)


HQ = 4


def wo_pieces(env):
    halves = [env[k][:, :, :, :].rearrange("p n j d -> p (n j d)").rearrange("p (h e) -> p h e", e=D) for k in ("sq", "qk")]
    return [x[:, at:at + HQ, :] for x in halves for at in range(0, H // 2, HQ)]


class HeadWeights:

    def __init__(self, nc, env, w, tmp):
        sem = env["sem"]
        self.sources = [w["L0_attn_" + k].rearrange("(c p) h d -> p c h d", p=P) for k in ("wq", "wk", "wv")]
        self.wf = [tmp(f"a0_wf{b}", [P, DC, 3, HD], F32) for b in range(2)]
        self.w_h, self.w_l = ([tmp(f"a0_w{x}{b}", [P, DC, 3, HD], F16) for b in range(2)] for x in "hl")
        self.lifts = tmp("a0_lifts", [P, 2], F32)
        self.w_loaded = [sem(f"a0_wld{b}") for b in range(2)]
        self.lifts_ready, self.w_high, self.w_scaled, self.w_ready = (sem("a0_" + s) for s in ("li", "wh", "ws", "wr"))

    def load(self, sp, h, b):
        for j, src in enumerate(self.sources):
            sp.dma_start(self.wf[b][:, :, j, :], src[:, :, bass.ds(h, 1), :].rearrange("p c o d -> p c (o d)"))\
              .then_inc(self.w_loaded[b], 16)

    def split(self, pool, t, b, loads):
        pool.wait_ge(self.w_loaded[b], 48 * loads)
        lift = self.lifts[:, 0:1].to_broadcast([P, DC * 3 * HD])
        flat, high, low = (x[b][:, :, :, :].rearrange("p c j d -> p (c j d)") for x in (self.wf, self.w_h, self.w_l))
        pool.tensor_tensor(high, flat, lift, ALU.mult).then_inc(self.w_high, 1)
        pool.wait_ge(self.w_high, t + 1)
        pool.tensor_tensor(flat, flat, lift, ALU.mult).then_inc(self.w_scaled, 1)
        pool.wait_ge(self.w_scaled, t + 1)
        pool.tensor_tensor(low, flat, high, ALU.subtract).then_inc(self.w_ready, 1)

    def load_first(self, sp):
        for h in range(2):
            self.load(sp, h, h)

    def split_first(self, pool):
        pool.memset(self.lifts[:, 0:1], WSCALE).then_inc(self.lifts_ready, 1)
        pool.memset(self.lifts[:, 1:2], 1.0 / WSCALE).then_inc(self.lifts_ready, 1)
        pool.wait_ge(self.lifts_ready, 2)
        for h in range(2):
            self.split(pool, h, h, 1)


def attention0(nc, env, w):
    sem, psum, ident, ident16 = env["sem"], env["psum"], env["ident"], env["ident16"]
    xT_h, xT_l, oT_h, oT_l = (env[k] for k in ("xT_h", "xT_l", "oT_h", "oT_l"))
    SIDE = [("qk", 0), ("qk", 1), ("qk", 2), ("qk", 3), ("turn", 0), ("turn", 1), ("turn", 2),
            ("turn", 3), ("v", 0), ("v", 1)]
    PLAN = {0: ([0], [1]), 1: ([2], [3]), 2: ([], []), 3: ([], []), 4: ([4], [5, 6]), 5: ([7], [8, 9]),
            6: ([], []), 7: ([], [])}
    VALUES = {2: [(1, 0), (1, 1)], 3: [(1, 2), (1, 3)], 6: [(0, 0), (0, 1)], 7: [(0, 2), (0, 3)]}
    SQUARES = {1: 0, 2: 1}
    NS = len(SIDE)
    QK_LAST = SIDE.index(("qk", 3))
    TURN_LAST = SIDE.index(("turn", 3))
    V_LAST = SIDE.index(("v", 1))
    TURN_1 = SIDE.index(("turn", 1))
    QT = NT
    KT = NT
    PROB = 4096.0
    S_BANK, T_BANK, O_BANK, SIDE_BANKS = 0, 4, 6, (7, 6)
    with ExitStack() as local:
        def tmp(name, shape, dt=F32):
            return local.enter_context(nc.sbuf_tensor("a0_" + name, shape, dt))
        qk, sq = env["qk"], env["sq"]
        qkT_f = tmp("qkTf", [P, 2, T])
        v_f = tmp("vf", [P, NT, HD])
        ss, power, rnorm = tmp("ss", [P, NT * 2]), tmp("power", [P, NT * 2]), tmp("rnorm", [P, NT * 2])
        qkT_h = [tmp(f"qkTh{b}", [P, 2, T], F16) for b in range(2)]
        qkT_l = [tmp(f"qkTl{b}", [P, 2, T], F16) for b in range(2)]
        v_h = [tmp(f"vh{b}", [P, NT, HD], F16) for b in range(2)]
        v_l = [tmp(f"vl{b}", [P, NT, HD], F16) for b in range(2)]
        weights = env["head_weights"]
        w_h, w_l, lifts, w_ready = weights.w_h, weights.w_l, weights.lifts, weights.w_ready
        scales = tmp("scales", [P, 2])
        qk_scale = tmp("qk_scale", [P, 2])
        nmax, total, tsc, rtot = (tmp(n, [P, 2]) for n in ("nmax", "total", "tsc", "rtot"))
        ex = [tmp(f"ex{b}", [P, T]) for b in range(2)]
        pr = [tmp(f"pr{b}", [P, 2, T], F16) for b in range(2)]
        pT = [tmp(f"pT{b}", [P, 2, KT, HALF], F16) for b in range(2)]

        scale_loaded = [sem(f"a0_sld{b}") for b in range(2)]
        (scale_ready, side_ready, qkT_ready, side_free, sq_ready, ss_ready,
         var_ready, v_ready, part_high, pow_ready, r_ready, qkn_ready, s_ready, max_ready, exp_ready, tsc_ready, rt_ready, ph_ready,
         p_ready, t_ready, pT_ready, pv_ready, o_high, o_free) = (sem("a0_" + s) for s in (
             "sc", "sr", "kt", "sf", "sq", "ss", "vr", "vv", "hi", "pw", "rr", "qn", "s", "mx", "ex",
             "ts", "rt", "ph", "p", "t", "pT", "pv", "oh", "of"))

        def heads(engine, head):
            head(0, 0, True, False)
            with engine.Fori(0, (H - 2) // 2) as i:
                for b in range(2):
                    head(2 * i + 1 + b, (1 + b) % 2, False, False)
            head(H - 1, (H - 1) % 2, False, True)

        def sides(m, part, job, t):
            for s in PLAN[m][part]:
                job(t, s)

        with nc.Block() as block:
            @block.sync
            def _(sp):
                for i, name in enumerate(("L0_attn_q_scale", "L0_attn_k_scale")):
                    sp.dma_start(scales[:, i:i + 1], w[name].rearrange("(p a) -> p a", a=1)).then_inc(scale_loaded[i], 16)

                with sp.Fori(0, (H - 2) // 2) as i:
                    for b in range(2):
                        sp.wait_ge(w_ready, 2 * i + b + 1)
                        weights.load(sp, 2 * i + b + 2, b)
                wo = w["L0_attn_wo"].rearrange("h d e -> d h e")
                for q, dst in enumerate(wo_pieces(env)):
                    sp.wait_ge(ss_ready, 2 * H)
                    sp.wait_ge(side_ready, NS * (H - 1) + TURN_LAST + 1)
                    sp.dma_start(dst, wo[:, q * HQ:(q + 1) * HQ, :]).then_inc(env["wo_loaded"][q], 16)

            @block.gpsimd
            def _(pool):
                pool.memset(power[:, :], -0.5).then_inc(pow_ready, 1)
                pool.wait_ge(scale_loaded[0], 16)
                pool.wait_ge(scale_loaded[1], 16)
                pool.tensor_tensor(qk_scale[:, 0:1], scales[:, 0:1], scales[:, 1:2], ALU.mult).then_inc(scale_ready, 1)
                pool.memset(qk_scale[:, 1:2], 1.0).then_inc(scale_ready, 1)
                pool.wait_ge(pow_ready, 1)

                def split_weights(t, b, loads):
                    pool.wait_ge(side_ready, NS * (t - 2) + V_LAST + 1)
                    weights.split(pool, t, b, loads)

                def normalise(t):
                    pool.wait_ge(side_free, NS * t + QK_LAST + 1)
                    pool.wait_ge(var_ready, t + 1)
                    pool.tensor_tensor(rnorm[:, :], ss[:, :], power[:, :], ALU.pow).then_inc(r_ready, 1)
                    pool.wait_ge(r_ready, 2 * t + 1)
                    pool.tensor_tensor(rnorm[:, :], rnorm[:, :], lifts[:, 1:2].to_broadcast([P, NT * 2]),
                                       ALU.mult).then_inc(r_ready, 1)
                    pool.wait_ge(r_ready, 2 * t + 2)
                    flat = qk[:, :, :, :].rearrange("p n j d -> p (n j) d")
                    pool.tensor_tensor(flat, flat, bcast(rnorm[:, :], 2, HD), ALU.mult).then_inc(qkn_ready, 1)

                def low_parts(t, b):
                    kinds = [(i, kind, g) for i, (kind, g) in enumerate(SIDE) if kind != "qk"]
                    for k, (i, kind, g) in enumerate(kinds):
                        pool.wait_ge(side_free, NS * t + i + 1)
                        pool.wait_ge(part_high, len(kinds) * t + k + 1)
                        if kind == "turn":
                            at = (slice(None), g // 2, slice((g % 2) * HALF, (g % 2 + 1) * HALF))
                            whole, high, low = qkT_f[at], qkT_h[b][at], qkT_l[b][at]
                        else:
                            whole, high, low = (x[:, 4 * g:4 * g + 4, :].rearrange("p n d -> p (n d)")
                                                for x in (v_f, v_h[b], v_l[b]))
                        pool.tensor_tensor(low, whole, high, ALU.subtract).then_inc(qkT_ready if kind == "turn" else v_ready, 1)

                normalise(0)
                low_parts(0, 0)
                with pool.Fori(0, (H - 2) // 2) as i:
                    for b in range(2):
                        normalise(2 * i + b + 1)
                        low_parts(2 * i + b + 1, (b + 1) % 2)
                        split_weights(2 * i + b + 2, b, i + 2)
                normalise(H - 1)
                low_parts(H - 1, (H - 1) % 2)

            @block.tensor
            def _(pe):
                def side(t, s, b):
                    kind, g = SIDE[s]
                    later = not isinstance(t, int)
                    if later or t > 0 or s >= 2:
                        pe.wait_ge(side_free, NS * t + s - 1)
                    if s in (1, TURN_1) and (later or t >= 2):
                        pe.wait_ge(o_free, 2 * t - (3 if s == 1 else 2))
                    out = psum[:, SIDE_BANKS[s % 2], :]
                    if kind == "turn":
                        if g == 0:
                            pe.wait_ge(qkn_ready, t + 1)
                        for k in range(4):
                            last = pe.transpose(out[:, k * P:(k + 1) * P], qk[:, 4 * (g % 2) + k, g // 2, :], ident[:, :])
                    else:
                        if s == 0:
                            pe.wait_ge(w_ready, t + 1)
                        tiles, j0, j1 = (2, 0, 2) if kind == "qk" else (4, 2, 3)
                        cols = (j1 - j0) * HD
                        for k in range(tiles):
                            n = g * tiles + k
                            dst = out[:, k * cols:(k + 1) * cols]
                            for c in range(DC):
                                xh, xl = (x[:, c, n * P:(n + 1) * P] for x in (xT_h, xT_l))
                                wh, wl = (x[b][:, c, j0:j1, :].rearrange("p j d -> p (j d)") for x in (w_h, w_l))
                                pe.matmul(dst, xh, wh, start=(c == 0), stop=False)
                                pe.matmul(dst, xh, wl, start=False, stop=False)
                                last = pe.matmul(dst, xl, wh, start=False, stop=(c == DC - 1))
                    last.then_inc(side_ready, 1)

                def scores(t, m, b):
                    if m == 0:
                        pe.wait_ge(qkT_ready, 4 * t + 4)
                    if not (isinstance(t, int) and t == 0 and m < 2):
                        pe.wait_ge(exp_ready, QT * t + m - 1)
                    qh, ql = (x[b][:, 0, m * P:(m + 1) * P] for x in (qkT_h, qkT_l))
                    bank = S_BANK + 2 * (m % 2)
                    kh, kl = ([x[b][:, 1, f * HALF:(f + 1) * HALF] for f in range(2)] for x in (qkT_h, qkT_l))
                    for f in range(2):
                        pe.matmul(psum[:, bank + f, :], qh, kh[f], start=True, stop=False)
                    for f in range(2):
                        pe.matmul(psum[:, bank + f, :], qh, kl[f], start=False, stop=False)
                    for f in range(2):
                        last = pe.matmul(psum[:, bank + f, :], ql, kh[f], start=False, stop=True)
                    last.then_inc(s_ready, 1)

                def turn(t, m):
                    pe.wait_ge(p_ready, QT * t + m + 1)
                    if not (isinstance(t, int) and t == 0 and m == 0):
                        pe.wait_ge(pT_ready, QT * t + m)
                    for part in range(2):
                        for k in range(KT):
                            out = psum[:, T_BANK + part, :].bitcast(F16)[:, k * P:(k + 1) * P]
                            last = pe.transpose(out, pr[m % 2][:, part, k * P:(k + 1) * P], ident16[:, :])
                    last.then_inc(t_ready, 1)

                def values(t, g, piece, b, end):
                    if piece == 0:
                        pe.wait_ge(pT_ready, QT * t + 4 * g + 4)
                        pe.wait_ge(v_ready, 2 * t + 2)
                        if not end:
                            pe.wait_ge(side_free, NS * (t + 2) + QK_LAST + 1 if g else NS * (t + 1) + NS)
                        if not (isinstance(t, int) and t == 0 and g == 0):
                            pe.wait_ge(o_free, 2 * t + g)
                    out = psum[:, O_BANK, :]
                    for k in (2 * piece, 2 * piece + 1):
                        ph, pl = (pT[g][:, part, k, :] for part in range(2))
                        pe.matmul(out, v_h[b][:, k, :], ph, start=(k == 0), stop=False)
                        pe.matmul(out, v_h[b][:, k, :], pl, start=False, stop=False)
                        last = pe.matmul(out, v_l[b][:, k, :], ph, start=False, stop=(k == KT - 1))
                    if piece == 3:
                        last.then_inc(pv_ready, 1)

                def head(t, b, first, end):
                    nb = 1 - b
                    for m in range(QT):
                        if not end:
                            sides(m, 0, lambda u, s: side(u, s, nb), t + 1)
                        if m > 0:
                            turn(t, m - 1)
                        elif not first:
                            turn(t - 1, QT - 1)
                        if m < QT - 2:
                            scores(t, m + 2, b)
                        elif not end:
                            scores(t + 1, m + 2 - QT, nb)
                        if not end:
                            sides(m, 1, lambda u, s: side(u, s, nb), t + 1)
                        for g, piece in VALUES.get(m, []):
                            if g == 0:
                                values(t, g, piece, b, end)
                            elif not first:
                                values(t - 1, g, piece, nb, end)

                for s in range(NS):
                    side(0, s, 0)
                scores(0, 0, 0)
                scores(0, 1, 0)
                heads(pe, head)
                turn(H - 1, QT - 1)
                for piece in range(4):
                    values(H - 1, 1, piece, (H - 1) % 2, True)

            @block.scalar
            def _(act):
                def side(t, s, b):
                    kind, g = SIDE[s]
                    act.wait_ge(side_ready, NS * t + s + 1)
                    bank = psum[:, SIDE_BANKS[s % 2], :]
                    later = not isinstance(t, int)
                    if kind == "qk":
                        if s == 0 and (later or t > 0):
                            act.wait_ge(side_ready, NS * (t - 1) + TURN_LAST + 1)
                            act.wait_ge(ss_ready, 2 * t)
                        two = slice(2 * g, 2 * g + 2)
                        act.activation(sq[:, two, :, :].rearrange("p n j d -> p (n j d)"), bank, ACT.Square).then_inc(sq_ready, 1)
                        act.activation(qk[:, two, :, :].rearrange("p n j d -> p (n j d)"), bank,
                                       ACT.Copy).then_inc(side_free, 1)
                    elif kind == "turn":
                        j, at = g // 2, (g % 2) * HALF
                        if g == 0 and (later or t > 0):
                            act.wait_ge(qkT_ready, 4 * t)
                            if later or t >= 2:
                                act.wait_ge(s_ready, QT * (t - 1))
                        cols = slice(at, at + HALF)
                        for dst, signal in ((qkT_h[b], part_high), (qkT_f, side_free)):
                            act.activation(dst[:, j, cols], bank, ACT.Copy, scale=qk_scale[:, j:j + 1]).then_inc(signal, 1)
                    else:
                        if g == 0 and (later or t > 0):
                            act.wait_ge(v_ready, 2 * t)
                            if later or t >= 2:
                                act.wait_ge(pv_ready, 2 * t - 2)
                        for dst, signal in ((v_h[b], part_high), (v_f, side_free)):
                            act.activation(dst[:, 4 * g:4 * g + 4, :].rearrange("p n d -> p (n d)"), bank, ACT.Copy,
                                           scale=1.0 / WSCALE).then_inc(signal, 1)

                def exps(t, m):
                    act.wait_ge(max_ready, QT * t + m + 1)
                    if not (isinstance(t, int) and t == 0 and m < 2):
                        act.wait_ge(p_ready, QT * t + m - 1)
                    bank = S_BANK + 2 * (m % 2)
                    act.activation(ex[m % 2][:, :], psum[:, bank:bank + 2, :].rearrange("p a b -> p (a b)"), ACT.Exp,
                                   bias=nmax[:, m % 2:m % 2 + 1], accum_out=total[:, m % 2:m % 2 + 1]).then_inc(exp_ready, 1)

                def turned(t, m):
                    act.wait_ge(t_ready, QT * t + m + 1)
                    if m % 4 == 0 and (not isinstance(t, int) or t > 0):
                        act.wait_ge(pv_ready, 2 * (t - 1) + m // 4 + 1)
                    dst = pT[m // 4][:, :, :, (m % 4) * P:(m % 4 + 1) * P].bitcast(F32)
                    src = psum[:, T_BANK:T_BANK + 2, :].rearrange("p a (k q) -> p a k q", k=KT)
                    act.copy(dst, src).then_inc(pT_ready, 1)

                def outputs(t, g):
                    act.wait_ge(pv_ready, 2 * t + g + 1)
                    act.activation(oT_h[:, bass.ds(t, 1), g * HALF:(g + 1) * HALF],
                                   psum[:, O_BANK:O_BANK + 1, :], ACT.Copy, scale=1.0 / PROB).then_inc(o_high, 1)

                def head(t, b, first, end):
                    nb = 1 - b
                    for m in range(QT):
                        if not end:
                            sides(m, 0, lambda u, s: side(u, s, nb), t + 1)
                        if m > 0:
                            turned(t, m - 1)
                        elif not first:
                            turned(t - 1, QT - 1)
                        if m < QT - 1:
                            if m != 4:
                                exps(t, m + 1)
                        elif not end:
                            exps(t + 1, 0)
                        if not end:
                            sides(m, 1, lambda u, s: side(u, s, nb), t + 1)
                        if m == 3:
                            exps(t, 5)
                            if not first:
                                outputs(t - 1, 1)
                        if m == 7:
                            outputs(t, 0)

                act.wait_ge(scale_ready, 2)
                for s in range(NS):
                    side(0, s, 0)
                exps(0, 0)
                heads(act, head)
                turned(H - 1, QT - 1)
                outputs(H - 1, 1)

            @block.vector
            def _(dve):
                def squares(t, half):
                    dve.wait_ge(sq_ready, 4 * t + 2 * half + 2)
                    tiles = slice(half * NT // 2, (half + 1) * NT // 2)
                    dve.reduce_sum(ss[:, half * NT:(half + 1) * NT], sq[:, tiles, :, :].rearrange("p n j d -> p (n j) d"),
                                   AX.X).then_inc(ss_ready, 1)
                    if half == 1:
                        dve.wait_ge(ss_ready, 2 * t + 2)
                        dve.tensor_scalar(ss[:, :], ss[:, :], 1.0 / (HD * WSCALE * WSCALE), RMS_EPS0, ALU.mult,
                                          ALU.add).then_inc(var_ready, 1)

                def maxima(t, m):
                    dve.wait_ge(s_ready, QT * t + m + 1)
                    if not (isinstance(t, int) and t == 0 and m < 2):
                        dve.wait_ge(exp_ready, QT * t + m - 1)
                    bank = S_BANK + 2 * (m % 2)
                    dve.tensor_reduce(nmax[:, m % 2:m % 2 + 1], psum[:, bank:bank + 2, :].rearrange("p a b -> p (a b)"),
                                      AX.X, ALU.max, negate=True).then_inc(max_ready, 1)

                def split(t, m):
                    k = m % 2
                    dve.wait_ge(exp_ready, QT * t + m + 1)
                    dve.tensor_scalar(tsc[:, k:k + 1], total[:, k:k + 1], 1.0 / PROB, None, ALU.mult).then_inc(tsc_ready, 1)
                    dve.wait_ge(tsc_ready, QT * t + m + 1)
                    dve.reciprocal(rtot[:, k:k + 1], tsc[:, k:k + 1]).then_inc(rt_ready, 1)
                    dve.wait_ge(rt_ready, QT * t + m + 1)
                    if not (isinstance(t, int) and t == 0 and m < 2):
                        dve.wait_ge(t_ready, QT * t + m - 1)
                    dve.tensor_scalar(pr[k][:, 0, :], ex[k][:, :], rtot[:, k:k + 1], None, ALU.mult).then_inc(ph_ready, 1)
                    dve.wait_ge(ph_ready, QT * t + m + 1)
                    dve.scalar_tensor_tensor(pr[k][:, 1, :], ex[k][:, :], rtot[:, k:k + 1], pr[k][:, 0, :],
                                             ALU.mult, ALU.subtract).then_inc(p_ready, 1)

                def outputs(t, g):
                    dve.wait_ge(o_high, 2 * t + g + 1)
                    at = (slice(None), bass.ds(t, 1), slice(g * HALF, (g + 1) * HALF))
                    dve.scalar_tensor_tensor(oT_l[at], psum[:, O_BANK:O_BANK + 1, :], 1.0 / PROB, oT_h[at],
                                             ALU.mult, ALU.subtract).then_inc(o_free, 1)

                def head(t, b, first, end):
                    nb = 1 - b
                    for m in range(QT):
                        if m < QT - 1:
                            maxima(t, m + 1)
                        elif not end:
                            maxima(t + 1, 0)
                        if not end and m in SQUARES:
                            squares(t + 1, SQUARES[m])
                        if not first and m in (0, 4):
                            outputs(t - 1, m // 4)
                        split(t, m)

                squares(0, 0)
                squares(0, 1)
                maxima(0, 0)
                heads(dve, head)
                outputs(H - 1, 0)
                outputs(H - 1, 1)


def project0(nc, env):
    sem, psum = env["sem"], env["psum"]
    oT_h, oT_l, x, gate0 = (env[k] for k in ("oT_h", "oT_l", "x", "gate0"))
    with ExitStack() as local:
        def tmp(name, shape, dt=F32):
            return local.enter_context(nc.sbuf_tensor("p0_" + name, shape, dt))
        wf = wo_pieces(env)
        wo_h, wo_l = tmp("wo_h", [P, H, D], F16), tmp("wo_l", [P, H, D], F16)
        sg = [tmp(f"sg{b}", [P, D]) for b in range(2)]
        raw = tmp("raw", [P, NT, 6])
        loaded, stats_done = env["wo_loaded"], sem("p0_st")
        wh_ready, w_ready, y_ready, sg_ready, x_ready = (sem("p0_" + s) for s in ("wh", "w", "y", "sg", "x"))
        with nc.Block() as block:
            @block.scalar
            def _(act):
                for q in range(H // HQ):
                    act.wait_ge(loaded[q], 16)
                    act.activation(wo_h[:, q * HQ:(q + 1) * HQ, :], wf[q], ACT.Copy,
                                   scale=WSCALE).then_inc(wh_ready, 1)

            @block.vector
            def _(dve):
                for q in range(H // HQ):
                    dve.wait_ge(wh_ready, q + 1)
                    part = (slice(None), slice(q * HQ, (q + 1) * HQ))
                    dve.scalar_tensor_tensor(wo_l[part], wf[q], WSCALE, wo_h[part],
                                             ALU.mult, ALU.subtract).then_inc(w_ready, 1)
                for n in range(NT):
                    dve.wait_ge(y_ready, n + 1)
                    if n >= 2:
                        dve.wait_ge(x_ready, n - 1)
                    dve.scalar_tensor_tensor(sg[n % 2][:, :], psum[:, n, 0:D], 1.0 / WSCALE, gate0[:, n, :],
                                             ALU.mult, ALU.mult).then_inc(sg_ready, 1)
                    dve.wait_ge(sg_ready, n + 1)
                    dve.tensor_tensor(x[:, n, :], x[:, n, :], sg[n % 2][:, :], ALU.add).then_inc(x_ready, 1)
                    dve.wait_ge(x_ready, n + 1)
                    dve.bn_stats(raw[:, n, :], x[:, n, :]).then_inc(stats_done, 1)
                    dve.wait_ge(stats_done, n + 1)
                    dve.bn_aggr(env["x1_stats"][:, n, :], raw[:, n, :])

            @block.tensor
            def _(pe):
                for q in range(H // HQ):
                    pe.wait_ge(w_ready, q + 1)
                    for n in range(NT):
                        for h in range(q * HQ, (q + 1) * HQ):
                            oh, ol = (o[:, h, n * P:(n + 1) * P] for o in (oT_h, oT_l))
                            pe.matmul(psum[:, n, 0:D], oh, wo_h[:, h, :], start=(h == 0), stop=False)
                            pe.matmul(psum[:, n, 0:D], oh, wo_l[:, h, :], start=False, stop=False)
                            last = pe.matmul(psum[:, n, 0:D], ol, wo_h[:, h, :], start=False, stop=(h == H - 1))
                        if q == H // HQ - 1:
                            last.then_inc(y_ready, 1)


class Router1:

    def __init__(self, nc, env, w, local, combT):
        def tmp(name, shape, dt=F32):
            return local.enter_context(nc.sbuf_tensor("r1_" + name, shape, dt))
        sem, self.psum, self.ident, self.xnT, self.comb_dram = (env[k] for k in ("sem", "psum", "ident", "xnT", "comb_dram"))
        self.router_w, self.router_bias = w["L1_ffn_router_w"], w["L1_ffn_router_bias"]
        self.rw, self.bias = tmp("rw", [P, DC, E1]), tmp("bias", [P, E1])
        self.es, self.er, self.sel = tmp("es", [P, NT, E1 + 8]), tmp("er", [P, NT, E1 + 8]), tmp("sel", [P, NT, E1])
        self.best, self.named = tmp("best", [P, NT, 8]), tmp("named", [P, NT, 8])
        self.shifted, self.prob, self.comb = (tmp(n, [P, NT, E1]) for n in ("shifted", "prob", "comb"))
        self.top, self.total = tmp("top", [P, NT]), tmp("total", [P, NT])
        self.combT = combT
        self.loaded = [sem(f"r1_ld{i}") for i in range(2)]
        self.logits_ready, self.dve_done, self.exp_ready, self.comb_ready, self.t_ready, self.ct_ready, self.stored = (
            sem("r1_" + s) for s in ("lg", "d", "ex", "cb", "t", "ct", "st"))
        self.logits = self.psum[:, 6, :].rearrange("p (n e) -> p n e", n=NT)

    def load(self, sp):
        sp.dma_start(self.rw[:, :, :], self.router_w.rearrange("(p c) e -> p c e", p=P)).then_inc(self.loaded[0], 16)
        sp.dma_start(self.bias[:, :], self.router_bias.partition_broadcast(P)).then_inc(self.loaded[1], 16)

    def store(self, sp):
        sp.wait_ge(self.ct_ready, 1)
        sp.dma_start(self.comb_dram, self.combT[:, :]).then_inc(self.stored, 16)

    def wait_stored(self, sp):
        sp.wait_ge(self.stored, 16)

    def make_logits(self, pe):
        pe.wait_ge(self.loaded[0], 16)
        for n in range(NT):
            for c in range(DC):
                last = pe.matmul(self.logits[:, n, :], self.xnT[:, c, n * P:(n + 1) * P], self.rw[:, c, :],
                                 start=(c == 0), stop=(c == DC - 1))
        last.then_inc(self.logits_ready, 1)

    def wait_logits_used(self, pe):
        pe.wait_ge(self.dve_done, 4)

    def turn(self, pe):
        pe.wait_ge(self.comb_ready, 1)
        for n in range(NT):
            last = pe.transpose(self.psum[0:E1, 6 + n // 4, (n % 4) * P:(n % 4 + 1) * P], self.comb[:, n, :], self.ident[:, :])
        last.then_inc(self.t_ready, 1)

    def exponentials(self, act):
        act.wait_ge(self.dve_done, 2)
        act.activation(self.prob[:, :, :], self.shifted[:, :, :], ACT.Exp).then_inc(self.exp_ready, 1)

    def turned(self, act):
        act.wait_ge(self.t_ready, 1)
        act.activation(self.combT[:, :], self.psum[0:E1, 6:8, :].rearrange("p a b -> p (a b)"), ACT.Copy).then_inc(self.ct_ready, 1)

    def choose(self, dve):
        chain = Chain(dve, self.dve_done)
        es, er, sel, best, named, shifted, prob, comb = (
            x[:, :, :] for x in (self.es, self.er, self.sel, self.best, self.named, self.shifted, self.prob, self.comb))
        top, total = self.top[:, :], self.total[:, :]
        dve.wait_ge(self.logits_ready, 1)
        dve.wait_ge(self.loaded[1], 16)
        chain(dve.reduce_max(top, self.logits, AX.X))
        chain(dve.tensor_tensor(shifted, self.logits, bcast(top, 2, E1), ALU.subtract))
        chain(dve.memset(es, SENTINEL))
        chain(dve.tensor_tensor(es[:, :, 0:E1], self.logits, bcast(self.bias[:, :], 1, NT), ALU.add))
        top_k_mask(dve, chain, es, K1, best, named, er, sel)
        dve.wait_ge(self.exp_ready, 1)
        chain(dve.reduce_sum(total, prob, AX.X))
        chain(dve.reciprocal(total, total))
        chain(dve.tensor_tensor(prob, prob, bcast(total, 2, E1), ALU.mult))
        chain(dve.tensor_tensor(prob, prob, sel, ALU.mult))
        chain(dve.reduce_sum(total, prob, AX.X))
        chain(dve.reciprocal(total, total))
        dve.tensor_tensor(comb, prob, bcast(total, 2, E1), ALU.mult).then_inc(self.comb_ready, 1)


class Shared1:
    QUARTERS = SH1 // P

    def __init__(self, nc, env, w, keep):
        sem = env["sem"]
        self.psum, self.xT_h, self.xT_l = env["psum"], env["xT_h"], env["xT_l"]
        self.sources = [w["L1_ffn_" + k] for k in ("swg", "swu", "swd")]
        Q = range(self.QUARTERS)
        self.gu_h, self.gu_l = ([keep(f"s1_gu{x}{q}", [P, 2 * DC, P], F16) for q in Q] for x in "hl")
        self.dn_h, self.dn_l, self.h_h, self.h_l = env["shared_parts"]
        self.loaded = [sem(f"s1_ld{q}") for q in Q]
        (self.high_ready, self.gu_ready, self.silu_done, self.up_done, self.h_ready, self.hh_ready, self.hl_ready) = (
            sem("s1_" + s) for s in ("wh", "gu", "si", "up", "h", "hh", "hl"))

    def staging(self, tmp):
        self.wf = [tmp(f"s1_wf{q}", [P, 3 * DC, P]) for q in range(self.QUARTERS)]

    def work_buffers(self, tmp):
        self.sg, self.up, self.hf = ([tmp(f"s1_{n}{b}", [P, HALF]) for b in range(2)] for n in ("sg", "up", "hf"))

    def load(self, sp):
        swg, swu, swd = self.sources
        for q in range(self.QUARTERS):
            e, at = q // 2, (q % 2) * P
            for j, src in enumerate((swg, swu)):
                sp.dma_start(self.wf[q][:, DC * j:DC * (j + 1), :], src[e, :, at:at + P].rearrange("(p c) f -> p c f", p=P))\
                  .then_inc(self.loaded[q], 16)
            sp.dma_start(self.wf[q][:, 2 * DC:, :].rearrange("p c d -> p (c d)"), swd[e, at:at + P, :]).then_inc(self.loaded[q], 16)

    def parts(self, q):
        return ((self.wf[q][:, 0:2 * DC, :], self.gu_h[q][:, :, :], self.gu_l[q][:, :, :]),
                (self.wf[q][:, 2 * DC:, :], self.dn_h[q][:, :, :], self.dn_l[q][:, :, :]))

    def weights_high(self, act, q):
        act.wait_ge(self.loaded[q], 48)
        for whole, high, _ in self.parts(q):
            act.activation(high, whole, ACT.Copy, scale=WSCALE).then_inc(self.high_ready, 1)

    def weights_low(self, dve, q):
        dve.wait_ge(self.high_ready, 2 * q + 2)
        for whole, high, low in self.parts(q):
            dve.scalar_tensor_tensor(low, whole, WSCALE, high, ALU.mult, ALU.subtract)

    def gate_up(self, pe, k):
        q, half = k // 2, k % 2
        if k >= 2:
            pe.wait_ge(self.up_done, k - 1)
        cols = slice(half * HALF, (half + 1) * HALF)
        for j in range(2):
            out = self.psum[:, 4 + 2 * half + j, :]
            for c in range(DC):
                wh, wl = self.gu_h[q][:, DC * j + c, :], self.gu_l[q][:, DC * j + c, :]
                pe.matmul(out, wh, self.xT_h[:, c, cols], start=(c == 0), stop=False)
                pe.matmul(out, wh, self.xT_l[:, c, cols], start=False, stop=False)
                last = pe.matmul(out, wl, self.xT_h[:, c, cols], start=False, stop=(c == DC - 1))
        last.then_inc(self.gu_ready, 1)

    def silu(self, act, k):
        half = k % 2
        act.wait_ge(self.gu_ready, k + 1)
        if k >= 2:
            act.wait_ge(self.h_ready, k - 1)
        act.activation(self.sg[half][:, :], self.psum[:, 4 + 2 * half, :], ACT.Silu, scale=1.0 / WSCALE).then_inc(self.silu_done, 1)
        act.activation(self.up[half][:, :], self.psum[:, 5 + 2 * half, :], ACT.Copy, scale=1.0 / WSCALE).then_inc(self.up_done, 1)

    def hidden(self, pool, k):
        pool.wait_ge(self.silu_done, k + 1)
        pool.wait_ge(self.up_done, k + 1)
        if k >= 2:
            pool.wait_ge(self.hl_ready, k - 1)
        pool.tensor_tensor(self.hf[k % 2][:, :], self.sg[k % 2][:, :], self.up[k % 2][:, :], ALU.mult).then_inc(self.h_ready, 1)

    def high(self, act, k):
        act.wait_ge(self.h_ready, k + 1)
        act.activation(self.h_h[k][:, :], self.hf[k % 2][:, :], ACT.Copy).then_inc(self.hh_ready, 1)

    def low(self, pool, k):
        pool.wait_ge(self.hh_ready, k + 1)
        pool.tensor_tensor(self.h_l[k][:, :], self.hf[k % 2][:, :], self.h_h[k][:, :], ALU.subtract).then_inc(self.hl_ready, 1)


def gated_linear_attention(nc, env, w):
    sem, psum, ident = env["sem"], env["psum"], env["ident"]
    xn, s1 = env["xn"], env["s1"]
    KD = GH * GK
    G1 = 16
    FT = -(-HID // P)
    with ExitStack() as outer:
        def keep(name, shape, dt=F32):
            return outer.enter_context(nc.sbuf_tensor("g1_" + name, shape, dt))
        fill_head_masks = head_masks(nc, env, keep)
        spread, gather_h = env["spread"], env["gather_h"]
        ln = keep("ln", [P, 2, DC])
        ms, inv, sq = keep("ms", [P, NT]), keep("inv", [P, NT]), keep("sq", [P, D])
        silu_g = keep("silu_g", [P, NT, D])
        o = keep("o", [P, NT, D])
        ln_loaded = [sem(f"g1_lnl{i}") for i in range(2)]
        shared = Shared1(nc, env, w, keep)
        wo = keep("wo", [P, DC, D])
        REST = HID - (FT - 1) * P
        mlp_h = [keep(n, [P, DC, HID], F16) for n in ("w1h", "w3h")] + [keep("w2h", [P, FT, D], F16)]
        mlp_l = [keep(n, [P, DC, HID], F16) for n in ("w1l", "w3l")] + [keep("w2l", [P, FT, D], F16)]
        mlp_high = sem("m1_wh")
        wo_loaded, mlp_loaded = sem("g4_wl"), [sem(f"m1_l{i}") for i in range(4)]

        squares_done = [sem(f"g1_ss{i}") for i in range(2)]

        def square(act, source, which, n):
            if n:
                act.wait_ge(squares_done[which], n)
            act.activation(sq[:, :], source[:, n, :], ACT.Square, accum_out=ms[:, n:n + 1]).then_inc(squares_done[which], 1)

        def rms_turned(tag, source, which, xT, xT_low=None, loads=None):
            ms_done, rt_done, inv_done, xr_ready, t_ready, evac, low_done = (
                sem(tag + s) for s in ("ms", "rt", "iv", "xr", "t", "e", "lo"))
            with ExitStack() as inner:
                xr = inner.enter_context(nc.sbuf_tensor(tag + "_xr", [P, NT, D], F32))
                with nc.Block() as block:
                    if loads:
                        block.sync(loads)

                    @block.vector
                    def _(dve):
                        dve.tensor_scalar(ms[:, :], ms[:, :], 1.0 / D, RMS_EPS1, ALU.mult, ALU.add).then_inc(ms_done, 1)
                        dve.wait_ge(rt_done, 1)
                        dve.reciprocal(inv[:, :], inv[:, :]).then_inc(inv_done, 1)
                        dve.wait_ge(inv_done, 1)
                        for n in range(NT):
                            dve.tensor_scalar(xr[:, n, :], source[:, n, :], inv[:, n:n + 1], None, ALU.mult).then_inc(xr_ready, 1)
                        if xT_low is not None:
                            for n in range(NT):
                                dve.wait_ge(evac, n + 1)
                                for c in range(DC):
                                    at = (slice(None), c, slice(n * P, (n + 1) * P))
                                    last = dve.scalar_tensor_tensor(xT_low[at], psum[:, n % 2, c * P:(c + 1) * P],
                                                                    ln[:, which, c:c + 1], xT[at], ALU.mult, ALU.subtract)
                                last.then_inc(low_done, 1)

                    @block.scalar
                    def _(act):
                        act.wait_ge(ms_done, 1)
                        act.activation(inv[:, :], ms[:, :], ACT.Sqrt).then_inc(rt_done, 1)
                        act.wait_ge(ln_loaded[which], 16)
                        for n in range(NT):
                            act.wait_ge(t_ready, n + 1)
                            for c in range(DC):
                                last = act.activation(xT[:, c, n * P:(n + 1) * P], psum[:, n % 2, c * P:(c + 1) * P],
                                                      ACT.Copy, scale=ln[:, which, c:c + 1])
                            last.then_inc(evac, 1)

                    @block.tensor
                    def _(pe):
                        for n in range(NT):
                            pe.wait_ge(xr_ready, n + 1)
                            if n >= 2:
                                pe.wait_ge(evac if xT_low is None else low_done, n - 1)
                            for c in range(DC):
                                last = pe.transpose(psum[:, n % 2, c * P:(c + 1) * P], xr[:, n, c * P:(c + 1) * P], ident[:, :])
                            last.then_inc(t_ready, 1)

        with ExitStack() as local:
            def tmp(name, shape, dt=F32):
                return local.enter_context(nc.sbuf_tensor("g1_" + name, shape, dt))
            qT, kT, dec = tmp("qT", [P, T]), tmp("kT", [P, T]), tmp("dec", [P, T])
            v_h, v_l = tmp("v_h", [P, 2, T], F16), tmp("v_l", [P, 2, T], F16)
            oT = tmp("oT", [P, 2, T])
            combT = tmp("combT", [E1, T])
            projections = ExitStack()

            def ptmp(name, shape, dt=F32):
                return projections.enter_context(nc.sbuf_tensor("g1_" + name, shape, dt))
            xT = ptmp("xT", [P, DC, T])
            wq, wk = ptmp("wq", [P, DC, KD]), ptmp("wk", [P, DC, KD])
            wg1, wg2, bg2 = ptmp("wg1", [P, DC, G1]), ptmp("wg2", [G1, KD]), ptmp("bg2", [P, 1])
            wv, wg, bg = ptmp("wv", [P, DC, D]), ptmp("wg", [P, DC, D]), ptmp("bg", [P, D])
            wv_dh = ptmp("wv_dh", [P, DC, D])
            wv_ready = sem("g1_wv")
            loads = [(wq, w["L1_attn_Wq"]), (wk, w["L1_attn_Wk"]), (wg1, w["L1_attn_Wkg1"]), (wv, w["L1_attn_Wv"]),
                     (wg, w["L1_attn_Wg"])]
            w_loaded = [sem(f"g1_wl{i}") for i in range(len(loads) + 3)]
            router = Router1(nc, env, w, projections, combT)
            def load_first(sp):
                for i, name in enumerate(("L1_attn_ln1_w", "L1_attn_ln2_w")):
                    sp.dma_start(ln[:, i, :], w[name].rearrange("(c p) -> p c", p=P), allow_slow_non_contiguous=True).then_inc(ln_loaded[i], 16)
                for i, (dst, src) in enumerate(loads):
                    sp.dma_start(dst[:, :, :], src.rearrange("(c p) n -> p c n", p=P)).then_inc(w_loaded[i], 16)
                router.load(sp)
                sp.dma_start(wg2[:, :], w["L1_attn_Wkg2"]).then_inc(w_loaded[5], 16)
                sp.dma_start(bg2[:, :], w["L1_attn_bkg2"].rearrange("(p a) -> p a", a=1)).then_inc(w_loaded[6], 16)
                sp.dma_start(bg[:, :], w["L1_attn_bg"].partition_broadcast(P)).then_inc(w_loaded[7], 16)

            def load_rest(sp):
                sp.dma_start(wo[:, :, :], w["L1_attn_Wo"].rearrange("(c p) n -> p c n", p=P)).then_inc(wo_loaded, 16)

            layer_norm(nc, env, "ln1", env["x"], xn, env["xnT"], interleaved=True, loads=load_first, stats=env["x1_stats"],
                       squares=lambda act, n: square(act, xn, 0, n))
            rms_turned("g1_r1", xn, 0, xT, loads=load_rest)

            mid = ptmp("mid", [G1, T])
            z, e = ptmp("z", [P, T]), ptmp("e", [P, T])
            q_ready, mid_ready, mid_done, z_ready, v_ready, g_ready = (sem("g1_" + s) for s in ("q", "m", "md", "z", "v", "g"))
            qk_done, act_done, dve_done, vh_done, g_added, v_free, x_high = (sem("g1_" + s) for s in ("qd", "ad", "dd", "vh", "ga", "vf", "xh"))

            def both(pe, banks, lhs, rhs_of, rows=P):
                for half in range(2):
                    for c in range(DC):
                        last = pe.matmul(psum[0:rows, banks + half, :], lhs(c), rhs_of(c, half),
                                         start=(c == 0), stop=(c == DC - 1))
                return last

            with nc.Block() as block:
                @block.sync
                def _(sp):
                    router.store(sp)

                @block.tensor
                def _(pe):
                    router.make_logits(pe)
                    for i in range(len(loads) + 1):
                        pe.wait_ge(w_loaded[i], 16)

                    def x_of(c, half):
                        return xT[:, c, half * HALF:(half + 1) * HALF]
                    both(pe, 0, lambda c: wg1[:, c, :], x_of, G1).then_inc(mid_ready, 1)
                    both(pe, 2, lambda c: wq[:, c, :], x_of).then_inc(q_ready, 1)
                    both(pe, 4, lambda c: wk[:, c, :], x_of).then_inc(q_ready, 1)
                    pe.wait_ge(mid_done, 1)
                    router.wait_logits_used(pe)
                    for half in range(2):
                        last = pe.matmul(psum[:, 6 + half, :], wg2[:, :], mid[:, half * HALF:(half + 1) * HALF],
                                         start=True, stop=True)
                    last.then_inc(z_ready, 1)
                    pe.wait_ge(qk_done, 1)
                    pe.wait_ge(wv_ready, DC)
                    for cv in range(2):
                        both(pe, 2 * cv, lambda c: wv_dh[:, c, cv * P:(cv + 1) * P], x_of).then_inc(v_ready, 1)
                    for n in range(NT):
                        if n == 0:
                            pe.wait_ge(qk_done, 2)
                        if n >= 2:
                            pe.wait_ge(g_added, n - 1)
                        for c in range(DC):
                            last = pe.matmul(psum[:, 4 + n % 2, 0:D], xT[:, c, n * P:(n + 1) * P], wg[:, c, :],
                                             start=(c == 0), stop=(c == DC - 1))
                        last.then_inc(g_ready, 1)
                    pe.wait_ge(act_done, 1)
                    router.turn(pe)

                @block.gpsimd
                def _(pool):
                    pool.wait_ge(w_loaded[3], 16)
                    for c in range(DC):
                        pool.tensor_copy(wv_dh[:, c, :].rearrange("p (c d h) -> p c d h", c=2, d=8),
                                         wv[:, c, :].rearrange("p (h c d) -> p c d h", c=2, d=8)).then_inc(wv_ready, 1)
                    fill_head_masks(pool)
                    xnT, high, low = env["xnT"], env["xT_h"], env["xT_l"]
                    pool.tensor_copy(high[:, :, :], xnT[:, :, :]).then_inc(x_high, 1)
                    pool.wait_ge(x_high, 1)
                    pool.tensor_tensor(low[:, :, :], xnT[:, :, :], high[:, :, :], ALU.subtract)

                def two(bank):
                    return psum[:, bank:bank + 2, :].rearrange("p a b -> p (a b)")

                @block.scalar
                def _(act):
                    chain = Chain(act, act_done)
                    act.wait_ge(mid_ready, 1)
                    act.activation(mid[:, :], psum[0:G1, 0:2, :].rearrange("p a b -> p (a b)"), ACT.Copy).then_inc(mid_done, 1)
                    act.wait_ge(q_ready, 1)
                    act.activation(qT[:, :], two(2), ACT.Copy).then_inc(qk_done, 1)
                    act.wait_ge(q_ready, 2)
                    act.activation(kT[:, :], two(4), ACT.Copy, scale=float(GV) ** -0.5).then_inc(qk_done, 1)
                    router.exponentials(act)
                    act.wait_ge(z_ready, 1)
                    act.wait_ge(w_loaded[6], 16)
                    chain(act.activation(z[:, :], two(6), ACT.Identity, bias=bg2[:, 0:1]))
                    chain(act.activation(e[:, :], z[:, :], ACT.Abs))
                    chain(act.activation(e[:, :], e[:, :], ACT.Exp, scale=-1.0))
                    chain(act.activation(e[:, :], e[:, :], ACT.Ln, bias=1.0))
                    act.wait_ge(dve_done, 1)
                    chain(act.activation(dec[:, :], z[:, :], ACT.Exp, scale=1.0 / GATE_NORM))
                    for cv in range(2):
                        act.wait_ge(v_ready, cv + 1)
                        act.activation(v_h[:, cv, :], two(2 * cv), ACT.Copy).then_inc(vh_done, 1)
                    router.turned(act)

                @block.vector
                def _(dve):
                    router.choose(dve)
                    dve.wait_ge(act_done, 4)
                    dve.scalar_tensor_tensor(z[:, :], z[:, :], 0.0, e[:, :], ALU.min, ALU.subtract).then_inc(dve_done, 1)
                    dve.wait_ge(w_loaded[7], 16)
                    for n in range(NT):
                        dve.wait_ge(g_ready, n + 1)
                        dve.tensor_tensor(silu_g[:, n, :], psum[:, 4 + n % 2, 0:D], bg[:, :], ALU.add).then_inc(g_added, 1)
                    for cv in range(2):
                        dve.wait_ge(vh_done, cv + 1)
                        dve.tensor_tensor(v_l[:, cv, :], two(2 * cv), v_h[:, cv, :], ALU.subtract).then_inc(v_free, 1)
            projections.close()

            w1, w3, w2 = tmp("w1", [P, DC, HID]), tmp("w3", [P, DC, HID]), tmp("w2", [P, FT, D])
            mlp_parts = [(f[at], high[at], low[at]) for f, high, low, at in zip(
                (w1, w3, w2, w2), (*mlp_h, mlp_h[2]), (*mlp_l, mlp_l[2]),
                ((slice(None),) * 3, (slice(None),) * 3, (slice(None), slice(0, FT - 1)), (slice(0, REST), FT - 1)))]
            recurrence = ExitStack()

            def rtmp(name, shape, dt=F32):
                return recurrence.enter_context(nc.sbuf_tensor("g2_" + name, shape, dt))
            kv, state, qs = ([rtmp(f"{n}{b}", [P, T]) for b in range(2)] for n in ("kv", "state", "qs"))
            shared.staging(rtmp)
            v_spread, kv_ready, st_ready, qs_ready, o_step = (sem("g2_" + s) for s in ("v", "kv", "st", "qs", "o"))
            oT_done = sem("g2_oT")
            STEPS = 2 * GK
            LOW_AFTER = {8 + q: q for q in range(shared.QUARTERS)}
            with nc.Block() as block:
                @block.sync
                def _(sp):
                    for i, (dst, src) in enumerate(((w1, w["L1_attn_W1"]), (w3, w["L1_attn_W3"]))):
                        sp.dma_start(dst[:, :, :], src.rearrange("(c p) n -> p c n", p=P)).then_inc(mlp_loaded[i], 16)
                    w2_src = w["L1_attn_W2"]
                    sp.dma_start(w2[:, 0:FT - 1, :], w2_src[0:(FT - 1) * P, :].rearrange("(f p) n -> p f n", p=P))\
                      .then_inc(mlp_loaded[2], 16)
                    sp.dma_start(w2[0:REST, FT - 1, :], w2_src[(FT - 1) * P:HID, :]).then_inc(mlp_loaded[3], 16)
                    shared.load(sp)
                    router.wait_stored(sp)

                @block.tensor
                def _(pe):
                    def spread_values(s):
                        cv, dd = s // 8, s % 8
                        if s >= 2:
                            pe.wait_ge(kv_ready, s - 1)
                        for half in range(2):
                            cols = slice(half * HALF, (half + 1) * HALF)
                            pe.matmul(psum[:, 2 * (s % 2) + half, :], spread[:, dd, :], v_h[:, cv, cols], start=True, stop=False)
                            last = pe.matmul(psum[:, 2 * (s % 2) + half, :], spread[:, dd, :], v_l[:, cv, cols],
                                             start=False, stop=True)
                        last.then_inc(v_spread, 1)

                    spread_values(0)
                    spread_values(1)
                    for s in range(STEPS):
                        if s + 2 < STEPS:
                            spread_values(s + 2)
                        cv, dd = s // 8, s % 8
                        pe.wait_ge(qs_ready, s + 1)
                        for half in range(2):
                            last = pe.matmul(psum[:, 4 + 2 * cv + half, :], gather_h[:, dd, :],
                                             qs[s % 2][:, half * HALF:(half + 1) * HALF], start=(dd == 0), stop=(dd == 7))
                        last.then_inc(o_step, 1)

                @block.vector
                def _(dve):
                    for s in range(STEPS):
                        dve.wait_ge(v_spread, s + 1)
                        if s >= 2:
                            dve.wait_ge(st_ready, s - 1)
                        dve.tensor_tensor(kv[s % 2][:, :], kT[:, :], psum[:, 2 * (s % 2):2 * (s % 2) + 2, :].rearrange("p a b -> p (a b)"),
                                          ALU.mult).then_inc(kv_ready, 1)
                        dve.wait_ge(kv_ready, s + 1)
                        if s >= 2:
                            dve.wait_ge(qs_ready, s - 1)
                        dve.tensor_tensor_scan(state[s % 2][:, :], dec[:, :], kv[s % 2][:, :], 0.0, ALU.mult,
                                               ALU.add).then_inc(st_ready, 1)
                        if s in LOW_AFTER:
                            shared.weights_low(dve, LOW_AFTER[s])

                @block.gpsimd
                def _(pool):
                    for s in range(STEPS):
                        pool.wait_ge(st_ready, s + 1)
                        if s >= 2:
                            pool.wait_ge(o_step, s - 1)
                        pool.tensor_tensor(qs[s % 2][:, :], qT[:, :], state[s % 2][:, :], ALU.mult).then_inc(qs_ready, 1)

                @block.scalar
                def _(act):
                    act.activation(silu_g[:, :, :], silu_g[:, :, :], ACT.Silu)
                    for i, (whole, high, low) in enumerate(mlp_parts):
                        act.wait_ge(mlp_loaded[i], 16)
                        act.activation(high, whole, ACT.Copy, scale=WSCALE).then_inc(mlp_high, 1)
                    for q in range(shared.QUARTERS):
                        shared.weights_high(act, q)
                    for cv in range(2):
                        act.wait_ge(o_step, 8 * (cv + 1))
                        act.activation(oT[:, cv, :], psum[:, 4 + 2 * cv:6 + 2 * cv, :].rearrange("p a b -> p (a b)"),
                                       ACT.Copy).then_inc(oT_done, 1)

            recurrence.close()

            t3_ready, o_done = sem("g3_t"), sem("g3_o")
            shared.work_buffers(tmp)
            mean, var, std = (tmp("g4_" + n, [P, NT * GH]) for n in ("mean", "var", "std"))
            big = tmp("g4_big", [P, NT * GH, GV])
            ogT = tmp("g4_ogT", [P, DC, T])
            dve_done, sq_done, rt_done, og_ready, t_ready, evac, y_ready, s_done = (
                sem("g4_" + s) for s in ("d", "sq", "rt", "og", "t", "e", "y", "s"))
            oh = o[:, :, :].rearrange("p n (h d) -> p (n h) d", h=GH)
            HALVES = 2 * shared.QUARTERS
            EARLY = HALVES - 2
            with nc.Block() as block:
                @block.vector
                def _(dve):
                    for i, (whole, high, low) in enumerate(mlp_parts):
                        dve.wait_ge(mlp_high, i + 1)
                        dve.scalar_tensor_tensor(low, whole, WSCALE, high, ALU.mult, ALU.subtract)
                    chain = Chain(dve, dve_done)
                    dve.wait_ge(o_done, NT)
                    chain(dve.reduce_sum(mean[:, :], oh, AX.X))
                    chain(dve.tensor_scalar(mean[:, :], mean[:, :], 1.0 / GV, None, ALU.mult))
                    chain(dve.tensor_tensor(oh, oh, bcast(mean[:, :], 2, GV), ALU.subtract))
                    dve.wait_ge(sq_done, 1)
                    chain(dve.reduce_sum(var[:, :], big[:, :, :], AX.X))
                    chain(dve.tensor_scalar(var[:, :], var[:, :], 1.0 / GV, RMS_EPS1, ALU.mult, ALU.add))
                    dve.wait_ge(rt_done, 1)
                    chain(dve.reciprocal(std[:, :], std[:, :]))
                    chain(dve.tensor_tensor(oh, oh, bcast(std[:, :], 2, GV), ALU.mult))
                    dve.tensor_tensor(o[:, :, :], o[:, :, :], silu_g[:, :, :], ALU.mult).then_inc(og_ready, 1)
                    for n in range(NT):
                        dve.wait_ge(y_ready, n + 1)
                        dve.tensor_tensor(s1[:, n, :], psum[:, 2 + n % 2, 0:D], xn[:, n, :], ALU.add).then_inc(s_done, 1)

                @block.gpsimd
                def _(pool):
                    shared.hidden(pool, 0)
                    for k in range(1, HALVES):
                        shared.hidden(pool, k)
                        shared.low(pool, k - 1)
                    shared.low(pool, HALVES - 1)

                @block.scalar
                def _(act):
                    for n in range(NT):
                        act.wait_ge(t3_ready, n + 1)
                        act.activation(o[:, n, :].rearrange("p (h c d) -> p c d h", c=2, d=8),
                                       psum[:, n % 2, 0:D].rearrange("p (c d h) -> p c d h", c=2, d=8), ACT.Copy).then_inc(o_done, 1)
                    shared.silu(act, 0)
                    shared.silu(act, 1)
                    shared.high(act, 0)
                    act.wait_ge(dve_done, 3)
                    act.activation(big[:, :, :], oh, ACT.Square).then_inc(sq_done, 1)
                    shared.silu(act, 2)
                    shared.high(act, 1)
                    act.wait_ge(dve_done, 5)
                    act.activation(std[:, :], var[:, :], ACT.Sqrt).then_inc(rt_done, 1)
                    for k in range(3, EARLY):
                        shared.silu(act, k)
                        shared.high(act, k - 1)
                    for n in range(NT):
                        act.wait_ge(t_ready, n + 1)
                        act.activation(ogT[:, :, n * P:(n + 1) * P], psum[:, n % 2, 0:D].rearrange("p (c t) -> p c t", c=DC),
                                       ACT.Copy).then_inc(evac, 1)
                    for k in range(EARLY, HALVES):
                        shared.silu(act, k)
                        shared.high(act, k - 1)
                    shared.high(act, HALVES - 1)
                    for n in range(NT):
                        act.wait_ge(s_done, n + 1)
                        square(act, s1, 1, n)

                @block.tensor
                def _(pe):
                    for n in range(NT):
                        if n >= 2:
                            pe.wait_ge(o_done, n - 1)
                        for cv in range(2):
                            last = pe.transpose(psum[:, n % 2, cv * P:(cv + 1) * P], oT[:, cv, n * P:(n + 1) * P], ident[:, :])
                        last.then_inc(t3_ready, 1)
                    for k in range(EARLY):
                        shared.gate_up(pe, k)
                    pe.wait_ge(og_ready, 1)
                    pe.wait_ge(wo_loaded, 16)
                    for n in range(NT):
                        if n >= 2:
                            pe.wait_ge(evac, n - 1)
                        for c in range(DC):
                            last = pe.transpose(psum[:, n % 2, c * P:(c + 1) * P], o[:, n, c * P:(c + 1) * P], ident[:, :])
                        last.then_inc(t_ready, 1)
                    for k in range(EARLY, HALVES):
                        shared.gate_up(pe, k)
                    for n in range(NT):
                        pe.wait_ge(evac, n + 1)
                        if n >= 2:
                            pe.wait_ge(s_done, n - 1)
                        for c in range(DC):
                            last = pe.matmul(psum[:, 2 + n % 2, 0:D], ogT[:, c, n * P:(n + 1) * P], wo[:, c, :],
                                             start=(c == 0), stop=(c == DC - 1))
                        last.then_inc(y_ready, 1)

        with ExitStack() as local:
            def tmp(name, shape, dt=F32):
                return local.enter_context(nc.sbuf_tensor("m1_" + name, shape, dt))
            xT_h, xT_l = tmp("xTh", [P, DC, T], F16), tmp("xTl", [P, DC, T], F16)
            rms_turned("g1_r2", s1, 1, xT_h, xT_l)
            sg = tmp("sg", [P, 2, HALF])
            hf = tmp("hf", [P, 2, HALF])
            hT_h, hT_l = tmp("hTh", [P, FT, T], F16), tmp("hTl", [P, FT, T], F16)
            gu_ready, silu_done, h_ready, hh_ready, hl_ready, y_ready, y_done = (
                sem("m1_" + s) for s in ("gu", "si", "h", "hh", "hl", "y", "yd"))
            with nc.Block() as block:
                steps = [(f, half) for f in range(FT) for half in range(2)]

                @block.tensor
                def _(pe):
                    (w1_h, w3_h, w2_h), (w1_l, w3_l, w2_l) = mlp_h, mlp_l
                    for s, (f, half) in enumerate(steps):
                        rows = min(P, HID - f * P)
                        if s >= 2:
                            pe.wait_ge(h_ready, s - 1)
                        hidden, cols = slice(f * P, f * P + rows), slice(half * HALF, (half + 1) * HALF)
                        for j, (wh, wl) in enumerate(((w1_h, w1_l), (w3_h, w3_l))):
                            out = psum[0:rows, 2 * (s % 2) + j, :]
                            for c in range(DC):
                                pe.matmul(out, wh[:, c, hidden], xT_h[:, c, cols], start=(c == 0), stop=False)
                                pe.matmul(out, wh[:, c, hidden], xT_l[:, c, cols], start=False, stop=False)
                                last = pe.matmul(out, wl[:, c, hidden], xT_h[:, c, cols], start=False, stop=(c == DC - 1))
                        last.then_inc(gu_ready, 1)
                    pe.wait_ge(hl_ready, len(steps) - 1)
                    for n in range(NT):
                        if n == NT // 2:
                            pe.wait_ge(hl_ready, len(steps))
                        if n >= 4:
                            pe.wait_ge(y_done, n - 3)
                        out = psum[:, 4 + n % 4, 0:D]
                        for f in range(FT):
                            rows = min(P, HID - f * P)
                            hh, hl = (h[0:rows, f, n * P:(n + 1) * P] for h in (hT_h, hT_l))
                            pe.matmul(out, hh, w2_h[0:rows, f, :], start=(f == 0), stop=False)
                            pe.matmul(out, hh, w2_l[0:rows, f, :], start=False, stop=False)
                            last = pe.matmul(out, hl, w2_h[0:rows, f, :], start=False, stop=(f == FT - 1))
                        last.then_inc(y_ready, 1)

                @block.scalar
                def _(act):
                    def silu(s, rows):
                        act.wait_ge(gu_ready, s + 1)
                        if s >= 2:
                            act.wait_ge(h_ready, s - 1)
                        act.activation(sg[0:rows, s % 2, :], psum[0:rows, 2 * (s % 2), :], ACT.Silu,
                                       scale=1.0 / WSCALE).then_inc(silu_done, 1)

                    for s, (f, half) in enumerate(steps):
                        rows = min(P, HID - f * P)
                        silu(s, rows)
                        act.wait_ge(h_ready, s + 1)
                        act.activation(hT_h[0:rows, f, half * HALF:(half + 1) * HALF], hf[0:rows, s % 2, :],
                                       ACT.Copy).then_inc(hh_ready, 1)

                @block.vector
                def _(dve):
                    for s, (f, half) in enumerate(steps):
                        rows, cols = min(P, HID - f * P), slice(half * HALF, (half + 1) * HALF)
                        dve.wait_ge(silu_done, s + 1)
                        if s >= 2:
                            dve.wait_ge(hl_ready, s - 1)
                        dve.scalar_tensor_tensor(hf[0:rows, s % 2, :], psum[0:rows, 2 * (s % 2) + 1, :], 1.0 / WSCALE,
                                                 sg[0:rows, s % 2, :], ALU.mult, ALU.mult).then_inc(h_ready, 1)
                        dve.wait_ge(hh_ready, s + 1)
                        dve.tensor_tensor(hT_l[0:rows, f, cols], hf[0:rows, s % 2, :], hT_h[0:rows, f, cols],
                                          ALU.subtract).then_inc(hl_ready, 1)
                    for n in range(NT):
                        dve.wait_ge(y_ready, n + 1)
                        dve.scalar_tensor_tensor(s1[:, n, :], psum[:, 4 + n % 4, 0:D], 1.0 / WSCALE, s1[:, n, :],
                                                 ALU.mult, ALU.add).then_inc(y_done, 1)


def mixture1(nc, env, w, out):
    sem, psum, ident = env["sem"], env["psum"], env["ident"]
    xT_h, xT_l, x, s1, comb_dram = (env[k] for k in ("xT_h", "xT_l", "x", "s1", "comb_dram"))
    PAIRS = E1 // 2
    shared_dn_h, shared_dn_l, shared_hh, shared_hl = env["shared_parts"]
    with ExitStack() as local:
        def tmp(name, shape, dt=F32):
            return local.enter_context(nc.sbuf_tensor("e1_" + name, shape, dt))
        gu_f = [tmp(f"guf{b}", [P, 2, 2, DC, F1]) for b in range(2)]
        gu_h = [tmp(f"guh{b}", [P, 2, DC, P], F16) for b in range(2)]
        gu_l = [tmp(f"gul{b}", [P, 2, DC, P], F16) for b in range(2)]
        dn_f = [tmp(f"dnf{b}", [P, DC, P]) for b in range(2)]
        dn_h = [tmp(f"dnh{b}", [P, DC, P], F16) for b in range(2)]
        dn_l = [tmp(f"dnl{b}", [P, DC, P], F16) for b in range(2)]
        cb = [tmp(f"cb{b}", [P, T]) for b in range(2)]
        sg = [tmp(f"sg{b}", [P, HALF]) for b in range(2)]
        hf = [tmp(f"hf{b}", [P, HALF]) for b in range(2)]
        h_h = [tmp(f"hh{b}", [P, HALF], F16) for b in range(4)]
        h_l = [tmp(f"hl{b}", [P, HALF], F16) for b in range(4)]
        yT = tmp("yT", [P, DC, T])
        gate1 = [tmp(f"gate{b}", [P, D]) for b in range(2)]
        prod = [tmp(f"prod{b}", [P, D]) for b in range(2)]
        gu_loaded = [sem(f"e1_gl{b}") for b in range(2)]
        dn_loaded = [sem(f"e1_dl{b}") for b in range(2)]
        cb_loaded = [sem(f"e1_cl{b}") for b in range(2)]
        OUT_TILES = 2
        stored = [sem(f"e1_st{i}") for i in range(NT // OUT_TILES)]
        (guh_ready, gul_ready, dnh_ready, dnl_ready, gu_ready, silu_ready, mixed, h_ready, hh_ready, hl_ready,
         down_done, y_ready, t_ready, g_ready, p_ready, x_ready) = (sem("e1_" + s) for s in (
             "gh", "gl", "dh", "dl", "gu", "si", "mi", "h", "hh", "hl", "dn", "y", "t", "g", "p", "x"))
        GU_LOADS = 2 * 16
        wg, wu, wd = (w["L1_ffn_" + k] for k in ("wg", "wu", "wd"))

        with nc.Block() as block:
            @block.sync
            def _(sp):
                def load_gate_up(pair, b):
                    for j, src in enumerate((wg, wu)):
                        sp.dma_start(gu_f[b][:, j, :, :, :].rearrange("p e c f -> p e (c f)"),
                                     src[bass.ds(2 * pair, 2), :, :].rearrange("e (p c) f -> p e (c f)", p=P))\
                          .then_inc(gu_loaded[b], 16)

                def load_down(pair, b):
                    sp.dma_start(dn_f[b][:, :, :].rearrange("p c d -> p (c d)"),
                                 wd[bass.ds(2 * pair, 2), :, :].rearrange("e f d -> (e f) d")).then_inc(dn_loaded[b], 16)

                def load_comb(pair, b):
                    for e in range(2):
                        sp.dma_start(cb[b][e * F1:(e + 1) * F1, :],
                                     comb_dram[bass.ds(2 * pair + e, 1), :].rearrange("o t -> (o t)").partition_broadcast(F1))\
                          .then_inc(cb_loaded[b], 16)

                def loads(pair, b, comb=True):
                    sp.wait_ge(gul_ready, pair - 1)
                    load_gate_up(pair, b)
                    if comb:
                        sp.wait_ge(mixed, 2 * pair - 4)
                        load_comb(pair - 1, 1 - b)
                    sp.wait_ge(dnl_ready, pair - 1)
                    load_down(pair, b)

                for b in range(2):
                    load_gate_up(b, b)
                    load_down(b, b)
                for b in range(2):
                    load_comb(b, b)
                loads(2, 0, comb=False)
                with sp.Fori(0, PAIRS // 2 - 2) as i:
                    loads(2 * i + 3, 1)
                    loads(2 * i + 4, 0)
                loads(PAIRS - 1, 1)
                sp.wait_ge(mixed, 2 * PAIRS - 4)
                load_comb(PAIRS - 1, 1)
                tokens = out.rearrange("(n p) d -> p n d", p=P)
                for at in range(0, NT, OUT_TILES):
                    sp.wait_ge(x_ready, at + OUT_TILES)
                    sp.dma_start(tokens[:, at:at + OUT_TILES, :], x[:, at:at + OUT_TILES, :]).then_inc(stored[at // OUT_TILES], 16)
                for done in stored:
                    sp.wait_ge(done, 16)

            @block.tensor
            def _(pe):
                def gate_up(s, b, half):
                    hs = 2 * s + half
                    if half == 0:
                        pe.wait_ge(gul_ready, s + 1)
                    if not (isinstance(s, int) and s == 0):
                        pe.wait_ge(h_ready, hs - 1)
                    cols = slice(half * HALF, (half + 1) * HALF)
                    for j in range(2):
                        out = psum[:, 4 + 2 * half + j, :]
                        for c in range(DC):
                            wh, wl = gu_h[b][:, j, c, :], gu_l[b][:, j, c, :]
                            pe.matmul(out, wh, xT_h[:, c, cols], start=(c == 0), stop=False)
                            pe.matmul(out, wh, xT_l[:, c, cols], start=False, stop=False)
                            last = pe.matmul(out, wl, xT_h[:, c, cols], start=False, stop=(c == DC - 1))
                    last.then_inc(gu_ready, 1)

                def down(s, b, half, end=False):
                    hs = 2 * s + half
                    if half == 0:
                        pe.wait_ge(dnl_ready, s + 1)
                    pe.wait_ge(hl_ready, hs + 1)
                    hh, hl = h_h[2 * b + half][:, :], h_l[2 * b + half][:, :]
                    for c in range(DC):
                        out = psum[:, 2 * c + half, :]
                        wh, wl = dn_h[b][:, c, :], dn_l[b][:, c, :]
                        pe.matmul(out, wh, hh, start=False, stop=False)
                        pe.matmul(out, wh, hl, start=False, stop=False)
                        last = pe.matmul(out, wl, hh, start=False, stop=end)
                    last.then_inc(down_done, 1)

                def shared_down(q, half):
                    hh, hl = shared_hh[2 * q + half][:, :], shared_hl[2 * q + half][:, :]
                    for c in range(DC):
                        out, wh, wl = psum[:, 2 * c + half, :], shared_dn_h[q][:, c, :], shared_dn_l[q][:, c, :]
                        pe.matmul(out, wh, hh, start=(q == 0), stop=False)
                        pe.matmul(out, wh, hl, start=False, stop=False)
                        pe.matmul(out, wl, hh, start=False, stop=False)

                for q in range(SH1 // P):
                    for half in range(2):
                        shared_down(q, half)
                gate_up(0, 0, 0)
                gate_up(0, 0, 1)
                for half in range(2):
                    gate_up(1, 1, half)
                    down(0, 0, half)
                with pe.Fori(0, PAIRS // 2 - 1) as i:
                    for b in range(2):
                        for half in range(2):
                            gate_up(2 * i + 2 + b, b, half)
                            down(2 * i + 1 + b, 1 - b, half)
                for half in range(2):
                    down(PAIRS - 1, 1, half, end=True)
                for n in range(NT):
                    pe.wait_ge(y_ready, n // 4 + 1)
                    if n >= 2:
                        pe.wait_ge(g_ready, n - 1)
                    for c in range(DC):
                        last = pe.transpose(psum[:, 4 + n % 2, c * P:(c + 1) * P], yT[:, c, n * P:(n + 1) * P], ident[:, :])
                    last.then_inc(t_ready, 1)

            @block.scalar
            def _(act):
                def gate_up_high(s, b, loads):
                    act.wait_ge(gu_loaded[b], GU_LOADS * loads)
                    if not (isinstance(s, int) and s < 2):
                        act.wait_ge(gu_ready, 2 * s - 2)
                    for j in range(2):
                        last = act.activation(gu_h[b][:, j, :, :].rearrange("p c (e f) -> p e c f", e=2), gu_f[b][:, j, :, :, :],
                                              ACT.Copy, scale=WSCALE)
                    last.then_inc(guh_ready, 1)

                def down_high(s, b, loads):
                    act.wait_ge(dn_loaded[b], 16 * loads)
                    if not (isinstance(s, int) and s < 2):
                        act.wait_ge(down_done, 2 * s - 2)
                    act.activation(dn_h[b][:, :, :], dn_f[b][:, :, :], ACT.Copy, scale=WSCALE).then_inc(dnh_ready, 1)

                def silu(s, b, half):
                    hs = 2 * s + half
                    act.wait_ge(gu_ready, hs + 1)
                    if not (isinstance(s, int) and s == 0):
                        act.wait_ge(h_ready, hs - 1)
                    act.activation(sg[half][:, :], psum[:, 4 + 2 * half, :], ACT.Silu, scale=1.0 / WSCALE).then_inc(silu_ready, 1)

                def high(s, b, half):
                    hs = 2 * s + half
                    act.wait_ge(h_ready, hs + 1)
                    if not (isinstance(s, int) and s < 2):
                        act.wait_ge(down_done, hs - 3)
                    act.activation(h_h[2 * b + half][:, :], hf[half][:, :], ACT.Copy).then_inc(hh_ready, 1)

                def step(s, b, gate_up=None, down=None):
                    silu(s, b, 0)
                    high(s, b, 0)
                    silu(s, b, 1)
                    if gate_up is not None:
                        gate_up_high(s + 2, b, gate_up)
                    high(s, b, 1)
                    if down is not None:
                        down_high(s + 1, 1 - b, down)

                gate_up_high(0, 0, 1)
                down_high(0, 0, 1)
                gate_up_high(1, 1, 1)
                step(0, 0, 2, 1)
                step(1, 1, 2, 2)
                with act.Fori(0, PAIRS // 2 - 2) as i:
                    step(2 * i + 2, 0, i + 3, i + 2)
                    step(2 * i + 3, 1, i + 3, i + 3)
                step(PAIRS - 2, 0, None, PAIRS // 2)
                step(PAIRS - 1, 1)
                for half in range(2):
                    act.wait_ge(down_done, 2 * PAIRS - 1 + half)
                    for c in range(DC):
                        last = act.activation(yT[:, c, half * HALF:(half + 1) * HALF], psum[:, 2 * c + half, :], ACT.Copy,
                                              scale=1.0 / WSCALE)
                    last.then_inc(y_ready, 1)
                for n in range(NT):
                    act.wait_ge(t_ready, n + 1)
                    if n >= 2:
                        act.wait_ge(p_ready, n - 1)
                    act.activation(gate1[n % 2][:, :], psum[:, 4 + n % 2, 0:D], ACT.Silu).then_inc(g_ready, 1)

            @block.gpsimd
            def _(pool):
                with pool.Fori(0, PAIRS // 2) as i:
                    for b in range(2):
                        for half in range(2):
                            pool.wait_ge(silu_ready, 2 * (2 * i + b) + half + 1)
                            if half == 0:
                                pool.wait_ge(cb_loaded[b], 32 * i + 32)
                            pool.tensor_tensor(sg[half][:, :], sg[half][:, :], cb[b][:, half * HALF:(half + 1) * HALF],
                                               ALU.mult).then_inc(mixed, 1)

            @block.vector
            def _(dve):
                def gate_up_low(s, b):
                    dve.wait_ge(guh_ready, s + 1)
                    by_expert = "p (e f) -> p e f"
                    for j in range(2):
                        for c in range(DC):
                            last = dve.scalar_tensor_tensor(
                                gu_l[b][:, j, c, :].rearrange(by_expert, e=2), gu_f[b][:, j, :, c, :], WSCALE,
                                gu_h[b][:, j, c, :].rearrange(by_expert, e=2), ALU.mult, ALU.subtract)
                    last.then_inc(gul_ready, 1)

                def down_low(s, b):
                    dve.wait_ge(dnh_ready, s + 1)
                    dve.scalar_tensor_tensor(dn_l[b][:, :, :], dn_f[b][:, :, :], WSCALE, dn_h[b][:, :, :],
                                             ALU.mult, ALU.subtract).then_inc(dnl_ready, 1)

                def hidden(s, b, half):
                    hs = 2 * s + half
                    dve.wait_ge(mixed, hs + 1)
                    if not (isinstance(s, int) and s == 0):
                        dve.wait_ge(hl_ready, hs - 1)
                    dve.scalar_tensor_tensor(hf[half][:, :], psum[:, 5 + 2 * half, :], 1.0 / WSCALE, sg[half][:, :],
                                             ALU.mult, ALU.mult).then_inc(h_ready, 1)

                def low(s, b, half):
                    hs = 2 * s + half
                    dve.wait_ge(hh_ready, hs + 1)
                    dve.tensor_tensor(h_l[2 * b + half][:, :], hf[half][:, :], h_h[2 * b + half][:, :],
                                      ALU.subtract).then_inc(hl_ready, 1)

                def step(s, b, gate_up=True, down=True):
                    hidden(s, b, 0)
                    low(s, b, 0)
                    if gate_up:
                        gate_up_low(s + 2, b)
                    hidden(s, b, 1)
                    low(s, b, 1)
                    if down:
                        down_low(s + 1, 1 - b)

                gate_up_low(0, 0)
                down_low(0, 0)
                gate_up_low(1, 1)
                step(0, 0)
                step(1, 1)
                with dve.Fori(0, PAIRS // 2 - 2) as i:
                    for b in range(2):
                        step(2 * i + 2 + b, b)
                step(PAIRS - 2, 0, gate_up=False)
                step(PAIRS - 1, 1, gate_up=False, down=False)
                for n in range(NT):
                    dve.wait_ge(g_ready, n + 1)
                    dve.tensor_tensor(prod[n % 2][:, :], gate1[n % 2][:, :], s1[:, n, :], ALU.mult).then_inc(p_ready, 1)
                    dve.wait_ge(p_ready, n + 1)
                    dve.tensor_tensor(x[:, n, :], x[:, n, :], prod[n % 2][:, :], ALU.add).then_inc(x_ready, 1)


def program(nc, w, out):
    with ExitStack() as ctx:
        def sb(name, shape, dt):
            return ctx.enter_context(nc.sbuf_tensor(name, shape, dt))

        in_use = []

        def sem(name):
            in_use.append(nc.alloc_semaphore(name=name))
            return in_use[-1]

        env = {"sem": sem, "sb": sb}
        env["psum"] = ctx.enter_context(nc.psum_tensor("psum", [P, 8, HALF], F32))
        env["x"] = x = sb("x", [P, NT, D], F32)
        env["x1_stats"] = sb("x1_stats", [P, NT, 2], F32)
        env["x_loaded"] = x_loaded = [env["sem"](f"x_loaded{i}") for i in range(NT // X_TILES)]
        with nc.Block() as block:
            @block.sync
            def _(sp):
                tokens = w["L0_attn_x"][0].rearrange("(n p) d -> p n d", p=P)
                for i, loaded in enumerate(x_loaded):
                    tiles = slice(i * X_TILES, (i + 1) * X_TILES)
                    sp.dma_start(x[:, tiles, :], tokens[:, tiles, :]).then_inc(loaded, 16)
        identities(nc, env)
        with ExitStack() as layer0:
            def tmp(name, shape, dt):
                return layer0.enter_context(nc.sbuf_tensor(name, shape, dt))
            env["gate0"] = tmp("gate0", [P, NT, D], F32)
            env["xT_h"], env["xT_l"] = tmp("xT_h", [P, DC, T], F16), tmp("xT_l", [P, DC, T], F16)
            env["head_weights"] = HeadWeights(nc, env, w, tmp)
            with ExitStack() as norm:
                env["xn"] = norm.enter_context(nc.sbuf_tensor("xn0", [P, NT, D], F32))
                env["xnT"] = xnT = norm.enter_context(nc.sbuf_tensor("xnT0", [P, DC, T], F32))
                mixture0(nc, env, w)
            env["oT_h"], env["oT_l"] = tmp("oT_h", [P, H, T], F16), tmp("oT_l", [P, H, T], F16)
            env["qk"], env["sq"] = tmp("qk", [P, NT, 2, HD], F32), tmp("sq", [P, NT, 2, HD], F32)
            env["wo_loaded"] = [sem(f"wo_loaded{q}") for q in range(H // HQ)]
            attention0(nc, env, w)
            project0(nc, env)
        nc.clear_and_free_semaphores(in_use)
        nc.all_engine_barrier()
        env["xn"], env["xnT"] = sb("xn1", [P, NT, D], F32), sb("xnT1", [P, DC, T], F32)
        env["s1"] = sb("s1", [P, NT, D], F32)
        env["xT_h"], env["xT_l"] = sb("xT1_h", [P, DC, T], F16), sb("xT1_l", [P, DC, T], F16)
        env["shared_parts"] = [[sb(f"sh_{n}{k}", shape, F16) for k in range(count)] for n, shape, count in (
            ("dnh", [P, DC, P], SH1 // P), ("dnl", [P, DC, P], SH1 // P),
            ("hh", [P, HALF], 2 * SH1 // P), ("hl", [P, HALF], 2 * SH1 // P))]
        env["comb_dram"] = nc.dram_tensor("comb_by_expert", [E1, T], F32, kind="Internal").ap()
        gated_linear_attention(nc, env, w)
        mixture1(nc, env, w, out)


_INS = ["L0_attn_x"] + ["L0_attn_" + k for k in ("wq", "wk", "wv", "wo", "q_scale", "k_scale")] \
    + ["L0_ffn_" + k for k in ("router_w", "e_bias", "W_gate", "W_up", "W_down", "shared_gate", "shared_up", "shared_down")] \
    + ["L1_attn_" + k for k in ("Wq", "Wk", "Wkg1", "Wkg2", "bkg2", "Wv", "Wg", "bg", "Wo", "ln1_w", "ln2_w", "W1", "W3", "W2")] \
    + ["L1_ffn_" + k for k in ("router_w", "router_bias", "wg", "wu", "wd", "swg", "swu", "swd")]


def kernel(**inputs):
    import concourse.bacc as bacc
    from concourse.bass_utils import run_bass_kernel_spmd

    nc = bacc.Bacc("TRN2", target_bir_lowering=False, num_devices=1)
    arrays, aps = {}, {}
    for name in _INS:
        a = np.ascontiguousarray(inputs[name])
        arrays["in_" + name] = a
        aps[name] = nc.dram_tensor("in_" + name, a.shape, mybir.dt.from_np(a.dtype), kind="ExternalInput").ap()
    out = nc.dram_tensor("out", [1, T, D], F32, kind="ExternalOutput").ap()
    program(nc, aps, out[0])
    r = run_bass_kernel_spmd(nc, [arrays], core_ids=[0])
    return r.results[0]["out"]
```
